# Optimizing a Trainium2 kernel written in Bass

```python
import numpy as np
import jax
import jax.numpy as jnp

def _softmax(x, axis=-1):
    return jax.nn.softmax(x, axis=axis)

def _gelu(x):
    return jax.nn.gelu(x, approximate=True)

def _silu(x):
    return jax.nn.silu(x)

def _sigmoid(x):
    return jax.nn.sigmoid(x)

def _layernorm(x, axis=-1, eps=1e-05):
    m = jnp.mean(x, axis=axis, keepdims=True)
    v = jnp.var(x, axis=axis, keepdims=True)
    return (x - m) / jnp.sqrt(v + eps)

def _scatter_add(tgt, idx, src, axis=0):
    return tgt.at[idx].add(src)

def _segment_sum(src, seg, n):
    return jax.ops.segment_sum(src, seg, n)
kernel_name = 'mk_decoder_preln_d2_seqx_r4_c517d3'

def setup_inputs(seed: int=0):
    np.random.seed(seed)
    _w = jnp.asarray

    def _rec_inputs():
        import jax
        import jax.numpy as jnp
        _rk = jax.random.key(seed)
        x = -0.0002928 + 1 * jax.random.normal(jax.random.fold_in(_rk, 1), (16, 112, 256), jnp.float32)
        _lenS = 112 - jax.random.randint(jax.random.fold_in(_rk, 7), (16,), 0, max(1, 112 // 4) + 1, jnp.int32)
        _lenS2 = 375 - jax.random.randint(jax.random.fold_in(_rk, 8), (16,), 0, max(1, 375 // 4) + 1, jnp.int32)
        _ctx_1024P = jax.random.normal(jax.random.fold_in(_rk, 11), (16, 16, 256), jnp.float32)
        _ctx_1024c = jax.random.dirichlet(jax.random.fold_in(_rk, 511), 0.3 * jnp.ones((16,), jnp.float32), (16, 375))
        _ctx_1024t = jnp.einsum('bsk,bkd->bsd', _ctx_1024c, _ctx_1024P)
        _ctx_1024t = _ctx_1024t * jax.lax.rsqrt(jnp.mean(jnp.square(_ctx_1024t)) + 1e-12) * 0.953939
        ctx_1024 = -1.39393e-06 + 0.999914 * (_ctx_1024t + 0.3 * jax.random.normal(jax.random.fold_in(_rk, 611), (16, 375, 256), jnp.float32))
        _validS = jnp.arange(112)[None, :] < _lenS[:, None]
        _validS2 = jnp.arange(375)[None, :] < _lenS2[:, None]
        _causal = jnp.tril(jnp.ones((112, 112), dtype=bool))
        mask_Bx1x1xS2_bk0 = jnp.logical_not(jnp.broadcast_to(_validS2[:, None, None, :], (16, 1, 1, 375)))
        return (x, ctx_1024, mask_Bx1x1xS2_bk0)
    x, ctx_1024, mask_Bx1x1xS2_bk0 = _rec_inputs()

    def _L0_attn_setup():
        import jax, jax.numpy as jnp
        import numpy as np
        N_HEAD = 16
        FUTURE_DIM = 4

        def _layernorm(x, g, b, eps=1e-05):
            mu = jnp.mean(x, axis=-1, keepdims=True)
            var = jnp.mean(jnp.square(x - mu), axis=-1, keepdims=True)
            return (x - mu) * jax.lax.rsqrt(var + eps) * g + b

        def _future_attn_head(h, W_qkvf, W_conv, W_proj):
            B, T, D = h.shape
            H, hs, F = (N_HEAD, D // N_HEAD, FUTURE_DIM)
            NEG = jnp.float32(-jnp.inf)
            qkvf = h @ W_qkvf.T
            q, k, v, f = jnp.split(qkvf, 4, axis=-1)
            to_h = lambda t: t.reshape(B, T, H, hs).transpose(0, 2, 1, 3)
            q, k, v, f = (to_h(q), to_h(k), to_h(v), to_h(f))
            attn = jnp.einsum('bhtd,bhsd->bhts', q, k) * hs ** (-0.5)
            rows = jnp.arange(T)[:, None]
            causal_mask = jnp.arange(T)[None, :] <= rows
            causal_attn = jnp.where(causal_mask, attn, 0.0)
            padded_causal = jnp.pad(causal_attn, ((0, 0), (0, 0), (0, 0), (0, F)))
            up_future = jnp.einsum('bhtc,cdf->btfhd', f, W_conv).reshape(B, T, F, D)
            k_future = jnp.einsum('btfc,dc->btfd', up_future, W_qkvf[D:2 * D])
            k_future = k_future.reshape(B, T, F, H, hs).transpose(0, 3, 1, 2, 4)
            future_attention = jnp.einsum('bhtd,bhtfd->bhtf', q, k_future)
            cols_f = rows + 1 + jnp.arange(F)[None, :]
            full_attn = padded_causal.at[:, :, rows, cols_f].set(future_attention)
            full_mask = jnp.arange(T + F)[None, :] <= rows + F
            full_attn = jnp.where(full_mask, full_attn, NEG)
            sm = jax.nn.softmax(full_attn, axis=-1)
            sm_causal = jnp.where(causal_mask, sm[..., :T], 0.0)
            unpadded_future = sm[:, :, rows, cols_f]
            v_future = jnp.einsum('btfc,dc->btfd', up_future, W_qkvf[2 * D:3 * D])
            v_future = v_future.reshape(B, T, F, H, hs).transpose(0, 3, 1, 2, 4)
            future_x = jnp.einsum('bhtf,bhtfd->bhtd', unpadded_future, v_future)
            causal_x = jnp.einsum('bhts,bhsd->bhtd', sm_causal, v)
            new_x = (causal_x + future_x).transpose(0, 2, 1, 3).reshape(B, T, D)
            return new_x @ W_proj.T
        key = jax.random.key(seed)
        ks = jax.random.split(key, 7)
        B, T, D, H, F = (2, 256, 256, N_HEAD, FUTURE_DIM)
        hs = D // H
        s = 0.02
        return {'x': jax.random.normal(ks[0], (B, T, D), jnp.float32), 'W_qkvf': jax.random.normal(ks[1], (4 * D, D), jnp.float32) * s, 'W_conv': jax.random.normal(ks[2], (hs, hs, F), jnp.float32) * s, 'W_proj': jax.random.normal(ks[3], (D, D), jnp.float32) * s, 'W_ff1': jax.random.normal(ks[4], (D, 4 * D), jnp.float32) * s, 'W_ff2': jax.random.normal(ks[5], (4 * D, D), jnp.float32) * s, 'ln1_g': jnp.ones((D,), jnp.float32), 'ln1_b': jnp.zeros((D,), jnp.float32), 'ln2_g': jnp.ones((D,), jnp.float32), 'ln2_b': jnp.zeros((D,), jnp.float32)}
    _L0_attn_all = _L0_attn_setup()
    _L0_attn_in = {k: v for k, v in _L0_attn_all.items() if k in ('W_qkvf', 'W_conv', 'W_proj', 'W_ff1', 'W_ff2', 'ln1_g', 'ln1_b', 'ln2_g', 'ln2_b')}
    del _L0_attn_all

    def _L0_xattn_setup():
        import jax, jax.numpy as jnp
        import numpy as np
        D_MODEL = 256
        N_HEADS = 16
        N_MEM = 64
        D_K = D_MODEL // N_HEADS
        key = jax.random.key(seed)
        ks = jax.random.split(key, 16)
        B, N = (2, 512)
        s = 1.0 / np.sqrt(D_MODEL)
        inp = {'q': jax.random.normal(ks[0], (B, N, D_MODEL), jnp.float32), 'k': jax.random.normal(ks[1], (B, N, D_MODEL), jnp.float32), 'v': jax.random.normal(ks[2], (B, N, D_MODEL), jnp.float32), 'attention_mask': jax.random.randint(ks[3], (B, 1, 1, N), 0, 2).astype(bool), 'Wq': jax.random.normal(ks[4], (D_MODEL, D_MODEL), jnp.float32) * s, 'bq': jnp.zeros((D_MODEL,), jnp.float32), 'Wk': jax.random.normal(ks[5], (D_MODEL, D_MODEL), jnp.float32) * s, 'bk': jnp.zeros((D_MODEL,), jnp.float32), 'Wv': jax.random.normal(ks[6], (D_MODEL, D_MODEL), jnp.float32) * s, 'bv': jnp.zeros((D_MODEL,), jnp.float32), 'Wo': jax.random.normal(ks[7], (D_MODEL, D_MODEL), jnp.float32) * s, 'bo': jnp.zeros((D_MODEL,), jnp.float32), 'm_k': jax.random.normal(ks[8], (1, N_MEM, D_MODEL), jnp.float32) * 0.01, 'm_v': jax.random.normal(ks[9], (1, N_MEM, D_MODEL), jnp.float32) * 0.01}
        return inp
    _L0_xattn_all = _L0_xattn_setup()
    _L0_xattn_in = {k: v for k, v in _L0_xattn_all.items() if k in ('Wq', 'bq', 'Wk', 'bk', 'Wv', 'bv', 'Wo', 'bo', 'm_k', 'm_v')}
    del _L0_xattn_all

    def _L0_ffn_setup():
        import jax, jax.numpy as jnp
        import numpy as np
        TOP_K = 2

        def _mlp(x, w_fc, w_proj):
            return jnp.square(jax.nn.relu(x @ w_fc.T)) @ w_proj.T
        key = jax.random.key(seed)
        ks = jax.random.split(key, 6)
        B, S, D, E = (4, 512, 256, 8)
        d_ff = 4 * D
        x = jax.random.normal(ks[0], (B, S, D), dtype=jnp.float32)
        router_w = jax.random.normal(ks[1], (E, D), dtype=jnp.float32) * 0.02
        w_fc = jax.random.normal(ks[2], (E, d_ff, D), dtype=jnp.float32) * 0.02
        w_proj = jax.random.normal(ks[3], (E, D, d_ff), dtype=jnp.float32) * 0.02
        shared_fc = jax.random.normal(ks[4], (d_ff, D), dtype=jnp.float32) * 0.02
        shared_proj = jax.random.normal(ks[5], (D, d_ff), dtype=jnp.float32) * 0.02
        return {'x': x, 'router_w': router_w, 'w_fc': w_fc, 'w_proj': w_proj, 'shared_fc': shared_fc, 'shared_proj': shared_proj}
    _L0_ffn_all = _L0_ffn_setup()
    _L0_ffn_in = {k: v for k, v in _L0_ffn_all.items() if k in ('router_w', 'w_fc', 'w_proj', 'shared_fc', 'shared_proj')}
    del _L0_ffn_all

    def _L1_attn_setup():
        import jax, jax.numpy as jnp
        import numpy as np
        _DENSE_LOCAL_W = 32
        _DYADIC = [48, 64, 96, 128, 192, 64, 96, 128, 192, 256, 384]
        OFFSETS = sorted(set(range(_DENSE_LOCAL_W + 1)) | set(_DYADIC))
        B, N, D, H = (2, 1024, 256, 16)
        HD = D // H
        NEG = -1e+30

        def _shift(t, o):
            if o == 0:
                return t
            n = t.shape[2]
            return jnp.pad(t, ((0, 0), (0, 0), (o, 0), (0, 0)))[:, :, :n]
        key = jax.random.key(seed)
        ks = jax.random.split(key, 9)
        alphas = jnp.linspace(0.2, 2.0, H)
        delta = jnp.log1p(jnp.asarray(OFFSETS, dtype=jnp.float32))
        pos_bias = -delta[:, None] * alphas[None, :]
        return {'x': jax.random.normal(ks[0], (B, N, D), jnp.float32), 'qkv_w': jax.random.normal(ks[1], (3 * D, D), jnp.float32) * 0.02, 'qkv_b': jax.random.normal(ks[2], (3 * D,), jnp.float32) * 0.01, 'out_w': jax.random.normal(ks[3], (D, D), jnp.float32) * 0.02, 'out_b': jnp.zeros((D,), jnp.float32), 'gate_w': jax.random.normal(ks[4], (D, D), jnp.float32) * 0.02, 'gate_b': jnp.zeros((D,), jnp.float32), 'pos_bias': pos_bias, 'scale_embed': jax.random.normal(ks[5], (len(OFFSETS), HD), jnp.float32) * 0.02, 'if_gain': 1.0 + jax.random.normal(ks[6], (H,), jnp.float32) * 0.05}
    _L1_attn_all = _L1_attn_setup()
    _L1_attn_in = {k: v for k, v in _L1_attn_all.items() if k in ('qkv_w', 'qkv_b', 'out_w', 'out_b', 'gate_w', 'gate_b', 'pos_bias', 'scale_embed', 'if_gain')}
    del _L1_attn_all

    def _L1_xattn_setup():
        import jax, jax.numpy as jnp
        import numpy as np
        from math import sqrt
        D_MODEL = 256
        N_HEADS = 16
        DK = D_MODEL // N_HEADS
        key = jax.random.key(seed)
        ks = jax.random.split(key, 11)
        B, L, S = (2, 512, 512)
        inp = {'queries': jax.random.normal(ks[0], (B, L, D_MODEL), jnp.float32), 'keys': jax.random.normal(ks[1], (B, S, D_MODEL), jnp.float32), 'values': jax.random.normal(ks[2], (B, S, D_MODEL), jnp.float32), 'Wq': jax.random.normal(ks[3], (D_MODEL, D_MODEL), jnp.float32) * 0.02, 'bq': jnp.zeros((D_MODEL,), jnp.float32), 'Wk': jax.random.normal(ks[4], (D_MODEL, D_MODEL), jnp.float32) * 0.02, 'bk': jnp.zeros((D_MODEL,), jnp.float32), 'Wv': jax.random.normal(ks[5], (D_MODEL, D_MODEL), jnp.float32) * 0.02, 'bv': jnp.zeros((D_MODEL,), jnp.float32), 'Wo': jax.random.normal(ks[6], (D_MODEL, D_MODEL), jnp.float32) * 0.02, 'bo': jnp.zeros((D_MODEL,), jnp.float32)}
        return inp
    _L1_xattn_all = _L1_xattn_setup()
    _L1_xattn_in = {k: v for k, v in _L1_xattn_all.items() if k in ('Wq', 'bq', 'Wk', 'bk', 'Wv', 'bv', 'Wo', 'bo')}
    del _L1_xattn_all

    def _L1_ffn_setup():
        import jax, jax.numpy as jnp
        import numpy as np
        QMAX = 127.0

        def _ste_round(v):
            return v + jax.lax.stop_gradient(jnp.round(v) - v)

        def _act_fake_quant(x, clip_factor):
            scale = jax.nn.sigmoid(clip_factor) * jnp.max(jnp.abs(x)) / QMAX
            return jnp.clip(_ste_round(x / scale), -QMAX - 1.0, QMAX) * scale

        def _weight_fake_quant(w):
            scale = jnp.max(jnp.abs(w), axis=1, keepdims=True) / QMAX
            return jnp.clip(_ste_round(w / scale), -QMAX - 1.0, QMAX) * scale
        key = jax.random.key(seed)
        k1, k2, k3, k4 = jax.random.split(key, 4)
        B, S, H, I = (8, 2048, 256, 704)
        return {'x': jax.random.normal(k1, (B, S, H), dtype=jnp.float32), 'clip_x': jnp.full((1,), 4.0, dtype=jnp.float32), 'clip_down': jnp.full((1,), 4.0, dtype=jnp.float32), 'w_gate': jax.random.normal(k2, (I, H), dtype=jnp.float32) * 0.02, 'w_up': jax.random.normal(k3, (I, H), dtype=jnp.float32) * 0.02, 'w_down': jax.random.normal(k4, (H, I), dtype=jnp.float32) * 0.02}
    _L1_ffn_all = _L1_ffn_setup()
    _L1_ffn_in = {k: v for k, v in _L1_ffn_all.items() if k in ('clip_x', 'clip_down', 'w_gate', 'w_up', 'w_down')}
    del _L1_ffn_all
    return {'x': x, 'ctx_1024': ctx_1024, 'mask_Bx1x1xS2_bk0': mask_Bx1x1xS2_bk0, 'L0_attn_W_qkvf': _L0_attn_in['W_qkvf'], 'L0_attn_W_conv': _L0_attn_in['W_conv'], 'L0_attn_W_proj': _L0_attn_in['W_proj'], 'L0_attn_W_ff1': _L0_attn_in['W_ff1'], 'L0_attn_W_ff2': _L0_attn_in['W_ff2'], 'L0_attn_ln1_g': _L0_attn_in['ln1_g'], 'L0_attn_ln1_b': _L0_attn_in['ln1_b'], 'L0_attn_ln2_g': _L0_attn_in['ln2_g'], 'L0_attn_ln2_b': _L0_attn_in['ln2_b'], 'L0_xattn_Wq': _L0_xattn_in['Wq'], 'L0_xattn_bq': _L0_xattn_in['bq'], 'L0_xattn_Wk': _L0_xattn_in['Wk'], 'L0_xattn_bk': _L0_xattn_in['bk'], 'L0_xattn_Wv': _L0_xattn_in['Wv'], 'L0_xattn_bv': _L0_xattn_in['bv'], 'L0_xattn_Wo': _L0_xattn_in['Wo'], 'L0_xattn_bo': _L0_xattn_in['bo'], 'L0_xattn_m_k': _L0_xattn_in['m_k'], 'L0_xattn_m_v': _L0_xattn_in['m_v'], 'L0_ffn_router_w': _L0_ffn_in['router_w'], 'L0_ffn_w_fc': _L0_ffn_in['w_fc'], 'L0_ffn_w_proj': _L0_ffn_in['w_proj'], 'L0_ffn_shared_fc': _L0_ffn_in['shared_fc'], 'L0_ffn_shared_proj': _L0_ffn_in['shared_proj'], 'L1_attn_qkv_w': _L1_attn_in['qkv_w'], 'L1_attn_qkv_b': _L1_attn_in['qkv_b'], 'L1_attn_out_w': _L1_attn_in['out_w'], 'L1_attn_out_b': _L1_attn_in['out_b'], 'L1_attn_gate_w': _L1_attn_in['gate_w'], 'L1_attn_gate_b': _L1_attn_in['gate_b'], 'L1_attn_pos_bias': _L1_attn_in['pos_bias'], 'L1_attn_scale_embed': _L1_attn_in['scale_embed'], 'L1_attn_if_gain': _L1_attn_in['if_gain'], 'L1_xattn_Wq': _L1_xattn_in['Wq'], 'L1_xattn_bq': _L1_xattn_in['bq'], 'L1_xattn_Wk': _L1_xattn_in['Wk'], 'L1_xattn_bk': _L1_xattn_in['bk'], 'L1_xattn_Wv': _L1_xattn_in['Wv'], 'L1_xattn_bv': _L1_xattn_in['bv'], 'L1_xattn_Wo': _L1_xattn_in['Wo'], 'L1_xattn_bo': _L1_xattn_in['bo'], 'L1_ffn_clip_x': _L1_ffn_in['clip_x'], 'L1_ffn_clip_down': _L1_ffn_in['clip_down'], 'L1_ffn_w_gate': _L1_ffn_in['w_gate'], 'L1_ffn_w_up': _L1_ffn_in['w_up'], 'L1_ffn_w_down': _L1_ffn_in['w_down']}

def reference(x, ctx_1024, mask_Bx1x1xS2_bk0, L0_attn_W_qkvf, L0_attn_W_conv, L0_attn_W_proj, L0_attn_W_ff1, L0_attn_W_ff2, L0_attn_ln1_g, L0_attn_ln1_b, L0_attn_ln2_g, L0_attn_ln2_b, L0_xattn_Wq, L0_xattn_bq, L0_xattn_Wk, L0_xattn_bk, L0_xattn_Wv, L0_xattn_bv, L0_xattn_Wo, L0_xattn_bo, L0_xattn_m_k, L0_xattn_m_v, L0_ffn_router_w, L0_ffn_w_fc, L0_ffn_w_proj, L0_ffn_shared_fc, L0_ffn_shared_proj, L1_attn_qkv_w, L1_attn_qkv_b, L1_attn_out_w, L1_attn_out_b, L1_attn_gate_w, L1_attn_gate_b, L1_attn_pos_bias, L1_attn_scale_embed, L1_attn_if_gain, L1_xattn_Wq, L1_xattn_bq, L1_xattn_Wk, L1_xattn_bk, L1_xattn_Wv, L1_xattn_bv, L1_xattn_Wo, L1_xattn_bo, L1_ffn_clip_x, L1_ffn_clip_down, L1_ffn_w_gate, L1_ffn_w_up, L1_ffn_w_down):
    import jax
    import jax.numpy as jnp

    def _L0_attn_ref(x, W_qkvf, W_conv, W_proj, W_ff1, W_ff2, ln1_g, ln1_b, ln2_g, ln2_b):
        import jax, jax.numpy as jnp
        import numpy as np
        N_HEAD = 16
        FUTURE_DIM = 4

        def _layernorm(x, g, b, eps=1e-05):
            mu = jnp.mean(x, axis=-1, keepdims=True)
            var = jnp.mean(jnp.square(x - mu), axis=-1, keepdims=True)
            return (x - mu) * jax.lax.rsqrt(var + eps) * g + b

        def _future_attn_head(h, W_qkvf, W_conv, W_proj):
            B, T, D = h.shape
            H, hs, F = (N_HEAD, D // N_HEAD, FUTURE_DIM)
            NEG = jnp.float32(-jnp.inf)
            qkvf = h @ W_qkvf.T
            q, k, v, f = jnp.split(qkvf, 4, axis=-1)
            to_h = lambda t: t.reshape(B, T, H, hs).transpose(0, 2, 1, 3)
            q, k, v, f = (to_h(q), to_h(k), to_h(v), to_h(f))
            attn = jnp.einsum('bhtd,bhsd->bhts', q, k) * hs ** (-0.5)
            rows = jnp.arange(T)[:, None]
            causal_mask = jnp.arange(T)[None, :] <= rows
            causal_attn = jnp.where(causal_mask, attn, 0.0)
            padded_causal = jnp.pad(causal_attn, ((0, 0), (0, 0), (0, 0), (0, F)))
            up_future = jnp.einsum('bhtc,cdf->btfhd', f, W_conv).reshape(B, T, F, D)
            k_future = jnp.einsum('btfc,dc->btfd', up_future, W_qkvf[D:2 * D])
            k_future = k_future.reshape(B, T, F, H, hs).transpose(0, 3, 1, 2, 4)
            future_attention = jnp.einsum('bhtd,bhtfd->bhtf', q, k_future)
            cols_f = rows + 1 + jnp.arange(F)[None, :]
            full_attn = padded_causal.at[:, :, rows, cols_f].set(future_attention)
            full_mask = jnp.arange(T + F)[None, :] <= rows + F
            full_attn = jnp.where(full_mask, full_attn, NEG)
            sm = jax.nn.softmax(full_attn, axis=-1)
            sm_causal = jnp.where(causal_mask, sm[..., :T], 0.0)
            unpadded_future = sm[:, :, rows, cols_f]
            v_future = jnp.einsum('btfc,dc->btfd', up_future, W_qkvf[2 * D:3 * D])
            v_future = v_future.reshape(B, T, F, H, hs).transpose(0, 3, 1, 2, 4)
            future_x = jnp.einsum('bhtf,bhtfd->bhtd', unpadded_future, v_future)
            causal_x = jnp.einsum('bhts,bhsd->bhtd', sm_causal, v)
            new_x = (causal_x + future_x).transpose(0, 2, 1, 3).reshape(B, T, D)
            return new_x @ W_proj.T
        x = x + _future_attn_head(_layernorm(x, ln1_g, ln1_b), W_qkvf, W_conv, W_proj)
        h = _layernorm(x, ln2_g, ln2_b)
        x = x + jax.nn.gelu(h @ W_ff1, approximate=False) @ W_ff2
        return x

    def _L0_xattn_ref(q, k, v, attention_mask, Wq, bq, Wk, bk, Wv, bv, Wo, bo, m_k, m_v):
        import jax, jax.numpy as jnp
        import numpy as np
        D_MODEL = 256
        N_HEADS = 16
        N_MEM = 64
        D_K = D_MODEL // N_HEADS
        B, Nq, D = q.shape
        nk = k.shape[1]
        H, dk, M = (N_HEADS, D_K, N_MEM)
        qh = (q @ Wq.T + bq).reshape(B, Nq, H, dk).transpose(0, 2, 1, 3)
        k_proj = k @ Wk.T + bk
        v_proj = v @ Wv.T + bv
        mk = jnp.broadcast_to(m_k * np.sqrt(dk), (B, M, D))
        mv = jnp.broadcast_to(m_v * np.sqrt(M), (B, M, D))
        kk = jnp.concatenate([k_proj, mk], axis=1)
        vv = jnp.concatenate([v_proj, mv], axis=1)
        kh = kk.reshape(B, nk + M, H, dk).transpose(0, 2, 1, 3)
        vh = vv.reshape(B, nk + M, H, dk).transpose(0, 2, 1, 3)
        scores = jnp.einsum('bhqd,bhkd->bhqk', qh, kh) / np.sqrt(dk)
        pad_mask = jnp.concatenate([jnp.broadcast_to(attention_mask, (B, 1, 1, nk)), jnp.zeros((B, 1, 1, M), bool)], axis=-1)
        scores = jnp.where(pad_mask, -jnp.inf, scores)
        p_attn = jax.nn.softmax(scores, axis=-1)
        out = jnp.einsum('bhqk,bhkd->bhqd', p_attn, vh)
        out = out.transpose(0, 2, 1, 3).reshape(B, Nq, D)
        return out @ Wo.T + bo

    def _L0_ffn_ref(x, router_w, w_fc, w_proj, shared_fc, shared_proj):
        import jax, jax.numpy as jnp
        import numpy as np
        TOP_K = 2

        def _mlp(x, w_fc, w_proj):
            return jnp.square(jax.nn.relu(x @ w_fc.T)) @ w_proj.T
        B, S, D = x.shape
        E = router_w.shape[0]
        T = B * S
        flat = x.reshape(T, D)
        logits = flat @ router_w.T
        probs = jax.nn.softmax(logits.astype(jnp.float32), axis=-1)
        topk_p, topk_i = jax.lax.top_k(probs, TOP_K)
        topk_w = (topk_p / jnp.maximum(topk_p.sum(-1, keepdims=True), 1e-09)).astype(flat.dtype)
        combine = jnp.zeros((T, E), dtype=flat.dtype)
        combine = combine.at[jnp.arange(T)[:, None], topk_i].add(topk_w)
        out = jnp.zeros_like(flat)
        for e in range(E):
            out = out + _mlp(flat, w_fc[e], w_proj[e]) * combine[:, e:e + 1]
        out = out + _mlp(flat, shared_fc, shared_proj)
        return out.reshape(B, S, D)

    def _L1_attn_ref(x, qkv_w, qkv_b, out_w, out_b, gate_w, gate_b, pos_bias, scale_embed, if_gain):
        import jax, jax.numpy as jnp
        import numpy as np
        _DENSE_LOCAL_W = 32
        _DYADIC = [48, 64, 96, 128, 192, 64, 96, 128, 192, 256, 384]
        OFFSETS = sorted(set(range(_DENSE_LOCAL_W + 1)) | set(_DYADIC))
        B, N, D, H = (2, 1024, 256, 16)
        HD = D // H
        NEG = -1e+30

        def _shift(t, o):
            if o == 0:
                return t
            n = t.shape[2]
            return jnp.pad(t, ((0, 0), (0, 0), (o, 0), (0, 0)))[:, :, :n]
        b, n, d = x.shape
        qkv = x @ qkv_w.T + qkv_b
        q, k, v = jnp.split(qkv, 3, axis=-1)
        heads = lambda t: t.reshape(b, n, H, HD).transpose(0, 2, 1, 3)
        q, k, v = (heads(q), heads(k), heads(v))
        inv = 1.0 / jnp.sqrt(jnp.asarray(HD, x.dtype))
        qs = jnp.einsum('bhnd,od->bhno', q, scale_embed)
        pos = jnp.arange(n)
        logits = []
        for i, o in enumerate(OFFSETS):
            qk = jnp.einsum('bhnd,bhnd->bhn', q, _shift(k, o))
            lg = qk * inv * (1.0 + qs[..., i]) + pos_bias[i][None, :, None]
            lg = jnp.where(pos[None, None, :] >= o, lg, NEG)
            logits.append(lg)
        logits = jnp.stack(logits, axis=-1)
        p = jax.nn.softmax(logits, axis=-1)
        out = jnp.zeros_like(q)
        for i, o in enumerate(OFFSETS):
            out = out + p[..., i][..., None] * _shift(v, o)
        out = out * if_gain[None, :, None, None]
        out_flat = out.transpose(0, 2, 1, 3).reshape(b, n, d)
        gate = jax.nn.sigmoid(x @ gate_w.T + gate_b)
        return out_flat * gate @ out_w.T + out_b

    def _L1_xattn_ref(queries, keys, values, Wq, bq, Wk, bk, Wv, bv, Wo, bo):
        import jax, jax.numpy as jnp
        import numpy as np
        from math import sqrt
        D_MODEL = 256
        N_HEADS = 16
        DK = D_MODEL // N_HEADS
        B, L, _ = queries.shape
        S = values.shape[1]
        H, dk = (N_HEADS, DK)
        q = (queries @ Wq + bq).reshape(B, L, H, dk)
        k = (keys @ Wk + bk).reshape(B, S, H, dk)
        v = (values @ Wv + bv).reshape(B, S, H, dk)
        scale = 1.0 / sqrt(dk)
        scores = jnp.einsum('blhd,bshd->bhls', q, k)
        causal = jnp.triu(jnp.ones((L, S), dtype=bool), k=1)
        scores = jnp.where(causal[None, None], -jnp.inf, scores)
        attn = jax.nn.softmax(scores * scale, axis=-1)
        out = jnp.einsum('bhls,bshd->blhd', attn, v).reshape(B, L, H * dk)
        out = out @ Wo + bo
        return out

    def _L1_ffn_ref(x, clip_x, clip_down, w_gate, w_up, w_down):
        import jax, jax.numpy as jnp
        import numpy as np
        QMAX = 127.0

        def _ste_round(v):
            return v + jax.lax.stop_gradient(jnp.round(v) - v)

        def _act_fake_quant(x, clip_factor):
            scale = jax.nn.sigmoid(clip_factor) * jnp.max(jnp.abs(x)) / QMAX
            return jnp.clip(_ste_round(x / scale), -QMAX - 1.0, QMAX) * scale

        def _weight_fake_quant(w):
            scale = jnp.max(jnp.abs(w), axis=1, keepdims=True) / QMAX
            return jnp.clip(_ste_round(w / scale), -QMAX - 1.0, QMAX) * scale
        xq = _act_fake_quant(x, clip_x[0])
        gate = jnp.einsum('bsh,ih->bsi', xq, _weight_fake_quant(w_gate))
        up = jnp.einsum('bsh,ih->bsi', xq, _weight_fake_quant(w_up))
        h = _act_fake_quant(jax.nn.silu(gate) * up, clip_down[0])
        return jnp.einsum('bsi,hi->bsh', h, _weight_fake_quant(w_down))
    x = x + _L0_attn_ref(_layernorm(x, axis=-1), L0_attn_W_qkvf, L0_attn_W_conv, L0_attn_W_proj, L0_attn_W_ff1, L0_attn_W_ff2, L0_attn_ln1_g, L0_attn_ln1_b, L0_attn_ln2_g, L0_attn_ln2_b)
    x = x + _L0_xattn_ref(_layernorm(x, axis=-1), ctx_1024, ctx_1024, mask_Bx1x1xS2_bk0, L0_xattn_Wq, L0_xattn_bq, L0_xattn_Wk, L0_xattn_bk, L0_xattn_Wv, L0_xattn_bv, L0_xattn_Wo, L0_xattn_bo, L0_xattn_m_k, L0_xattn_m_v)
    x = x + _L0_ffn_ref(_layernorm(x, axis=-1), L0_ffn_router_w, L0_ffn_w_fc, L0_ffn_w_proj, L0_ffn_shared_fc, L0_ffn_shared_proj)
    x = x + _L1_attn_ref(_layernorm(x, axis=-1), L1_attn_qkv_w, L1_attn_qkv_b, L1_attn_out_w, L1_attn_out_b, L1_attn_gate_w, L1_attn_gate_b, L1_attn_pos_bias, L1_attn_scale_embed, L1_attn_if_gain)
    x = x + _L1_xattn_ref(_layernorm(x, axis=-1), ctx_1024, ctx_1024, L1_xattn_Wq, L1_xattn_bq, L1_xattn_Wk, L1_xattn_bk, L1_xattn_Wv, L1_xattn_bv, L1_xattn_Wo, L1_xattn_bo)
    x = x + _L1_ffn_ref(_layernorm(x, axis=-1), L1_ffn_clip_x, L1_ffn_clip_down, L1_ffn_w_gate, L1_ffn_w_up, L1_ffn_w_down)
    return x

_drawn_inputs = setup_inputs


def setup_inputs(seed=0):
    import zlib

    import numpy as np

    out = dict(_drawn_inputs(seed))
    spreads = {'L0_attn_ln1_g': (1.0, 0.6),
     'L0_attn_ln1_b': (0.0, 0.8),
     'L0_attn_ln2_g': (1.0, 0.6),
     'L0_attn_ln2_b': (0.0, 2.0),
     'L0_xattn_bq': (0.0, 0.76),
     'L0_xattn_bk': (0.0, 2.0),
     'L0_xattn_bv': (0.0, 0.43),
     'L0_xattn_bo': (0.0, 0.416),
     'L1_attn_out_b': (0.0, 0.8),
     'L1_attn_gate_b': (0.0, 0.8),
     'L1_xattn_bq': (0.0, 2.0),
     'L1_xattn_bk': (0.0, 2.0),
     'L1_xattn_bv': (0.0, 2.0),
     'L1_xattn_bo': (0.0, 0.8)}
    factors = {'L0_attn_W_qkvf': 6.135,
     'L0_attn_W_conv': 8.0,
     'L0_attn_W_proj': 6.012,
     'L0_xattn_m_k': 64.0,
     'L0_xattn_m_v': 64.0,
     'L1_attn_qkv_w': 4.501,
     'L1_attn_qkv_b': 8.0,
     'L1_attn_out_w': 4.346,
     'L1_attn_gate_w': 8.0,
     'L1_attn_pos_bias': 5.635,
     'L1_attn_scale_embed': 8.0,
     'L1_attn_if_gain': 8.0,
     'L1_xattn_Wq': 54.09,
     'L1_xattn_Wk': 52.155,
     'L1_ffn_w_gate': 3.758,
     'L1_ffn_w_up': 3.448,
     'L1_ffn_w_down': 3.4,
     'L0_ffn_router_w': 5.256,
     'L0_ffn_w_fc': 5.001,
     'L0_ffn_w_proj': 4.626,
     'L0_ffn_shared_fc': 3.732,
     'L0_ffn_shared_proj': 3.372,
     'L1_xattn_Wv': 5.707,
     'L1_xattn_Wo': 3.329}
    for name, (base, spread) in spreads.items():
        noise = np.random.default_rng([zlib.crc32(name.encode()), seed]).standard_normal(out[name].shape)
        drawn = base * np.exp(spread * noise) if base else spread * noise
        out[name] = jnp.asarray(drawn.astype(out[name].dtype))
    for name, factor in factors.items():
        out[name] = (out[name] * factor).astype(out[name].dtype)
    return out
```

```python
from contextlib import ExitStack

import numpy as np

import concourse.bass as bass
from concourse import mybir

F32 = mybir.dt.float32
BF16 = mybir.dt.bfloat16
U8 = mybir.dt.uint8
ALU = mybir.AluOpType
ACT = mybir.ActivationFunctionType
X = mybir.AxisListType.X

P = 128
NB, T, D = 16, 112, 256
C = D // P
TOK = NB * T
S2, MEM = 375, 64
H, HD = 16, 16
HG = 4
NG = H // HG
PADW = NG * P
FUT = 4
G = 448
GROUPS = TOK // G
DFF, E = 1024, 8
M8 = DFF // P
INTER = 704
KC = 110
NKEY = 4 * KC
NEG = -1e30
EPS = 1e-5
ROUND = 12582912.0
QMAX = 127.0
OFFSETS = [o for o in sorted(set(range(33)) | {48, 64, 96, 128, 192, 256, 384})]


class At:

    def __init__(self, const=0, regs=()):
        self.const, self.regs = const, tuple(regs)

    def __add__(self, k):
        return At(self.const + k, self.regs)

    def __sub__(self, k):
        return self + (-k)

    def times(self, f, plus=0):
        v = self.const * f + plus
        for r, c in self.regs:
            v = r * (c * f) + v
        return v

    @property
    def parity(self):
        return self.const % 2


AHEAD = 4


class Signal:

    def __init__(self, sem, per):
        self.sem, self.per = sem, per

    def start(self, eng):
        eng.sem_inc(self.sem, AHEAD * self.per)

    def after(self, step, k=0):
        return self.sem, step.times(self.per, AHEAD * self.per + k + 1)


class Loads:

    def __init__(self, sems, per):
        self.sems, self.per = sems, per

    def sem(self, step):
        return self.sems[step.parity]

    def after(self, step):
        half = At(step.const // 2, [(r, c // 2) for r, c in step.regs])
        return self.sem(step), half.times(16 * self.per, 16 * self.per)


class Chain:

    def __init__(self, sem):
        self.sem, self.n = sem, 0

    def inc(self, ins, by=1):
        ins.then_inc(self.sem, by)
        self.n += by
        return self.n


def tok(step, width=T):
    return bass.ds(step.times(width), width)


def batch_steps(eng, step):
    step(At(0), mid=False, end=False)
    step(At(1), end=False)
    with eng.Fori(0, (NB - 2) // 2) as i:
        step(At(2, [(i, 2)]))
        step(At(3, [(i, 2)]))
    step(At(NB), now=False)
    step(At(NB + 1), now=False, mid=False)


class Scope:

    def __init__(self, nc, stage):
        self.nc, self.stage, self.stack, self.sems = nc, stage, ExitStack(), []

    def __enter__(self):
        self.stack.__enter__()
        return self

    def __exit__(self, *e):
        self.stack.__exit__(*e)
        if self.sems:
            with self.nc.Block() as block:

                @block.gpsimd
                def _(pool):
                    for sem in self.sems:
                        pool.sem_clear(sem)

            for sem in self.sems:
                self.nc.release_semaphore(sem)

    def semaphore(self, name):
        self.sems.append(self.nc.alloc_semaphore(f"{self.stage}_{name}"))
        return self.sems[-1]

    def sb(self, name, shape, dt=F32):
        return self.stack.enter_context(self.nc.sbuf_tensor(f"{self.stage}_{name}", shape, dt))

    def counter(self, name, per):
        return Signal(self.semaphore(name), per)

    def loads(self, name, per):
        return Loads([self.semaphore(f"{name}_{w}") for w in ("even", "odd")], per)

    def chain(self, name):
        return Chain(self.semaphore(name))

    def block(self):
        return self.stack.enter_context(self.nc.Block())




class NormSignals:
    def __init__(self, nc):
        self.mean, self.centered, self.squared, self.var, self.logvar, self.rstd, self.normed, self.affined = (
            Signal(nc.alloc_semaphore(f"norm_{name}"), 1)
            for name in ("mean", "centered", "squared", "var", "logvar", "rstd", "normed", "affined"))
        self.steps = 0


def layer_norm(nc, stage, ns, psum, averager, src, dst, eps, gb=None):
    base = ns.steps
    ns.steps += GROUPS
    with Scope(nc, stage) as s:
        cen = s.sb("cen", [P, 2, C, G])
        sq = s.sb("sq", [P, 2, C, G])
        lv = s.sb("lv", [P, 2, G])
        rs = s.sb("rs", [P, 2, G])
        block = s.block()

        def groups(eng):
            with eng.Fori(0, GROUPS // 2) as i:
                yield [(At(base + u, [(i, 2)]), bass.ds(i * (2 * G) + u * G, G), u) for u in (0, 1)]

        @block.tensor
        def _(pe):
            if base == 0:
                ns.mean.start(pe)
                ns.var.start(pe)
            for pair in groups(pe):
                for n, t, u in pair:
                    pe.wait_ge(*ns.centered.after(n - 2))
                    for c in range(C):
                        mm = nc.tensor.matmul(psum[:, u, 0:G], averager[:], src[:, c, t], start=c == 0, stop=c == C - 1)
                    mm.then_inc(ns.mean.sem, 1)
                for n, t, u in pair:
                    pe.wait_ge(*ns.squared.after(n))
                    pe.wait_ge(*ns.logvar.after(n - 2))
                    for c in range(C):
                        mm = nc.tensor.matmul(psum[:, 2 + u, 0:G], averager[:], sq[:, u, c, :], start=c == 0, stop=c == C - 1)
                    mm.then_inc(ns.var.sem, 1)

        @block.scalar
        def _(act):
            if base == 0:
                for x in (ns.squared, ns.logvar, ns.rstd, ns.affined):
                    x.start(act)
            nc.scalar.preload_act_table_set("natural_log_exp_and_others")
            for pair in groups(act):
                for n, t, u in pair:
                    act.wait_ge(*ns.centered.after(n))
                    act.wait_ge(*ns.var.after(n - 2))
                    nc.scalar.activation(sq[:, u], cen[:, u], ACT.Square).then_inc(ns.squared.sem, 1)
                for n, t, u in pair:
                    act.wait_ge(*ns.var.after(n))
                    act.wait_ge(*ns.rstd.after(n - 2))
                    nc.scalar.activation(lv[:, u], psum[:, 2 + u, 0:G], ACT.Ln, bias=eps[:, 0:1]).then_inc(ns.logvar.sem, 1)
                    act.wait_ge(*ns.logvar.after(n))
                    act.wait_ge(*ns.normed.after(n - 2))
                    nc.scalar.activation(rs[:, u], lv[:, u], ACT.Exp, scale=-0.5).then_inc(ns.rstd.sem, 1)
                for n, t, u in pair:
                    if gb is None:
                        act.sem_inc(ns.affined.sem, 1)
                        continue
                    act.wait_ge(*ns.normed.after(n))
                    nc.scalar.activation(dst[:, 0, t], dst[:, 0, t], ACT.Identity, bias=gb[:, 1, 0:1], scale=gb[:, 0, 0:1])
                    nc.scalar.activation(dst[:, 1, t], dst[:, 1, t], ACT.Identity, bias=gb[:, 1, 1:2], scale=gb[:, 0, 1:2]).then_inc(ns.affined.sem, 1)

        @block.vector
        def _(dve):
            if base == 0:
                ns.centered.start(dve)
                ns.normed.start(dve)
            for pair in groups(dve):
                for n, t, u in pair:
                    dve.wait_ge(*ns.mean.after(n))
                    dve.wait_ge(*ns.normed.after(n - 2))
                    dve.wait_ge(*ns.squared.after(n - 2))
                    m = psum[:, u, 0:G].unsqueeze(1).broadcast_to([P, C, G])
                    nc.vector.tensor_tensor(cen[:, u], src[:, :, t], m, ALU.subtract).then_inc(ns.centered.sem, 1)
                for n, t, u in pair:
                    dve.wait_ge(*ns.rstd.after(n))
                    dve.wait_ge(*ns.centered.after(n))
                    r = rs[:, u].unsqueeze(1).broadcast_to([P, C, G])
                    nc.vector.tensor_tensor(dst[:, :, t], cen[:, u], r, ALU.mult).then_inc(ns.normed.sem, 1)




def perceptrons(nc, stage, psum, hT, accT, w_up, w_down, func, combine=None):
    nx = w_up.shape[0]
    gelu = func == ACT.Gelu
    with Scope(nc, stage) as s:
        up = s.sb("up", [P, 2, C, DFF])
        down = s.sb("down", [P, 2, M8, D])
        hidden = s.sb("hidden", [P, M8, G])
        relu = s.sb("relu", [P, 2, G])
        weight = s.sb("weight", [P, 2, TOK])
        part = s.sb("part", [P, C, G])
        loaded = s.loads("weights_loaded", 2)
        weighed = s.loads("token_weights_loaded", 1)
        up_ready = s.counter("up_ready", M8)
        act_done = s.counter("act_done", M8)
        hidden_ready = act_done if gelu else s.counter("hidden_ready", M8)
        hidden_read = s.counter("hidden_read", M8)
        part_ready = s.counter("part_ready", 1)
        added = s.counter("added", 1)
        block = s.block()

        def perceptron_steps(eng, step):
            if nx > 1:
                with eng.Fori(0, nx // 2) as i:
                    for u in range(2):
                        with eng.Fori(0, GROUPS) as g:
                            step(At(GROUPS * u, [(i, 2 * GROUPS), (g, 1)]), At(u, [(i, 2)]), u, g, True)
            with eng.Fori(0, GROUPS) as g:
                step(At(GROUPS * (nx - 1), [(g, 1)]), At(nx - 1), 0, g, False)

        @block.sync
        def _(sp):
            def load(x, weighted):
                u = x.parity
                n = At(x.const * GROUPS, [(r, c * GROUPS) for r, c in x.regs])
                if x.regs or x.const:
                    sp.wait_ge(*hidden_read.after(n - (GROUPS + 1), M8 - 1))
                sp.dma_start(up[:, u], w_up[bass.ds(x.times(1), 1)].rearrange("o (c p) n -> p (o c) n", p=P)).then_inc(loaded.sem(x), 16)
                sp.dma_start(down[:, u], w_down[bass.ds(x.times(1), 1)].rearrange("o (k p) n -> p (o k) n", p=P)).then_inc(loaded.sem(x), 16)
                if weighted:
                    if x.regs or x.const:
                        sp.wait_ge(*added.after(n - (GROUPS + 1)))
                    row = combine[bass.ds(x.times(1), 1), :].broadcast_to([P, TOK])
                    sp.dma_start(weight[:, u], row).then_inc(weighed.sem(x), 16)

            if nx > 1:
                load(At(0), True)
                load(At(1), True)
                with sp.Fori(0, nx // 2 - 1) as i:
                    load(At(2, [(i, 2)]), True)
                    load(At(3, [(i, 2)]), True)
            load(At(nx - 1), False)

        @block.tensor
        def _(pe):
            up_ready.start(pe)
            hidden_read.start(pe)

            def step(n, x, u, g, weighted):
                t = bass.ds(g * G, G)
                pe.wait_ge(*loaded.after(x))
                for m in range(M8):
                    pe.wait_ge(*act_done.after(n if m >= 4 else n - 1, (m - 4) % M8))
                    for c in range(C):
                        mm = nc.tensor.matmul(psum[:, m % 4, 0:G], up[:, u, c, m * P:(m + 1) * P], hT[:, c, t], start=c == 0, stop=c == C - 1)
                    mm.then_inc(up_ready.sem, 1)
                pe.wait_ge(*(added if gelu else part_ready).after(n - 1))
                for k in range(M8):
                    pe.wait_ge(*hidden_ready.after(n, k))
                    for m in range(C):
                        mm = nc.tensor.matmul(psum[:, 4 + m, 0:G], down[:, u, k, m * P:(m + 1) * P], hidden[:, k], start=k == 0, stop=k == M8 - 1)
                    mm.then_inc(hidden_read.sem, 1)

            perceptron_steps(pe, step)

        @block.scalar
        def _(act):
            act_done.start(act)
            nc.scalar.preload_act_table(func)

            def step(n, x, u, g, weighted):
                for m in range(M8):
                    act.wait_ge(*up_ready.after(n, m))
                    if gelu:
                        act.wait_ge(*hidden_read.after(n - 1, m))
                        dst = hidden[:, m]
                    else:
                        act.wait_ge(*hidden_ready.after(n if m >= 2 else n - 1, (m - 2) % M8))
                        dst = relu[:, m % 2]
                    nc.scalar.activation(dst, psum[:, m % 4, 0:G], func).then_inc(act_done.sem, 1)

            perceptron_steps(act, step)

        @block.vector
        def _(dve):
            if not gelu:
                hidden_ready.start(dve)
                part_ready.start(dve)
            added.start(dve)

            def step(n, x, u, g, weighted):
                t = bass.ds(g * G, G)
                if not gelu:
                    for m in range(M8):
                        dve.wait_ge(*act_done.after(n, m))
                        dve.wait_ge(*hidden_read.after(n - 1, m))
                        nc.vector.tensor_tensor(hidden[:, m], relu[:, m % 2], relu[:, m % 2], ALU.mult).then_inc(hidden_ready.sem, 1)
                dve.wait_ge(*hidden_read.after(n, M8 - 1))
                dve.wait_ge(*added.after(n - 1))
                both = psum[:, 4:4 + C, 0:G]
                if gelu:
                    nc.vector.tensor_tensor(accT[:, :, t], accT[:, :, t], both, ALU.add).then_inc(added.sem, 1)
                    return
                if weighted:
                    dve.wait_ge(*weighed.after(x))
                    w = weight[:, u, t].unsqueeze(1).broadcast_to([P, C, G])
                    nc.vector.tensor_tensor(part[:], both, w, ALU.mult).then_inc(part_ready.sem, 1)
                    dve.wait_ge(*part_ready.after(n))
                    nc.vector.tensor_tensor(accT[:, :, t], accT[:, :, t], part[:], ALU.add).then_inc(added.sem, 1)
                else:
                    nc.vector.tensor_tensor(accT[:, :, t], accT[:, :, t], both, ALU.add).then_inc(part_ready.sem, 1)
                    dve.wait_ge(*part_ready.after(n))
                    dve.sem_inc(added.sem, 1)

            perceptron_steps(dve, step)


def add_into(nc, stage, dst, src):
    with Scope(nc, stage) as s:
        block = s.block()

        @block.vector
        def _(dve):
            nc.vector.tensor_tensor(dst[:], dst[:], src[:], ALU.add)




class Units:

    def __init__(self, s, units):
        self.all = units
        self.bank = {name: b for name, b, _ in units}
        self.reader = {name: eng for name, _, eng in units}
        self.made = s.counter("product_made", len(units))
        self.order = {name: k for k, (name, _, _) in enumerate(units)}
        self.read = {}
        for eng in ("act", "dve"):
            named = [name for name, _, e in units if e == eng]
            read = s.counter(f"product_read_by_{eng}", len(named)) if named else None
            self.read.update((name, (read, k)) for k, name in enumerate(named))

    def start_reads(self, eng, which):
        for sig in {sig for name, (sig, _) in self.read.items() if self.reader[name] == which}:
            sig.start(eng)

    def after_made(self, name, n):
        return self.made.after(n, self.order[name])

    def after_read(self, name, n):
        sig, k = self.read[name]
        return sig.after(n, k)

    def bank_before(self, name):
        before = [u for u, b, _ in self.all[:self.order[name]] if b == self.bank[name]]
        return before[-1] if before else None

    def last_in(self, bank):
        return ([None] + [u for u, b, _ in self.all if b == bank])[-1]


UNITS = {
    "future": [("q", 6, "act"), ("f", 4, "act"), ("k", 5, "act"), ("qm", 6, "act"), ("up0", 4, "act"),
               ("up1", 5, "act"), ("v", 6, "act"), ("kf0", 4, "dve"), ("kf1", 5, "dve"),
               ("vf0", 6, "act"), ("vf1", 4, "act")],
    "memory": [("q", 6, "dve"), ("k0", 4, "act"), ("k1", 5, "act"), ("k2", 6, "act"), ("k3", 4, "act"),
               ("v0", 5, "dve"), ("v1", 6, "dve"), ("v2", 4, "dve"), ("v3", 5, "dve")],
    "offset": [("k", 6, "dve"), ("v", 4, "dve")],
    "causal": [("q", 6, "dve"), ("k", 4, "dve"), ("v", 5, "dve")],
}


def attention(nc, stage, kind, psum, const, w, hT, accT, ctxT=None, qT_all=None, gateT=None, skewed=None):
    memory, future, offset = kind == "memory", kind == "future", kind == "offset"
    NS = 8 if memory else NG
    NT = H if memory else NG
    KEYS = NKEY if memory else T
    KR = KC if memory else T
    CHUNKS = NKEY // KC if memory else 1
    NCTX = S2 if memory else T
    OUT_SLOT = NS - 1 if not memory else 4
    scale = 1.0 if future or offset else HD ** -0.5
    ident, identb, maskb = const["ident"], const["identb"], const["maskb"]

    with Scope(nc, stage) as s:
        hb = s.sb("hb", [P, 2, C, T])
        ctx = s.sb("ctx", [P, 2, C, NCTX]) if ctxT is not None else None
        qT = s.sb("qT", [P, 2, NG, T])
        kT = s.sb("kT", [P, 2, NG, NCTX + MEM if memory else T])
        v = s.sb("v", [P, 2, CHUNKS, H, 32])
        rowmax = s.sb("rowmax", [T, 2, H])
        negmax = s.sb("negmax", [T, 2, H]) if memory else None
        probs = s.sb("probs", [T, 2, H, KEYS])
        turned = s.sb("turned", [P, 4, 4, T])
        mixT = s.sb("mixT", [P, 2, NG * T])
        rden = s.sb("rden", [P, 2, NG * T])
        names = [x for x in w if x not in ("m_k", "m_v")]
        wt = {x: s.sb(x, list(w[x][1])) for x in names}
        if future:
            fT = s.sb("fT", [P, 2, C, T])
            qm = s.sb("qm", [T, 2, D])
            upT = s.sb("upT", [P, 2, C, FUT, T])
            vf = s.sb("vf", [T, 2, FUT, D])
            qk = s.sb("qk", [T, FUT, D])
            fscore = s.sb("fscore", [T, 2, FUT, H])
            fmax = s.sb("fmax", [T, 2, H])
            fprob = s.sb("fprob", [T, 2, FUT, H])
            weighted = s.sb("weighted", [T, FUT, D])
            fmix = s.sb("fmix", [T, 2, H, 32])
        if offset:
            factor = s.sb("factor", [T, 2, H, T])
            bias = s.sb("bias", [T, H, T])
        if memory:
            mk = s.sb("mk", [P, NG, MEM])
            mv = s.sb("mv", [MEM, H, HD])
            mvs = s.sb("mvs", [MEM, H, 32])

        units = Units(s, UNITS[kind])
        n_in = 1 + (ctxT is not None) + offset
        inputs = s.loads("inputs_loaded", n_in)
        factors = s.loads("factors_loaded", 1)
        scored = s.counter("scored", NS)
        maxed = s.counter("maxed", NS)
        shifted = s.counter("shifted", NS)
        probs_ready = s.counter("probs_ready", NS)
        tile_turned = s.counter("tile_turned", NT)
        turned_act = s.counter("turned_copied_by_act", NT // 2)
        turned_dve = s.counter("turned_copied_by_dve", NT // 2)
        mixed_in = s.counter("mixed_in", NT)
        dve_step = s.counter("dve_step", 6) if future else s.counter("scaled", NS) if offset else None
        biased = s.counter("biased", NS) if offset else None
        mix_copied = s.counter("mix_copied", 1)
        spread = s.counter("denominators_spread", 1)
        logged = s.counter("denominators_logged", 1)
        inverted = s.counter("denominators_inverted", 1)
        normed = s.counter("mix_normed", 1)
        gated = s.counter("mix_gated", 1) if offset else normed
        projected = s.counter("projected", 1)
        added = s.counter("added", 1)
        max_with_future = s.counter("max_with_future", NS) if future else None
        fexp = s.counter("future_exps", 1) if future else None
        ready = s.chain("ready")

        with nc.Block() as block:

            @block.sync
            def _(sp):
                for x in names:
                    ready.inc(sp.dma_start(wt[x][:], w[x][0]), 16)
                if offset:
                    ready.inc(sp.dma_start(bias[:], skewed["bias"]), 16)
                if memory:
                    ready.inc(sp.dma_start(mk[:], w["m_k"][0]), 16)
                    ready.inc(sp.dma_start(mv[:], w["m_v"][0]), 16)
                sp.wait_ge(ready.sem, ready.n)

            @block.vector
            def _(dve):
                nc.vector.memset(v[:], 1.0)
                if future:
                    nc.vector.memset(fmix[:], 1.0)
                if memory:
                    nc.vector.memset(probs[:, :, :, NKEY - 1:NKEY], 0.0)
                    nc.vector.memset(mvs[:], 1.0)

        if memory:
            with nc.Block() as block:

                @block.vector
                def _(dve):
                    for u in range(2):
                        nc.vector.tensor_scalar(kT[:, u, :, S2:S2 + MEM], mk[:], HD ** 0.5, None, ALU.mult)
                    nc.vector.tensor_scalar(mvs[:, :, 0:HD], mv[:], MEM ** 0.5, None, ALU.mult)

            with nc.Block() as block:

                @block.sync
                def _(sp):
                    first = S2 - 3 * KC
                    for u in range(2):
                        ready.inc(sp.dma_start(v[first:first + MEM, u, 3], mvs[:]), 16)
                    sp.wait_ge(ready.sem, ready.n)

        def slot_heads(j):
            return [2 * j, 2 * j + 1] if memory else [HG * c + j for c in range(NG)]

        def heads_view(ap, j):
            return ap[:, 2 * j:2 * j + 2] if memory else ap.rearrange("p (c j) -> p j c", j=HG)[:, j]

        def turn_tiles(i):
            if memory:
                return [(i, c) for c in range(4)]
            return [(HG * c + i, 0) for c in range(NG)]

        def last_slot(i):
            return i // 2 if memory else i

        block = s.block()

        @block.sync
        def _(sp):
            with sp.Fori(0, NB // 2) as i:
                for u in range(2):
                    n = At(u, [(i, 2)])
                    sp.wait_ge(*units.after_made(units.all[-1][0], n - 2))
                    sp.dma_start(hb[:, u], hT[:, :, tok(n)]).then_inc(inputs.sem(n), 16)
                    if ctxT is not None:
                        src = ctxT[bass.ds(n.times(1), 1)].rearrange("o (c p) s -> p (o c) s", p=P)[:, :, 0:NCTX]
                        sp.dma_start(ctx[:, u], src).then_inc(inputs.sem(n), 16)
                    if offset:
                        start = sp.snap(n.times(H * T * T, T - 1))
                        sp.wait_ge(*dve_step.after(n - 2, NS - 1))
                        src = bass.AP(skewed["dram"].tensor, start, [[T - 1, T], [T * T, H], [1, T]])
                        sp.dma_start(factor[:, u], src).then_inc(factors.sem(n), 16)
                        sp.dma_start(qT[:, u], qT_all[:, :, tok(n)]).then_inc(inputs.sem(n), 16)

        @block.tensor
        def _(pe):
            for x in (units.made, scored, tile_turned, mixed_in, spread, projected):
                x.start(pe)
            src_kv = ctx if ctxT is not None else hb

            def product(parts):
                for out, terms in parts:
                    for k, (a, b) in enumerate(terms):
                        mm = nc.tensor.matmul(out, a, b, start=k == 0, stop=k == len(terms) - 1)
                mm.then_inc(units.made.sem, 1)

            def front(n):
                u = n.parity
                pe.wait_ge(*inputs.after(n))
                for name, b, _ in units.all:
                    before = units.bank_before(name)
                    if before:
                        pe.wait_ge(*units.after_read(before, n))
                    else:
                        pe.wait_ge(*units.after_read(units.last_in(b), n - 1))
                        pe.wait_ge(*(added.after(n - 3) if b == 6 else (turned_act if b == 4 else turned_dve).after(n - 2, NT // 2 - 1)))
                    out = psum[:, b]
                    if name in ("q", "k") and not (name == "k" and memory):
                        src = hb if name == "q" else src_kv
                        product([(out[:, g * T:(g + 1) * T],
                                           [(wt["w" + name][:, c, g * P:(g + 1) * P], src[:, u, c, 0:T]) for c in range(C)])
                                          for g in range(NG)])
                    elif memory and name[0] == "k":
                        g = int(name[1])
                        product([(out[:, 0:S2], [(wt["wk"][:, c, g * P:(g + 1) * P], ctx[:, u, c, :]) for c in range(C)]
                                           + [(const["maskrow"][0:1, :], const["masked"][0:1, bass.ds(n.times(S2), S2)])])])
                    elif memory and name[0] == "v":
                        k0 = int(name[1]) * KC
                        rows = min(KC, S2 - k0)
                        product([(out[0:rows, 0:D], [(ctx[:, u, c, k0:k0 + rows], wt["wv"][:, c, :]) for c in range(C)])])
                    elif name == "v":
                        product([(out[0:T, 0:D], [(src_kv[:, u, c, 0:T], wt["wv"][:, c, :]) for c in range(C)])])
                    elif name == "f":
                        product([(out[:, m * T:(m + 1) * T],
                                           [(wt["wf"][:, c, m * P:(m + 1) * P], hb[:, u, c, :]) for c in range(C)]) for m in range(C)])
                    elif name == "qm":
                        product([(out[0:T, 0:D], [(hb[:, u, c, :], wt["wqm"][:, c, :]) for c in range(C)])])
                    elif name[:2] == "up":
                        m = int(name[2])
                        if m == 0:
                            pe.wait_ge(*units.after_read("f", n))
                        product([(out[:, f * T:(f + 1) * T], [(wt["conv"][:, f, :], fT[:, u, m, :])]) for f in range(FUT)])
                    else:
                        if name == "kf0":
                            pe.wait_ge(*units.after_read("up1", n))
                        half = int(name[2])
                        wx = wt["wkm" if name[0] == "k" else "wv"]
                        product([(out[0:T, f * D:(f + 1) * D],
                                           [(upT[:, u, c, 2 * half + f, :], wx[:, c, :]) for c in range(C)]) for f in range(2)])

            def scores(n, j):
                u = n.parity
                if j == 0:
                    for name in ("q", "k", "k3"):
                        if name in units.reader:
                            pe.wait_ge(*units.after_read(name, n))
                if memory:
                    pe.wait_ge(*probs_ready.after(n if j >= 2 else n - 1, (j - 2) % NS))
                    for b, h in enumerate(slot_heads(j)):
                        r = 32 * (h % HG)
                        mm = nc.tensor.matmul(psum[0:T, 2 * (j % 2) + b, 0:S2 + MEM], qT[r:r + 32, u, h // HG, :], kT[r:r + 32, u, h // HG, :], start=True, stop=True)
                else:
                    pe.wait_ge(*(dve_step if offset else shifted).after(n - 1, j))
                    if not offset:
                        nc.tensor.matmul(psum[0:T, j, 0:G], identb[0:T, 0:T], maskb[:], start=True, stop=False, skip_group_check=True)
                    for c, h in enumerate(slot_heads(j)):
                        r = 32 * j
                        mm = nc.tensor.matmul(psum[0:T, j, c * T:(c + 1) * T], qT[r:r + 32, u, c, :], kT[r:r + 32, u, c, :],
                                              start=offset, stop=True, skip_group_check=not offset)
                mm.then_inc(scored.sem, 1)

            def turn(n, i, last):
                u = n.parity
                if i < 2 and not last and units.last_in(4 + i):
                    pe.wait_ge(*units.after_read(units.last_in(4 + i), n + 1))
                pe.wait_ge(*probs_ready.after(n, last_slot(i)))
                pe.wait_ge(*(turned_act if i % 2 == 0 else turned_dve).after(n if i >= 2 else n - 1, ((i - 2) % NT) // 2))
                for k, (h, c) in enumerate(turn_tiles(i)):
                    col = h if memory else i * NG + k
                    mm = nc.tensor.transpose(psum[0:KR, 4 + i % 2, k * T:(k + 1) * T], probs[:, u, col, c * KR:(c + 1) * KR], ident[0:T, 0:T])
                mm.then_inc(tile_turned.sem, 1)

            def mix(n, i):
                u = n.parity
                if i == 0:
                    for name in ("v", "v3"):
                        if name in units.reader:
                            pe.wait_ge(*units.after_read(name, n))
                    pe.wait_ge(*mix_copied.after(n - 1))
                    if future:
                        pe.wait_ge(*dve_step.after(n, 5))
                        for g in range(NG):
                            nc.tensor.matmul(psum[:, 7, g * T:(g + 1) * T], fmix[:, u, HG * g:HG * (g + 1)].rearrange("p h e -> p (h e)"),
                                             ident[0:T, 0:T], start=g == 0, stop=False, skip_group_check=True)
                wait_for = turned_act if i % 2 == 0 else turned_dve
                pe.wait_ge(*wait_for.after(n, i // 2))
                for k, (h, c) in enumerate(turn_tiles(i)):
                    g, r = h // HG, 32 * (h % HG)
                    mm = nc.tensor.matmul(psum[r:r + 32, 7, g * T:(g + 1) * T], v[0:KR, u, c, h, :], turned[0:KR, i % 4, k, :],
                                          start=c == 0 and not future, stop=c == CHUNKS - 1, skip_group_check=future)
                mm.then_inc(mixed_in.sem, 1)

            def spread_denominators(n, last):
                pe.wait_ge(*units.after_read(units.last_in(6), At(NB - 1) if last else n + 2))
                pe.wait_ge(*added.after(n - 1))
                pe.wait_ge(*mix_copied.after(n))
                nc.tensor.matmul(psum[:, 6, 0:NG * T], const["spreader"][:], mixT[:, n.parity], start=True, stop=True).then_inc(spread.sem, 1)

            def output(n):
                pe.wait_ge(*gated.after(n))
                pe.wait_ge(*inverted.after(n))
                for m in range(C):
                    for g in range(NG):
                        mm = nc.tensor.matmul(psum[:, 6, m * T:(m + 1) * T], wt["wo"][:, g, m * P:(m + 1) * P], mixT[:, n.parity, g * T:(g + 1) * T],
                                              start=g == 0, stop=g == NG - 1)
                mm.then_inc(projected.sem, 1)

            def step(n, now=True, mid=True, end=True):
                if now:
                    front(n)
                for j in range(NS):
                    if now:
                        scores(n, j)
                    if end and j == 0:
                        spread_denominators(n - 2, not now)
                    if end and j == OUT_SLOT:
                        output(n - 2)
                    if mid:
                        for i in range(j * NT // NS, (j + 1) * NT // NS):
                            turn(n - 1, i, not now)
                            if i >= 2:
                                mix(n - 1, i - 2)
                if mid:
                    mix(n - 1, NT - 2)
                    mix(n - 1, NT - 1)

            batch_steps(pe, step)

        @block.scalar
        def _(act):
            units.start_reads(act, "act")
            for x in [probs_ready, turned_act, mix_copied, logged, inverted] + ([fexp] if future else []):
                x.start(act)
            nc.scalar.preload_act_table_set("natural_log_exp_and_others")

            def read(name, n, out, in_, **how):
                act.wait_ge(*units.after_made(name, n))
                nc.scalar.activation(out, in_, ACT.Identity if "bias" in how else ACT.Copy, **how).then_inc(units.read[name][0].sem, 1)

            def front(n):
                u = n.parity
                for name, b, eng in units.all:
                    if eng != "act":
                        continue
                    if memory:
                        if name == "k0":
                            act.wait_ge(*scored.after(n - 2, NS - 1))
                        g = int(name[1])
                        read(name, n, kT[:, u, g, 0:S2], psum[:, b, 0:S2], bias=wt["bk"][:, g:g + 1])
                        continue
                    if name == "q":
                        act.wait_ge(*scored.after(n - 2, NS - 1))
                        read(name, n, qT[:, u], psum[:, b, 0:G].rearrange("p (g t) -> p g t", g=NG), scale=HD ** -0.5)
                    elif name == "k":
                        read(name, n, kT[:, u], psum[:, b, 0:G].rearrange("p (g t) -> p g t", g=NG))
                    elif name == "f":
                        act.wait_ge(*units.after_made("vf1", n - 2))
                        read(name, n, fT[:, u], psum[:, b, 0:C * T].rearrange("p (c t) -> p c t", c=C))
                    elif name == "v":
                        act.wait_ge(*mixed_in.after(n - 2, NT - 1))
                        read(name, n, v[0:T, u, 0, :, 0:HD], psum[0:T, b, 0:D].rearrange("p (h d) -> p h d", h=H))
                    elif name == "qm":
                        act.wait_ge(*units.after_read("kf1", n - 2))
                        read(name, n, qm[:, u], psum[0:T, b, 0:D])
                    elif name[:2] == "up":
                        read(name, n, upT[:, u, int(name[2])], psum[:, b, 0:G].rearrange("p (f t) -> p f t", f=FUT))
                    else:
                        if name == "vf0":
                            act.wait_ge(*dve_step.after(n - 2, 4))
                        k = int(name[2])
                        read(name, n, vf[:, u, 2 * k:2 * k + 2], psum[0:T, b, :].rearrange("p (f d) -> p f d", f=2))

            def exps(n, j):
                u = n.parity
                if memory:
                    act.wait_ge(*shifted.after(n, j))
                    act.wait_ge(*tile_turned.after(n - 2, 2 * j + 1))
                    for b, h in enumerate(slot_heads(j)):
                        e = nc.scalar.activation(probs[:, u, h, 0:S2 + MEM], psum[0:T, 2 * (j % 2) + b, 0:S2 + MEM], ACT.Exp, bias=negmax[:, u, h:h + 1], scale=scale)
                else:
                    act.wait_ge(*shifted.after(n, j))
                    x = probs[:, u, j * NG:(j + 1) * NG, :]
                    e = nc.scalar.activation(x, x, ACT.Exp, scale=scale)
                e.then_inc(probs_ready.sem, 1)

            def copy_turned(n, i):
                act.wait_ge(*tile_turned.after(n, i))
                act.wait_ge(*mixed_in.after(n if i >= 4 else n - 1, (i - 4) % NT))
                nc.scalar.copy(turned[0:KR, i % 4], psum[0:KR, 4 + i % 2, 0:G].rearrange("p (k t) -> p k t", k=4)).then_inc(turned_act.sem, 1)

            def invert(n):
                u = n.parity
                act.wait_ge(*spread.after(n))
                act.wait_ge(*normed.after(n - 2))
                nc.scalar.activation(rden[:, u], psum[:, 6, 0:NG * T], ACT.Ln).then_inc(logged.sem, 1)
                act.wait_ge(*logged.after(n))
                nc.scalar.activation(rden[:, u], rden[:, u], ACT.Exp, scale=-1.0).then_inc(inverted.sem, 1)

            def step(n, now=True, mid=True, end=True):
                if now:
                    front(n)
                for j in range(NS):
                    if mid:
                        for i in range(j * NT // NS, (j + 1) * NT // NS):
                            if i % 2 == 0:
                                copy_turned(n - 1, i)
                    if now:
                        exps(n, j)
                    if end and j == 0:
                        invert(n - 2)
                if now and future:
                    act.wait_ge(*dve_step.after(n, 2))
                    act.wait_ge(*dve_step.after(n - 2, 4))
                    nc.scalar.activation(fprob[:, n.parity], fscore[:, n.parity], ACT.Exp).then_inc(fexp.sem, 1)
                if mid:
                    act.wait_ge(*mixed_in.after(n - 1, NT - 1))
                    act.wait_ge(*projected.after(n - 3))
                    nc.scalar.copy(mixT[:, (n - 1).parity], psum[:, 7, 0:NG * T]).then_inc(mix_copied.sem, 1)

            batch_steps(act, step)

        @block.vector
        def _(dve):
            units.start_reads(dve, "dve")
            for x in [maxed, shifted, turned_dve, added] + ([dve_step, max_with_future] if future else []) + ([dve_step, biased] if offset else []):
                x.start(dve)

            def read(name, n, out, in_, other, op=ALU.add):
                dve.wait_ge(*units.after_made(name, n))
                nc.vector.tensor_tensor(out, in_, other, op).then_inc(units.read[name][0].sem, 1)

            def front(n):
                u = n.parity
                for name, b, eng in units.all:
                    if eng != "dve":
                        continue
                    if name in ("q", "k"):
                        dve.wait_ge(*scored.after(n - 2, NS - 1))
                        dst = qT if name == "q" else kT
                        bb = wt["b" + name][:].unsqueeze(2).broadcast_to([P, NG, T])
                        read(name, n, dst[:, u], psum[:, b, 0:G].rearrange("p (g t) -> p g t", g=NG), bb)
                    elif name[0] == "v":
                        dve.wait_ge(*mixed_in.after(n - 2, NT - 1))
                        c = int(name[1]) if memory else 0
                        rows = min(KC, S2 - c * KC) if memory else T
                        read(name, n, v[0:rows, u, c, :, 0:HD], psum[0:rows, b, 0:D].rearrange("p (h d) -> p h d", h=H),
                             wt["bv"][0:rows, :].rearrange("p (h d) -> p h d", h=H))
                    else:
                        if name == "kf0":
                            dve.wait_ge(*units.after_read("qm", n))
                            dve.wait_ge(*dve_step.after(n - 1, 0))
                        k = int(name[2])
                        read(name, n, qk[:, 2 * k:2 * k + 2], psum[0:T, b, :].rearrange("p (f d) -> p f d", f=2),
                             qm[:, u].unsqueeze(1).broadcast_to([T, 2, D]), ALU.mult)
                if future:
                    dve.wait_ge(*units.after_read("kf1", n))
                    dve.wait_ge(*dve_step.after(n - 2, 2))
                    dve.wait_ge(*fexp.after(n - 2))
                    nc.vector.tensor_reduce(fscore[:, u], qk[:].rearrange("p f (h d) -> p f h d", d=HD), X, ALU.add).then_inc(dve_step.sem, 1)
                    dve.wait_ge(*dve_step.after(n, 0))
                    dve.wait_ge(*max_with_future.after(n - 2, NS - 1))
                    nc.vector.tensor_reduce(fmax[:, u], fscore[:, u].rearrange("p f h -> p h f"), X, ALU.max).then_inc(dve_step.sem, 1)

            def shift(n, j):
                u = n.parity
                dve.wait_ge(*scored.after(n, j))
                mx = heads_view(rowmax[:, u], j)
                if memory:
                    nc.vector.tensor_reduce(mx, psum[0:T, 2 * (j % 2):2 * (j % 2) + 2, 0:S2 + MEM], X, ALU.max).then_inc(maxed.sem, 1)
                    dve.wait_ge(*maxed.after(n, j))
                    dve.wait_ge(*probs_ready.after(n - 2, j))
                    nc.vector.tensor_scalar(heads_view(negmax[:, u], j), mx, -scale, None, ALU.mult).then_inc(shifted.sem, 1)
                    return
                x = probs[:, u, j * NG:(j + 1) * NG, :]
                src = psum[0:T, j, 0:G].rearrange("p (c s) -> p c s", c=NG)
                dve.wait_ge(*tile_turned.after(n - 2, j))
                if offset:
                    f = factor[:, u].rearrange("p (c j) s -> p j c s", j=HG)[:, j]
                    bj = bias[:].rearrange("p (c j) s -> p j c s", j=HG)[:, j]
                    if j == 0:
                        dve.wait_ge(*factors.after(n))
                    nc.vector.scalar_tensor_tensor(x, f, 1.0, src, ALU.add, ALU.mult).then_inc(dve_step.sem, 1)
                    dve.wait_ge(*dve_step.after(n, j))
                    nc.vector.scalar_tensor_tensor(x, x, HD ** -0.5, bj, ALU.mult, ALU.add).then_inc(biased.sem, 1)
                    dve.wait_ge(*biased.after(n, j))
                    src = x
                nc.vector.tensor_reduce(mx, src, X, ALU.max).then_inc(maxed.sem, 1)
                dve.wait_ge(*maxed.after(n, j))
                if future:
                    dve.wait_ge(*dve_step.after(n, 1))
                    nc.vector.tensor_tensor(mx, mx, heads_view(fmax[:, u], j), ALU.max).then_inc(max_with_future.sem, 1)
                    dve.wait_ge(*max_with_future.after(n, j))
                nc.vector.tensor_tensor(x, src, mx.unsqueeze(2).broadcast_to([T, NG, T]), ALU.subtract).then_inc(shifted.sem, 1)

            def copy_turned(n, i):
                dve.wait_ge(*tile_turned.after(n, i))
                dve.wait_ge(*mixed_in.after(n if i >= 4 else n - 1, (i - 4) % NT))
                nc.vector.tensor_copy(turned[0:KR, i % 4], psum[0:KR, 4 + i % 2, 0:G].rearrange("p (k t) -> p k t", k=4)).then_inc(turned_dve.sem, 1)

            def future_centered(n):
                u = n.parity
                dve.wait_ge(*max_with_future.after(n, NS - 1))
                nc.vector.tensor_tensor(fscore[:, u], fscore[:, u], rowmax[:, u].unsqueeze(1).broadcast_to([T, FUT, H]), ALU.subtract).then_inc(dve_step.sem, 1)

            def future_mix(n):
                u = n.parity
                dve.wait_ge(*fexp.after(n))
                dve.wait_ge(*units.after_read("vf1", n))
                dve.wait_ge(*dve_step.after(n - 1, 5))
                dve.wait_ge(*mixed_in.after(n - 2, 0))
                nc.vector.tensor_reduce(fmix[:, u, :, HD:HD + 1].rearrange("p h e -> p (h e)"), fprob[:, u].rearrange("p f h -> p h f"), X, ALU.add).then_inc(dve_step.sem, 1)
                w4 = weighted[:].rearrange("p f (h d) -> p (f h) d", d=HD)
                v4 = vf[:, u].rearrange("p f (h d) -> p (f h) d", d=HD)
                p4 = fprob[:, u].rearrange("p f h -> p (f h)").unsqueeze(2).broadcast_to([T, FUT * H, HD])
                nc.vector.tensor_tensor(w4, v4, p4, ALU.mult).then_inc(dve_step.sem, 1)
                dve.wait_ge(*dve_step.after(n, 4))
                nc.vector.tensor_reduce(fmix[:, u, :, 0:HD], weighted[:].rearrange("p f (h d) -> p h d f", d=HD), X, ALU.add).then_inc(dve_step.sem, 1)

            def add_output(n):
                dve.wait_ge(*projected.after(n))
                out = psum[:, 6, 0:C * T].rearrange("p (c t) -> p c t", c=C)
                if future:
                    nc.vector.tensor_tensor(accT[:, :, tok(n)], accT[:, :, tok(n)], out, ALU.add).then_inc(added.sem, 1)
                    return
                for c in range(C):
                    a = nc.vector.scalar_tensor_tensor(accT[:, c, tok(n)], out[:, c], wt["bo"][:, c:c + 1], accT[:, c, tok(n)], ALU.add, ALU.add)
                a.then_inc(added.sem, 1)

            def step(n, now=True, mid=True, end=True):
                if now:
                    front(n)
                for j in range(NS):
                    if now:
                        shift(n, j)
                    if mid:
                        for i in range(j * NT // NS, (j + 1) * NT // NS):
                            if i % 2:
                                copy_turned(n - 1, i)
                    if end and j == OUT_SLOT:
                        add_output(n - 2)
                if now and future:
                    future_centered(n)
                if now and future:
                    future_mix(n)

            batch_steps(dve, step)

        @block.gpsimd
        def _(pool):
            normed.start(pool)
            if offset:
                gated.start(pool)

            def normalise(n):
                u = n.parity
                pool.wait_ge(*inverted.after(n))
                nc.gpsimd.tensor_tensor(mixT[:, u], mixT[:, u], rden[:, u], ALU.mult).then_inc(normed.sem, 1)
                if offset:
                    pool.wait_ge(*normed.after(n))
                    m = mixT[:, u].rearrange("p (g t) -> p g t", g=NG)
                    nc.gpsimd.tensor_tensor(m, m, gateT[:, :, tok(n)], ALU.mult).then_inc(gated.sem, 1)

            with pool.Fori(0, NB // 2) as i:
                for u in range(2):
                    normalise(At(u, [(i, 2)]))


def offset_factors(nc, psum, w, hT, qT_all, gateT, skewed):
    with Scope(nc, "prep") as s:
        names = ("wq", "bq", "gate_w", "gate_b", "gain", "rel")
        wt = {x: s.sb(x, list(w[x][1])) for x in names}
        loaded = s.chain("weights_loaded")
        with nc.Block() as block:

            @block.sync
            def _(sp):
                for x in names:
                    loaded.inc(sp.dma_start(wt[x][:], w[x][0]), 16)
                sp.wait_ge(loaded.sem, loaded.n)

        made = s.counter("made", 2 * NG)
        q_read = s.counter("queries_read", NG)
        gate_read = s.counter("gates_read", NG)
        gained = s.counter("gained", NG)
        with nc.Block() as block:

            @block.tensor
            def _(pe):
                made.start(pe)
                with pe.Fori(0, GROUPS) as g:
                    n, t = At(0, [(g, 1)]), bass.ds(g * G, G)
                    for k in range(2 * NG):
                        if k < NG:
                            pe.wait_ge(*q_read.after(n - 1, k))
                            lhs = wt["wq"][:, :, k * P:(k + 1) * P]
                        else:
                            pe.wait_ge(*gate_read.after(n - 1, k - NG))
                            lhs = wt["gate_w"][:, :, (k - NG) * P:(k - NG + 1) * P]
                        for c in range(C):
                            mm = nc.tensor.matmul(psum[:, k, 0:G], lhs[:, c], hT[:, c, t], start=c == 0, stop=c == C - 1)
                        mm.then_inc(made.sem, 1)

            @block.scalar
            def _(act):
                gate_read.start(act)
                nc.scalar.preload_act_table(ACT.Sigmoid)
                with act.Fori(0, GROUPS) as g:
                    n, t = At(0, [(g, 1)]), bass.ds(g * G, G)
                    for k in range(NG):
                        act.wait_ge(*made.after(n, NG + k))
                        nc.scalar.activation(gateT[:, k, t], psum[:, NG + k, 0:G], ACT.Sigmoid, bias=wt["gate_b"][:, k:k + 1]).then_inc(gate_read.sem, 1)

            @block.vector
            def _(dve):
                q_read.start(dve)
                gained.start(dve)
                with dve.Fori(0, GROUPS) as g:
                    n, t = At(0, [(g, 1)]), bass.ds(g * G, G)
                    for k in range(NG):
                        dve.wait_ge(*made.after(n, k))
                        nc.vector.tensor_scalar(qT_all[:, k, t], psum[:, k, 0:G], wt["bq"][:, k:k + 1], None, ALU.add).then_inc(q_read.sem, 1)
                    for k in range(NG):
                        dve.wait_ge(*gate_read.after(n, k))
                        nc.vector.tensor_scalar(gateT[:, k, t], gateT[:, k, t], wt["gain"][:, k:k + 1], None, ALU.mult).then_inc(gained.sem, 1)

        qb = s.sb("qb", [P, 2, NG, T])
        rows = s.sb("rows", [T, 2, H, T])
        queries = s.loads("queries_loaded", 1)
        stored = s.loads("rows_stored", 1)
        product = s.counter("product", NG)
        even = s.counter("even_copied", NG // 2)
        odd = s.counter("odd_copied", NG // 2)
        block = s.block()

        def batches(eng):
            with eng.Fori(0, NB // 2) as i:
                yield [At(u, [(i, 2)]) for u in range(2)]

        def head_rows(u, j):
            return rows[:, u].rearrange("p (c j) s -> p j c s", j=HG)[:, j]

        def bank(u, j):
            return psum[0:T, 4 * u + j, 0:G]

        @block.sync
        def _(sp):
            for pair in batches(sp):
                for n in pair:
                    sp.wait_ge(*product.after(n - 2, NG - 1))
                    sp.dma_start(qb[:, n.parity], qT_all[:, :, tok(n)]).then_inc(queries.sem(n), 16)
                for n in pair:
                    start = sp.snap(n.times(H * T * T))
                    sp.wait_ge(*even.after(n, NG // 2 - 1))
                    sp.wait_ge(*odd.after(n, NG // 2 - 1))
                    dst = bass.AP(skewed.tensor, start, [[T, T], [T * T, H], [1, T]])
                    sp.dma_start(dst, rows[:, n.parity]).then_inc(stored.sem(n), 16)
            for n in (At(NB - 2), At(NB - 1)):
                sp.wait_ge(*stored.after(n))

        @block.tensor
        def _(pe):
            product.start(pe)
            for pair in batches(pe):
                for n in pair:
                    u = n.parity
                    pe.wait_ge(*queries.after(n))
                    for j in range(NG):
                        pe.wait_ge(*(odd if j % 2 else even).after(n - 2, j // 2))
                        r = slice(32 * j, 32 * j + 32)
                        for c in range(NG):
                            mm = nc.tensor.matmul(bank(u, j)[:, c * T:(c + 1) * T], qb[r, u, c, :], wt["rel"][r, :], start=True, stop=True)
                        mm.then_inc(product.sem, 1)

        def wait_stored(eng, n):
            half = At(0, [(r, c // 2) for r, c in n.regs])
            eng.wait_ge(stored.sem(n), half.times(16))

        @block.scalar
        def _(act):
            even.start(act)
            for pair in batches(act):
                for n in pair:
                    wait_stored(act, n)
                    for j in (0, 2):
                        act.wait_ge(*product.after(n, j))
                        nc.scalar.copy(head_rows(n.parity, j), bank(n.parity, j).rearrange("p (c s) -> p c s", c=NG)).then_inc(even.sem, 1)

        @block.vector
        def _(dve):
            odd.start(dve)
            for pair in batches(dve):
                for n in pair:
                    wait_stored(dve, n)
                    for j in (1, 3):
                        dve.wait_ge(*product.after(n, j))
                        nc.vector.tensor_copy(head_rows(n.parity, j), bank(n.parity, j).rearrange("p (c s) -> p c s", c=NG)).then_inc(odd.sem, 1)




def router(nc, psum, const, w_router, hT, combine):
    with Scope(nc, "router") as s:
        rw = s.sb("rw", [P, C, E])
        names = ["shifted", "prob", "is1", "rank1", "pick1", "rest", "is2", "rank2", "pick2", "picks", "kept"]
        t = {x: s.sb(x, [T, NB, E]) for x in names}
        small = {x: s.sb(x, [T, NB]) for x in ("mx", "sum", "inv", "top1", "best1", "top2", "best2", "both", "den", "iden")}
        byexpert = s.sb("byexpert", [T, E, NB])
        rowsE = s.sb("rows", [P, T])
        loaded, scored, chain, exped, copied, stored = (s.chain(x) for x in ("loaded", "scored", "chain", "exped", "copied", "stored"))
        turned = s.chain("turned")
        block = s.block()
        links = 22

        @block.sync
        def _(sp):
            sp.dma_start(rw[:], w_router.rearrange("(c p) e -> p c e", p=P)).then_inc(loaded.sem, 16)
            sp.wait_ge(copied.sem, 1)
            sp.dma_start(combine.rearrange("e (b t) -> (e b) t", t=T), rowsE[:]).then_inc(stored.sem, 16)
            sp.wait_ge(stored.sem, 16)

        @block.tensor
        def _(pe):
            pe.wait_ge(loaded.sem, 16)
            for b in range(NB):
                for c in range(C):
                    mm = nc.tensor.matmul(psum[0:T, 0, b * E:(b + 1) * E], hT[:, c, b * T:(b + 1) * T], rw[:, c, :], start=c == 0, stop=c == C - 1)
            mm.then_inc(scored.sem, 1)
            pe.wait_ge(chain.sem, links)
            nc.tensor.transpose(psum[:, 1, 0:T], byexpert[:].rearrange("p e b -> p (e b)"), const["ident"][0:T, 0:T]).then_inc(turned.sem, 1)

        @block.scalar
        def _(act):
            act.wait_ge(chain.sem, 2)
            nc.scalar.activation(t["prob"][:], t["shifted"][:], ACT.Exp).then_inc(exped.sem, 1)
            act.wait_ge(turned.sem, 1)
            nc.scalar.copy(rowsE[:], psum[:, 1, 0:T]).then_inc(copied.sem, 1)

        @block.vector
        def _(dve):
            def link(ins):
                dve.wait_ge(chain.sem, chain.inc(ins))

            def wide(x):
                return small[x][:].unsqueeze(2).broadcast_to([T, NB, E])

            tt, red = nc.vector.tensor_tensor, nc.vector.tensor_reduce
            rank = const["rank"][0:T].unsqueeze(1).broadcast_to([T, NB, E])
            dve.wait_ge(scored.sem, 1)
            logits = psum[0:T, 0, 0:NB * E].rearrange("p (b e) -> p b e", e=E)
            link(red(small["mx"][:], logits, X, ALU.max))
            link(tt(t["shifted"][:], logits, wide("mx"), ALU.subtract))
            dve.wait_ge(exped.sem, 1)
            link(red(small["sum"][:], t["prob"][:], X, ALU.add))
            link(nc.vector.reciprocal(small["inv"][:], small["sum"][:]))
            link(tt(t["kept"][:], t["prob"][:], wide("inv"), ALU.mult))
            link(red(small["top1"][:], t["kept"][:], X, ALU.max))
            link(tt(t["is1"][:], t["kept"][:], wide("top1"), ALU.is_equal))
            link(tt(t["rank1"][:], t["is1"][:], rank, ALU.mult))
            link(red(small["best1"][:], t["rank1"][:], X, ALU.max))
            link(tt(t["pick1"][:], t["rank1"][:], wide("best1"), ALU.is_equal))
            link(nc.vector.scalar_tensor_tensor(t["rest"][:], t["pick1"][:], -4.0, t["kept"][:], ALU.mult, ALU.add))
            link(red(small["top2"][:], t["rest"][:], X, ALU.max))
            link(tt(t["is2"][:], t["rest"][:], wide("top2"), ALU.is_equal))
            link(tt(t["rank2"][:], t["is2"][:], rank, ALU.mult))
            link(red(small["best2"][:], t["rank2"][:], X, ALU.max))
            link(tt(t["pick2"][:], t["rank2"][:], wide("best2"), ALU.is_equal))
            link(tt(t["picks"][:], t["pick1"][:], t["pick2"][:], ALU.add))
            link(tt(t["shifted"][:], t["picks"][:], t["kept"][:], ALU.mult))
            link(tt(small["both"][:], small["top1"][:], small["top2"][:], ALU.add))
            link(nc.vector.tensor_scalar(small["den"][:], small["both"][:], 1e-9, None, ALU.max))
            link(nc.vector.reciprocal(small["iden"][:], small["den"][:]))
            link(tt(byexpert[:].rearrange("p e b -> p b e"), t["shifted"][:], wide("iden"), ALU.mult))
            assert chain.n == 22




def quantised(nc, psum, const, w, hT, accT):
    NT_, FULL, REST = 6, 4, 96
    tiles = [(m, P if m < FULL else REST) for m in range(NT_)]
    first = [m * P if m < FULL else FULL * P + (m - FULL) * REST for m in range(NT_)]
    assert first[-1] + REST == INTER
    with Scope(nc, "quant") as s:
        wg = s.sb("wg", [P, NT_, D])
        wu = s.sb("wu", [P, NT_, D])
        wd = s.sb("wd", [P, C, INTER])
        clips = s.sb("clips", [P, 2])
        clip_sig = s.sb("clip_sig", [P, 2])
        wmax = s.sb("wmax", [P, 2 * NT_ + C])
        wscale = s.sb("wscale", [P, 2 * NT_ + C])
        winv = s.sb("winv", [P, 2 * NT_ + C])
        big = s.sb("big", [P, 3, NT_ * D])
        qb = s.sb("qb", [P, 3, NT_ * D], BF16)
        wgT = s.sb("wgT", [P, C, INTER], BF16)
        wuT = s.sb("wuT", [P, C, INTER], BF16)
        wdT = s.sb("wdT", [P, NT_, D], BF16)
        xq = s.sb("xq", [P, C, TOK], BF16)
        hq = s.sb("hq", [P, NT_, G], BF16)
        h = s.sb("h", [P, NT_, TOK])
        gates = s.sb("gates", [P, 2, G])
        sc = s.sb("scales", [P, 16])
        both = s.sb("both", [P, 2 * NT_])
        outs = s.sb("outs", [P, C])
        hmax = s.sb("hmax", [P, GROUPS * NT_])
        ld = s.chain("ld")

        with nc.Block() as block:

            @block.sync
            def _(sp):
                for dst, src in ((wg, w["gate"]), (wu, w["up"])):
                    ld.inc(sp.dma_start(dst[:, 0:FULL], src[0:FULL * P].rearrange("(m p) n -> p m n", p=P)), 16)
                    ld.inc(sp.dma_start(dst[0:REST, FULL:NT_], src[FULL * P:INTER].rearrange("(m p) n -> p m n", p=REST)), 16)
                ld.inc(sp.dma_start(wd[:], w["down"].rearrange("(c p) n -> p c n", p=P)), 16)
                ld.inc(sp.dma_start(clips[:, 0:1], w["clip_x"].unsqueeze(0).broadcast_to([P, 1])), 16)
                ld.inc(sp.dma_start(clips[:, 1:2], w["clip_down"].unsqueeze(0).broadcast_to([P, 1])), 16)
                sp.wait_ge(ld.sem, ld.n)

            @block.vector
            def _(dve):
                for x in (wmax, hmax):
                    nc.vector.memset(x[:], 1.0)
                nc.vector.memset(sc[:], 0.0)

        parts = [(wg, 0), (wu, 1), (wd, 2)]

        def pieces():
            for a, k in parts[:2]:
                for m, rows in tiles:
                    yield rows, a[0:rows, m], k * NT_ + m, (k, m * D, D)
            for c in range(C):
                yield P, wd[:, c], 2 * NT_ + c, (2, c * INTER, INTER)

        vx, ax, gx, tx = (s.chain(x) for x in ("vx", "ax", "gx", "tx"))
        n_pieces = len(list(pieces()))
        with nc.Block() as block:

            @block.vector
            def _(dve):
                def link(ins):
                    dve.wait_ge(vx.sem, vx.inc(ins))

                nc.vector.memset(hmax[:], 0.0)
                link(nc.vector.tensor_reduce(sc[:, 0:1], hT[:].rearrange("p c t -> p (c t)"), X, ALU.max, apply_absolute_value=True))
                for rows, a, col, _ in pieces():
                    last = nc.vector.tensor_reduce(wmax[0:rows, col:col + 1], a, X, ALU.max, apply_absolute_value=True)
                link(last)
                link(nc.vector.tensor_scalar(wscale[:], wmax[:], 1.0 / QMAX, None, ALU.mult))
                link(nc.vector.reciprocal(winv[:], wscale[:]))
                for k, (rows, a, col, (p, o, width)) in enumerate(pieces()):
                    dve.wait_ge(ax.sem, 2 + k)
                    b = big[0:rows, p, o:o + width]
                    link(nc.vector.tensor_scalar(b, b, ROUND + QMAX, ROUND - QMAX - 1, ALU.min, ALU.max))
                    link(nc.vector.tensor_scalar(qb[0:rows, p, o:o + width], b, ROUND, None, ALU.subtract))

            @block.gpsimd
            def _(pool):
                pool.wait_ge(vx.sem, 1)
                nc.gpsimd.partition_all_reduce(sc[:, 1:2], sc[:, 0:1], P, bass.bass_isa.ReduceOp.max).then_inc(gx.sem, 1)

            @block.scalar
            def _(act):
                nc.scalar.activation(clip_sig[:], clips[:], ACT.Sigmoid).then_inc(ax.sem, 1)
                act.wait_ge(vx.sem, 4)
                for rows, a, col, (p, o, width) in pieces():
                    nc.scalar.activation(big[0:rows, p, o:o + width], a, ACT.Identity, bias=const["round"][0:rows, 0:1], scale=winv[0:rows, col:col + 1]).then_inc(ax.sem, 1)

        turns = [(0, m, c, rows) for m, rows in tiles for c in range(C)] + [(1, m, c, rows) for m, rows in tiles for c in range(C)]
        turns += [(2, m, c, rows) for m, rows in tiles for c in range(C)]
        tp, tr, rx = (s.chain(x) for x in ("tp", "tr", "rx"))
        xf = s.sb("xf", [P, C, TOK])
        with nc.Block() as block:

            @block.tensor
            def _(pe):
                for k, (p, m, c, rows) in enumerate(turns):
                    if k >= 8:
                        pe.wait_ge(tr.sem, k - 7)
                    dst = psum[:, k % 8, :].bitcast(BF16)
                    if p < 2:
                        mm = nc.tensor.transpose(dst[:, 0:rows], qb[0:rows, p, m * D + c * P:m * D + (c + 1) * P], const["identb"][0:rows, 0:rows])
                    else:
                        mm = nc.tensor.transpose(dst[0:rows, 0:P], qb[:, 2, c * INTER + first[m]:c * INTER + first[m] + rows], const["identb"][:])
                    mm.then_inc(tp.sem, 1)

            @block.scalar
            def _(act):
                for k, (p, m, c, rows) in enumerate(turns):
                    act.wait_ge(tp.sem, k + 1)
                    src = psum[:, k % 8, :].bitcast(BF16)
                    if p < 2:
                        nc.scalar.copy((wgT, wuT)[p][:, c, first[m]:first[m] + rows], src[:, 0:rows]).then_inc(tr.sem, 1)
                    else:
                        nc.scalar.copy(wdT[0:rows, m, c * P:(c + 1) * P], src[0:rows, 0:P]).then_inc(tr.sem, 1)

            @block.vector
            def _(dve):
                def link(ins):
                    dve.wait_ge(rx.sem, rx.inc(ins))

                link(nc.vector.scalar_tensor_tensor(sc[:, 2:3], sc[:, 1:2], 1.0 / QMAX, clip_sig[:, 0:1], ALU.mult, ALU.mult))
                link(nc.vector.reciprocal(sc[:, 3:4], sc[:, 2:3]))
                link(nc.vector.tensor_scalar(both[:], wscale[:, 0:2 * NT_], sc[:, 2:3], None, ALU.mult))
                flat = xf[:].rearrange("p c t -> p (c t)")
                link(nc.vector.tensor_scalar(flat, hT[:].rearrange("p c t -> p (c t)"), sc[:, 3:4], ROUND, ALU.mult, ALU.add))
                link(nc.vector.tensor_scalar(flat, flat, ROUND + QMAX, ROUND - QMAX - 1, ALU.min, ALU.max))
                link(nc.vector.tensor_scalar(xq[:].rearrange("p c t -> p (c t)"), flat, ROUND, None, ALU.subtract))

        up_made = s.counter("up_made", 2 * NT_)
        gated = s.counter("gated", NT_)
        joined = s.counter("joined", NT_)
        measured = s.counter("measured", NT_)
        with nc.Block() as block:

            @block.tensor
            def _(pe):
                up_made.start(pe)
                with pe.Fori(0, GROUPS) as g:
                    n, t = At(0, [(g, 1)]), bass.ds(g * G, G)
                    for m, rows in tiles:
                        b = m % 3
                        for k, wT in enumerate((wgT, wuT)):
                            pe.wait_ge(*(gated, joined)[k].after(n if m >= 3 else n - 1, (m - 3) % NT_))
                            for c in range(C):
                                mm = nc.tensor.matmul(psum[0:rows, 2 * b + k, 0:G], wT[:, c, first[m]:first[m] + rows], xq[:, c, t], start=c == 0, stop=c == C - 1)
                            mm.then_inc(up_made.sem, 1)

            @block.scalar
            def _(act):
                gated.start(act)
                nc.scalar.preload_act_table(ACT.Silu)
                with act.Fori(0, GROUPS) as g:
                    n = At(0, [(g, 1)])
                    for m, rows in tiles:
                        act.wait_ge(*up_made.after(n, 2 * m))
                        act.wait_ge(*joined.after(n if m >= 2 else n - 1, (m - 2) % NT_))
                        nc.scalar.activation(gates[0:rows, m % 2], psum[0:rows, 2 * (m % 3), 0:G], ACT.Silu, scale=both[0:rows, m:m + 1]).then_inc(gated.sem, 1)

            @block.vector
            def _(dve):
                joined.start(dve)
                measured.start(dve)
                with dve.Fori(0, GROUPS) as g:
                    n, t = At(0, [(g, 1)]), bass.ds(g * G, G)
                    for m, rows in tiles:
                        dve.wait_ge(*gated.after(n, m))
                        dve.wait_ge(*up_made.after(n, 2 * m + 1))
                        nc.vector.scalar_tensor_tensor(h[0:rows, m, t], psum[0:rows, 2 * (m % 3) + 1, 0:G], both[0:rows, NT_ + m:NT_ + m + 1], gates[0:rows, m % 2], ALU.mult, ALU.mult).then_inc(joined.sem, 1)
                    for m, rows in tiles:
                        dve.wait_ge(*joined.after(n, m))
                        nc.vector.tensor_reduce(hmax[0:rows, bass.ds(g * NT_ + m, 1)], h[0:rows, m, t], X, ALU.max, apply_absolute_value=True).then_inc(measured.sem, 1)

        hx, hg = s.chain("hx"), s.chain("hg")
        with nc.Block() as block:

            @block.vector
            def _(dve):
                def link(ins):
                    dve.wait_ge(hx.sem, hx.inc(ins))

                link(nc.vector.tensor_reduce(sc[:, 4:5], hmax[:], X, ALU.max))
                dve.wait_ge(hg.sem, 1)
                link(nc.vector.scalar_tensor_tensor(sc[:, 6:7], sc[:, 5:6], 1.0 / QMAX, clip_sig[:, 1:2], ALU.mult, ALU.mult))
                link(nc.vector.reciprocal(sc[:, 7:8], sc[:, 6:7]))
                link(nc.vector.tensor_scalar(outs[:], wscale[:, 2 * NT_:2 * NT_ + C], sc[:, 6:7], None, ALU.mult))

            @block.gpsimd
            def _(pool):
                pool.wait_ge(hx.sem, 1)
                nc.gpsimd.partition_all_reduce(sc[:, 5:6], sc[:, 4:5], P, bass.bass_isa.ReduceOp.max).then_inc(hg.sem, 1)

        scaled = s.counter("h_scaled", NT_)
        clipped = s.counter("h_clipped", NT_)
        rounded = s.counter("h_rounded", NT_)
        down_used = s.counter("down_used", NT_)
        added = s.counter("added", 1)
        block = s.block()

        @block.scalar
        def _(act):
            scaled.start(act)
            with act.Fori(0, GROUPS) as g:
                n, t = At(0, [(g, 1)]), bass.ds(g * G, G)
                for m, rows in tiles:
                    nc.scalar.activation(h[0:rows, m, t], h[0:rows, m, t], ACT.Identity, bias=const["round"][0:rows, 0:1], scale=sc[0:rows, 7:8]).then_inc(scaled.sem, 1)

        @block.vector
        def _(dve):
            clipped.start(dve)
            rounded.start(dve)
            added.start(dve)
            with dve.Fori(0, GROUPS) as g:
                n, t = At(0, [(g, 1)]), bass.ds(g * G, G)
                for m, rows in tiles:
                    dve.wait_ge(*scaled.after(n, m))
                    x = h[0:rows, m, t]
                    nc.vector.tensor_scalar(x, x, ROUND + QMAX, ROUND - QMAX - 1, ALU.min, ALU.max).then_inc(clipped.sem, 1)
                    dve.wait_ge(*clipped.after(n, m))
                    dve.wait_ge(*down_used.after(n - 1, m))
                    nc.vector.tensor_scalar(hq[0:rows, m], x, ROUND, None, ALU.subtract).then_inc(rounded.sem, 1)
                dve.wait_ge(*down_used.after(n, NT_ - 1))
                for c in range(C):
                    a = nc.vector.scalar_tensor_tensor(accT[:, c, t], psum[:, c, 0:G], outs[:, c:c + 1], accT[:, c, t], ALU.mult, ALU.add)
                a.then_inc(added.sem, 1)

        @block.tensor
        def _(pe):
            down_used.start(pe)
            with pe.Fori(0, GROUPS) as g:
                n = At(0, [(g, 1)])
                pe.wait_ge(*added.after(n - 1))
                for m, rows in tiles:
                    pe.wait_ge(*rounded.after(n, m))
                    for c in range(C):
                        mm = nc.tensor.matmul(psum[:, c, 0:G], wdT[0:rows, m, c * P:(c + 1) * P], hq[0:rows, m], start=m == 0, stop=m == NT_ - 1)
                    mm.then_inc(down_used.sem, 1)




def decoder(nc, a, out, stages=6):
    with ExitStack() as stack:
        def sb(name, shape, dt=F32):
            return stack.enter_context(nc.sbuf_tensor(name, shape, dt))

        psum = stack.enter_context(nc.psum_tensor("psum", [P, 8, 512], F32))
        xT = sb("xT", [P, C, TOK])
        hT = sb("hT", [P, C, TOK])
        averager = sb("averager", [P, P])
        eps = sb("eps", [P, 1])
        rnd = sb("rnd", [P, 1])
        ident = sb("ident", [P, P])
        identb = sb("identb", [P, P], BF16)
        spreader = sb("spreader", [P, P])
        maskf = sb("maskf", [T, T])
        maskb = sb("maskb", [T, HG * T], BF16)
        rank = sb("rank", [P, E])
        rowf = sb("rowf", [1, P])
        maskrow = sb("maskrow", [1, P], BF16)
        ln1 = sb("ln1", [P, 2, C])
        ln2 = sb("ln2", [P, 2, C])
        flags = sb("flags", [1, NB * S2 // 4], mybir.dt.uint32)
        masked = sb("masked", [1, NB * S2], BF16)
        const = {"ident": ident, "spreader": spreader, "identb": identb, "maskb": maskb, "maskrow": maskrow, "masked": masked, "round": rnd, "rank": rank}
        loaded = Chain(nc.alloc_semaphore("constants_loaded"))

        with nc.Block() as block:

            @block.sync
            def _(sp):
                for dst, src in ((xT[:], a["xT"].rearrange("(c p) t -> p c t", p=P)), (ident[:], a["ident"]), (spreader[:], a["spreader"]), (maskf[:], a["causal"]),
                                 (rank[:], a["rank"]), (rowf[:], a["maskrow"]), (ln1[:], a["ln1"]), (ln2[:], a["ln2"]),
                                 (flags[:], a["mask"])):
                    loaded.inc(sp.dma_start(dst, src), 16)
                sp.wait_ge(loaded.sem, loaded.n)

            @block.vector
            def _(dve):
                nc.vector.memset(averager[:], 1.0 / D)
                nc.vector.memset(eps[:], EPS)
                nc.vector.memset(rnd[:], ROUND)

        with nc.Block() as block:

            @block.vector
            def _(dve):
                nc.vector.tensor_copy(identb[:], ident[:])
                nc.vector.tensor_copy(maskb[:].rearrange("p (g s) -> p g s", g=HG), maskf[:].unsqueeze(1).broadcast_to([T, HG, T]))
                nc.vector.tensor_copy(maskrow[:], rowf[:])
                nc.vector.tensor_scalar(masked[:], flags[:].bitcast(U8), NEG, None, ALU.mult)

        ns = NormSignals(nc)

        def dram(name, shape):
            return nc.dram_tensor(name, shape, F32).ap()

        def fm(x, n):
            return a[x].rearrange("(c p) n -> p c n", p=P), (P, C, n)

        def flat(x, *shape):
            return a[x], shape

        def wide(x):
            return a[x].rearrange("(g p) n -> p g n", p=P), (P, NG, D)

        def row(x):
            return a[x].unsqueeze(0).broadcast_to([P, D]), (P, D)

        with nc.sbuf_tensor("yT", [P, C, TOK], F32) as yT:
            layer_norm(nc, "n0", ns, psum, averager, xT, yT, eps)
            layer_norm(nc, "n1", ns, psum, averager, yT, hT, eps, ln1)
            attention(nc, "a0", "future", psum, const,
                      {"wq": fm("a0_wq", PADW), "wk": fm("a0_wk", PADW), "wv": fm("a0_wv", D), "wf": fm("a0_wf", D),
                       "wqm": fm("a0_wqm", D), "wkm": fm("a0_wkm", D), "conv": flat("a0_conv", P, FUT, P), "wo": wide("a0_wo")}, hT, yT)
            add_into(nc, "s0", xT, yT)
            layer_norm(nc, "n2", ns, psum, averager, yT, hT, eps, ln2)
        perceptrons(nc, "f0", psum, hT, xT, a["a0_ff1"], a["a0_ff2"], ACT.Gelu)
        if stages > 1:
            layer_norm(nc, "n3", ns, psum, averager, xT, hT, eps)
            attention(nc, "x0", "memory", psum, const,
                      {"wq": fm("x0_wq", PADW), "wk": fm("x0_wk", PADW), "wv": fm("x0_wv", D), "wo": wide("x0_wo"),
                       "bq": flat("x0_bq", P, NG), "bk": flat("x0_bk", P, NG), "bv": row("x0_bv"), "bo": flat("x0_bo", P, C),
                       "m_k": flat("x0_mk", P, NG, MEM), "m_v": flat("x0_mv", MEM, H, HD)}, hT, xT, a["ctxT"])
        if stages > 2:
            layer_norm(nc, "n4", ns, psum, averager, xT, hT, eps)
            combine = dram("combine", (E, TOK))
            router(nc, psum, const, a["router_w"], hT, combine)
            perceptrons(nc, "moe", psum, hT, xT, a["moe_up"], a["moe_down"], ACT.Relu, combine)
        if stages > 3:
            layer_norm(nc, "n5", ns, psum, averager, xT, hT, eps)
            with nc.sbuf_tensor("qT_all", [P, NG, TOK], F32) as qT_all, nc.sbuf_tensor("gateT", [P, NG, TOK], F32) as gateT:
                skew = dram("offset_rows", (NB * H * T * T,))
                offset_factors(nc, psum, {"wq": fm("a1_wq", PADW), "bq": flat("a1_bq", P, NG), "gate_w": fm("a1_gate_w", PADW),
                                          "gate_b": flat("a1_gate_b", P, NG), "gain": flat("a1_gain", P, NG), "rel": flat("a1_rel", P, T)},
                               hT, qT_all, gateT, skew)
                attention(nc, "a1", "offset", psum, const,
                          {"wk": fm("a1_wk", PADW), "wv": fm("a1_wv", D), "wo": wide("a1_wo"), "bk": flat("a1_bk", P, NG),
                           "bv": row("a1_bv"), "bo": flat("a1_bo", P, C)}, hT, xT, qT_all=qT_all, gateT=gateT,
                          skewed={"dram": skew, "bias": a["a1_bias"]})
        if stages > 4:
            layer_norm(nc, "n6", ns, psum, averager, xT, hT, eps)
            attention(nc, "x1", "causal", psum, const,
                      {"wq": fm("x1_wq", PADW), "wk": fm("x1_wk", PADW), "wv": fm("x1_wv", D), "wo": wide("x1_wo"),
                       "bq": flat("x1_bq", P, NG), "bk": flat("x1_bk", P, NG), "bv": row("x1_bv"), "bo": flat("x1_bo", P, C)}, hT, xT, a["ctxT"])
        if stages > 5:
            layer_norm(nc, "n7", ns, psum, averager, xT, hT, eps)
            quantised(nc, psum, const, {"gate": a["q_gate"], "up": a["q_up"], "down": a["q_down"], "clip_x": a["q_clip_x"], "clip_down": a["q_clip_down"]}, hT, xT)

        with nc.Block() as block:

            @block.sync
            def _(sp):
                done = Chain(nc.alloc_semaphore("stored"))
                done.inc(sp.dma_start(out.rearrange("(c p) t -> p c t", p=P), xT[:]), 16)
                sp.wait_ge(done.sem, done.n)




def padded_heads(w):
    w = np.asarray(w)
    out = np.zeros(w.shape[:-1] + (H, 32), np.float32)
    out[..., :HD] = w.reshape(w.shape[:-1] + (H, HD))
    return out.reshape(w.shape[:-1] + (PADW,))


def padded_rows(w):
    return np.ascontiguousarray(padded_heads(np.asarray(w).T).T)


def head_rows(b, spare=0.0):
    p = padded_heads(b).reshape(H, 32).copy()
    p[:, HD] = spare
    return np.ascontiguousarray(p.reshape(NG, P).T)


def laid_out(i):
    t = lambda x: np.ascontiguousarray(np.asarray(x).T)
    col = lambda x: np.ascontiguousarray(np.asarray(x).reshape(C, P).T)
    f = {}
    f["xT"] = np.ascontiguousarray(i["x"].reshape(TOK, D).T)
    f["ctxT"] = np.ascontiguousarray(i["ctx_1024"].transpose(0, 2, 1))
    f["mask"] = np.ascontiguousarray(i["mask_Bx1x1xS2_bk0"].reshape(1, NB * S2)).view(np.uint32)
    f["ident"] = np.eye(P, dtype=np.float32)
    f["causal"] = np.where(np.arange(T)[None, :] <= np.arange(T)[:, None], 0.0, NEG).astype(np.float32)
    f["rank"] = np.ascontiguousarray(np.broadcast_to(np.arange(E, 0, -1, dtype=np.float32), (P, E)))
    f["spreader"] = ((np.arange(P)[:, None] // 32 == np.arange(P) // 32) & (np.arange(P)[:, None] % 32 == HD)).astype(np.float32)
    f["maskrow"] = (np.arange(P) % 32 == HD).astype(np.float32)[None]
    for k in (1, 2):
        f[f"ln{k}"] = np.ascontiguousarray(np.stack([col(i[f"L0_attn_ln{k}_g"]), col(i[f"L0_attn_ln{k}_b"])], 1))
    wq, wk, wv, wf = (t(x) for x in np.split(i["L0_attn_W_qkvf"], 4))
    f["a0_wq"], f["a0_wk"], f["a0_wv"], f["a0_wf"], f["a0_wqm"], f["a0_wkm"] = padded_heads(wq), padded_heads(wk), wv, wf, wq, wk
    conv = np.zeros((P // HD, HD, FUT, P // HD, HD), np.float32)
    for h in range(P // HD):
        conv[h, :, :, h, :] = i["L0_attn_W_conv"].transpose(0, 2, 1)
    f["a0_conv"] = conv.reshape(P, FUT, P)
    f["a0_wo"] = padded_rows(t(i["L0_attn_W_proj"]))
    f["a0_ff1"], f["a0_ff2"] = i["L0_attn_W_ff1"][None], i["L0_attn_W_ff2"][None]
    for n, l in (("x0", "L0_xattn"), ("x1", "L1_xattn")):
        tt = t if n == "x0" else np.ascontiguousarray
        f[n + "_wq"], f[n + "_wk"] = padded_heads(tt(i[l + "_Wq"])), padded_heads(tt(i[l + "_Wk"]))
        f[n + "_wv"], f[n + "_wo"] = tt(i[l + "_Wv"]), padded_rows(tt(i[l + "_Wo"]))
        f[n + "_bq"] = head_rows(i[l + "_bq"], 1.0 if n == "x0" else 0.0)
        f[n + "_bk"], f[n + "_bv"], f[n + "_bo"] = head_rows(i[l + "_bk"]), i[l + "_bv"], col(i[l + "_bo"])
    f["x0_mk"] = np.ascontiguousarray(padded_heads(i["L0_xattn_m_k"][0]).reshape(MEM, NG, P).transpose(2, 1, 0))
    f["x0_mv"] = np.ascontiguousarray(i["L0_xattn_m_v"][0].reshape(MEM, H, HD))
    f["router_w"] = t(i["L0_ffn_router_w"])
    f["moe_up"] = np.ascontiguousarray(np.concatenate([i["L0_ffn_w_fc"], i["L0_ffn_shared_fc"][None]]).transpose(0, 2, 1))
    f["moe_down"] = np.ascontiguousarray(np.concatenate([i["L0_ffn_w_proj"], i["L0_ffn_shared_proj"][None]]).transpose(0, 2, 1))
    wq, wk, wv = (t(x) for x in np.split(i["L1_attn_qkv_w"], 3))
    bq, bk, bv = np.split(i["L1_attn_qkv_b"], 3)
    f["a1_wq"], f["a1_wk"], f["a1_wv"], f["a1_wo"] = padded_heads(wq), padded_heads(wk), wv, padded_rows(t(i["L1_attn_out_w"]))
    f["a1_bq"], f["a1_bk"], f["a1_bv"], f["a1_bo"] = head_rows(bq), head_rows(bk), np.ascontiguousarray(bv), col(i["L1_attn_out_b"])
    f["a1_gate_w"], f["a1_gate_b"] = padded_heads(t(i["L1_attn_gate_w"])), head_rows(i["L1_attn_gate_b"])
    f["a1_gain"] = head_rows(np.repeat(i["L1_attn_if_gain"], HD))
    rel = np.zeros((HG, 32, T), np.float32)
    bias = np.full((T, H, T), NEG, np.float32)
    for k, o in enumerate(OFFSETS):
        if o < T:
            rel[:, :HD, T - 1 - o] = i["L1_attn_scale_embed"][k]
            for q in range(o, T):
                bias[q, :, q - o] = i["L1_attn_pos_bias"][k]
    f["a1_rel"], f["a1_bias"] = rel.reshape(P, T), bias
    f["q_gate"], f["q_up"], f["q_down"] = i["L1_ffn_w_gate"], i["L1_ffn_w_up"], i["L1_ffn_w_down"]
    f["q_clip_x"], f["q_clip_down"] = i["L1_ffn_clip_x"], i["L1_ffn_clip_down"]
    return f


def kernel(**inputs):
    import concourse.bacc as bacc
    from concourse.bass_utils import run_bass_kernel_spmd

    fed = {f"in_{k}": np.ascontiguousarray(v) for k, v in laid_out({k: np.asarray(v) for k, v in inputs.items()}).items()}
    nc = bacc.Bacc("TRN2", target_bir_lowering=False, num_devices=1)
    a = {k[3:]: nc.dram_tensor(k, v.shape, mybir.dt.from_np(v.dtype), kind="ExternalInput").ap() for k, v in fed.items()}
    out = nc.dram_tensor("out_xT", (D, TOK), F32, kind="ExternalOutput").ap()
    decoder(nc, a, out)
    r = run_bass_kernel_spmd(nc, [fed], core_ids=[0])
    return np.ascontiguousarray(r.results[0]["out_xT"].T).reshape(NB, T, D)
```

```python
from contextlib import ExitStack

import numpy as np

import concourse.bass as bass
from concourse import mybir

F32 = mybir.dt.float32
BF16 = mybir.dt.bfloat16
U8 = mybir.dt.uint8
U32 = mybir.dt.uint32
ALU = mybir.AluOpType
ACT = mybir.ActivationFunctionType
X = mybir.AxisListType.X

P = 128
NB, T, D = 16, 112, 256
C = D // P
TOK = NB * T
S2, MEM = 375, 64
H, HD = 16, 16
HG = 4
NG = H // HG
PADW = NG * P
FUT = 4
G = 448
GROUPS = TOK // G
DFF, E = 1024, 8
M8 = DFF // P
INTER = 704
KC = 110
NKEY = 4 * KC
NEG = -1e30
EPS = 1e-5
ROUND = 12582912.0
QMAX = 127.0
OFFSETS = [o for o in sorted(set(range(33)) | {48, 64, 96, 128, 192, 256, 384})]


class At:

    def __init__(self, const=0, regs=()):
        self.const, self.regs = const, tuple(regs)

    def __add__(self, k):
        return At(self.const + k, self.regs)

    def __sub__(self, k):
        return self + (-k)

    def times(self, f, plus=0):
        v = self.const * f + plus
        for r, c in self.regs:
            v = r * (c * f) + v
        return v

    @property
    def parity(self):
        return self.const % 2


AHEAD = 4


class Signal:

    def __init__(self, sem, per):
        self.sem, self.per = sem, per

    def start(self, eng):
        eng.sem_inc(self.sem, AHEAD * self.per)

    def after(self, step, k=0):
        return self.sem, step.times(self.per, AHEAD * self.per + k + 1)


class Loads:

    def __init__(self, sems, per):
        self.sems, self.per = sems, per

    def sem(self, step):
        return self.sems[step.const % len(self.sems)]

    def after(self, step):
        ways = len(self.sems)
        turn = At(step.const // ways, [(r, c // ways) for r, c in step.regs])
        return self.sem(step), turn.times(16 * self.per, 16 * self.per)

    def after_one_before(self, step):
        turn = At(0, [(r, c // len(self.sems)) for r, c in step.regs])
        return self.sem(step), turn.times(16 * self.per)


class Chain:

    def __init__(self, sem):
        self.sem, self.n = sem, 0

    def inc(self, ins, by=1):
        ins.then_inc(self.sem, by)
        self.n += by
        return self.n


def tok(step, width=T):
    return bass.ds(step.times(width), width)


def batch_steps(eng, step):
    step(At(0), mid=False, end=False)
    step(At(1), end=False)
    with eng.Fori(0, (NB - 2) // 2) as i:
        step(At(2, [(i, 2)]))
        step(At(3, [(i, 2)]))
    step(At(NB), now=False)
    step(At(NB + 1), now=False, mid=False)


class Scope:

    def __init__(self, nc, stage):
        self.nc, self.stage, self.stack, self.sems = nc, stage, ExitStack(), []

    def __enter__(self):
        self.stack.__enter__()
        return self

    def __exit__(self, *e):
        self.stack.__exit__(*e)
        if self.sems:
            with self.nc.Block() as block:

                @block.gpsimd
                def _(pool):
                    for sem in self.sems:
                        pool.sem_clear(sem)

            for sem in self.sems:
                self.nc.release_semaphore(sem)

    def semaphore(self, name):
        self.sems.append(self.nc.alloc_semaphore(f"{self.stage}_{name}"))
        return self.sems[-1]

    def sb(self, name, shape, dt=F32):
        return self.stack.enter_context(self.nc.sbuf_tensor(f"{self.stage}_{name}", shape, dt))

    def counter(self, name, per):
        return Signal(self.semaphore(name), per)

    def loads(self, name, per, ways=2):
        return Loads([self.semaphore(f"{name}_{w}") for w in range(ways)], per)

    def chain(self, name):
        return Chain(self.semaphore(name))

    def block(self):
        return self.stack.enter_context(self.nc.Block())




class NormSignals:
    def __init__(self, nc):
        self.mean, self.centered, self.squared, self.var, self.logvar, self.rstd, self.normed, self.affined = (
            Signal(nc.alloc_semaphore(f"norm_{name}"), 1)
            for name in ("mean", "centered", "squared", "var", "logvar", "rstd", "normed", "affined"))
        self.steps = 0


def layer_norm(nc, stage, ns, psum, averager, src, dst, eps, gb=None):
    base = ns.steps
    ns.steps += GROUPS
    with Scope(nc, stage) as s:
        cen = s.sb("cen", [P, 2, C, G])
        sq = s.sb("sq", [P, 2, C, G])
        lv = s.sb("lv", [P, 2, G])
        rs = s.sb("rs", [P, 2, G])
        block = s.block()

        def groups(eng):
            with eng.Fori(0, GROUPS // 2) as i:
                yield [(At(base + u, [(i, 2)]), bass.ds(i * (2 * G) + u * G, G), u) for u in (0, 1)]

        @block.tensor
        def _(pe):
            if base == 0:
                ns.mean.start(pe)
                ns.var.start(pe)
            for pair in groups(pe):
                for n, t, u in pair:
                    pe.wait_ge(*ns.centered.after(n - 2))
                    for c in range(C):
                        mm = nc.tensor.matmul(psum[:, u, 0:G], averager[:], src[:, c, t], start=c == 0, stop=c == C - 1)
                    mm.then_inc(ns.mean.sem, 1)
                for n, t, u in pair:
                    pe.wait_ge(*ns.squared.after(n))
                    pe.wait_ge(*ns.logvar.after(n - 2))
                    for c in range(C):
                        mm = nc.tensor.matmul(psum[:, 2 + u, 0:G], averager[:], sq[:, u, c, :], start=c == 0, stop=c == C - 1)
                    mm.then_inc(ns.var.sem, 1)

        @block.scalar
        def _(act):
            if base == 0:
                for x in (ns.squared, ns.logvar, ns.rstd, ns.affined):
                    x.start(act)
            nc.scalar.preload_act_table_set("natural_log_exp_and_others")
            for pair in groups(act):
                for n, t, u in pair:
                    act.wait_ge(*ns.centered.after(n))
                    act.wait_ge(*ns.var.after(n - 2))
                    nc.scalar.activation(sq[:, u], cen[:, u], ACT.Square).then_inc(ns.squared.sem, 1)
                for n, t, u in pair:
                    act.wait_ge(*ns.var.after(n))
                    act.wait_ge(*ns.rstd.after(n - 2))
                    nc.scalar.activation(lv[:, u], psum[:, 2 + u, 0:G], ACT.Ln, bias=eps[:, 0:1]).then_inc(ns.logvar.sem, 1)
                    act.wait_ge(*ns.logvar.after(n))
                    act.wait_ge(*ns.normed.after(n - 2))
                    nc.scalar.activation(rs[:, u], lv[:, u], ACT.Exp, scale=-0.5).then_inc(ns.rstd.sem, 1)
                for n, t, u in pair:
                    if gb is None:
                        act.sem_inc(ns.affined.sem, 1)
                        continue
                    act.wait_ge(*ns.normed.after(n))
                    nc.scalar.activation(dst[:, 0, t], dst[:, 0, t], ACT.Identity, bias=gb[:, 1, 0:1], scale=gb[:, 0, 0:1])
                    nc.scalar.activation(dst[:, 1, t], dst[:, 1, t], ACT.Identity, bias=gb[:, 1, 1:2], scale=gb[:, 0, 1:2]).then_inc(ns.affined.sem, 1)

        @block.vector
        def _(dve):
            if base == 0:
                ns.centered.start(dve)
                ns.normed.start(dve)
            for pair in groups(dve):
                for n, t, u in pair:
                    dve.wait_ge(*ns.mean.after(n))
                    dve.wait_ge(*ns.normed.after(n - 2))
                    dve.wait_ge(*ns.squared.after(n - 2))
                    m = psum[:, u, 0:G].unsqueeze(1).broadcast_to([P, C, G])
                    nc.vector.tensor_tensor(cen[:, u], src[:, :, t], m, ALU.subtract).then_inc(ns.centered.sem, 1)
                for n, t, u in pair:
                    dve.wait_ge(*ns.rstd.after(n))
                    dve.wait_ge(*ns.centered.after(n))
                    r = rs[:, u].unsqueeze(1).broadcast_to([P, C, G])
                    nc.vector.tensor_tensor(dst[:, :, t], cen[:, u], r, ALU.mult).then_inc(ns.normed.sem, 1)




def perceptron(nc, stage, psum, hT, accT, w_up, w_down, func, groups=range(GROUPS), beside=None):
    gelu = func == ACT.Gelu
    with Scope(nc, stage) as s:
        up = s.sb("up", [P, C, DFF])
        down = s.sb("down", [P, M8, D])
        hidden = s.sb("hidden", [P, M8, G])
        relu = None if gelu else s.sb("relu", [P, 2, G])
        up_loaded, down_loaded = s.chain("up_loaded"), s.chain("down_loaded")
        up_ready = s.counter("up_ready", M8)
        act_done = s.counter("act_done", M8)
        hidden_ready = act_done if gelu else s.counter("hidden_ready", M8)
        hidden_read = s.counter("hidden_read", M8)
        added = s.counter("added", 1)
        block = s.block()

        def group_steps(eng, step):
            with eng.Fori(0, len(groups)) as g:
                step(At(0, [(g, 1)]), bass.ds(g * G + groups[0] * G, G))

        if beside:

            @block.gpsimd
            def _(pool):
                beside(pool)

        @block.sync
        def _(sp):
            sp.dma_start(up[:], w_up.rearrange("(c p) n -> p c n", p=P)).then_inc(up_loaded.sem, 16)
            sp.dma_start(down[:], w_down.rearrange("(k p) n -> p k n", p=P)).then_inc(down_loaded.sem, 16)

        @block.tensor
        def _(pe):
            up_ready.start(pe)
            hidden_read.start(pe)

            def step(n, t):
                pe.wait_ge(up_loaded.sem, 16)
                for m in range(M8):
                    pe.wait_ge(*act_done.after(n if m >= 4 else n - 1, (m - 4) % M8))
                    for c in range(C):
                        mm = nc.tensor.matmul(psum[:, m % 4, 0:G], up[:, c, m * P:(m + 1) * P], hT[:, c, t], start=c == 0, stop=c == C - 1)
                    mm.then_inc(up_ready.sem, 1)
                pe.wait_ge(down_loaded.sem, 16)
                pe.wait_ge(*added.after(n - 1))
                for k in range(M8):
                    pe.wait_ge(*hidden_ready.after(n, k))
                    for m in range(C):
                        mm = nc.tensor.matmul(psum[:, 4 + m, 0:G], down[:, k, m * P:(m + 1) * P], hidden[:, k], start=k == 0, stop=k == M8 - 1)
                    mm.then_inc(hidden_read.sem, 1)

            group_steps(pe, step)

        @block.scalar
        def _(act):
            act_done.start(act)
            nc.scalar.preload_act_table(func)

            def step(n, t):
                for m in range(M8):
                    act.wait_ge(*up_ready.after(n, m))
                    if gelu:
                        act.wait_ge(*hidden_read.after(n - 1, m))
                        dst = hidden[:, m]
                    else:
                        act.wait_ge(*hidden_ready.after(n if m >= 2 else n - 1, (m - 2) % M8))
                        dst = relu[:, m % 2]
                    nc.scalar.activation(dst, psum[:, m % 4, 0:G], func).then_inc(act_done.sem, 1)

            group_steps(act, step)

        @block.vector
        def _(dve):
            if not gelu:
                hidden_ready.start(dve)
            added.start(dve)

            def step(n, t):
                if not gelu:
                    for m in range(M8):
                        dve.wait_ge(*act_done.after(n, m))
                        dve.wait_ge(*hidden_read.after(n - 1, m))
                        nc.vector.tensor_tensor(hidden[:, m], relu[:, m % 2], relu[:, m % 2], ALU.mult).then_inc(hidden_ready.sem, 1)
                dve.wait_ge(*hidden_read.after(n, M8 - 1))
                nc.vector.tensor_tensor(accT[:, :, t], accT[:, :, t], psum[:, 4:4 + C, 0:G], ALU.add).then_inc(added.sem, 1)

            group_steps(dve, step)


def add_into(nc, stage, dst, src):
    with Scope(nc, stage) as s:
        block = s.block()

        @block.vector
        def _(dve):
            nc.vector.tensor_tensor(dst[:], dst[:], src[:], ALU.add)




class Units:

    def __init__(self, s, units):
        self.all = units
        self.bank = {name: b for name, b, _ in units}
        self.reader = {name: eng for name, _, eng in units}
        self.made = s.counter("product_made", len(units))
        self.order = {name: k for k, (name, _, _) in enumerate(units)}
        self.read = {}
        for eng in ("act", "dve"):
            named = [name for name, _, e in units if e == eng]
            read = s.counter(f"product_read_by_{eng}", len(named)) if named else None
            self.read.update((name, (read, k)) for k, name in enumerate(named))

    def start_reads(self, eng, which):
        for sig in {sig for name, (sig, _) in self.read.items() if self.reader[name] == which}:
            sig.start(eng)

    def after_made(self, name, n):
        return self.made.after(n, self.order[name])

    def after_read(self, name, n):
        sig, k = self.read[name]
        return sig.after(n, k)

    def bank_before(self, name):
        before = [u for u, b, _ in self.all[:self.order[name]] if b == self.bank[name]]
        return before[-1] if before else None

    def last_in(self, bank):
        return ([None] + [u for u, b, _ in self.all if b == bank])[-1]


UNITS = {
    "future": [("q", 6, "act"), ("f", 4, "act"), ("k", 5, "act"), ("qm", 6, "act"), ("up0", 4, "act"),
               ("up1", 5, "act"), ("v", 6, "act"), ("kf0", 4, "dve"), ("kf1", 5, "dve"),
               ("vf0", 6, "act"), ("vf1", 4, "act")],
    "memory": [("q", 6, "dve"), ("k0", 4, "act"), ("k1", 5, "act"), ("k2", 6, "act"), ("k3", 4, "act"),
               ("v0", 5, "dve"), ("v1", 6, "dve"), ("v2", 4, "dve"), ("v3", 5, "dve")],
    "offset": [("k", 6, "dve"), ("v", 4, "dve")],
    "causal": [("q", 6, "dve"), ("k", 4, "dve"), ("v", 5, "dve")],
}


def attention(nc, stage, kind, psum, const, w, hT, accT, ctxT=None, qT_all=None, gateT=None, skewed=None):
    memory, future, offset = kind == "memory", kind == "future", kind == "offset"
    NS = 8 if memory else NG
    NT = H if memory else NG
    KEYS = NKEY if memory else T
    KR = KC if memory else T
    CHUNKS = NKEY // KC if memory else 1
    NCTX = S2 if memory else T
    OUT_SLOT = NS - 1 if not memory else 4
    scale = 1.0 if future or offset else HD ** -0.5
    ident, identb, maskb = const["ident"], const["identb"], const["maskb"]

    with Scope(nc, stage) as s:
        hb = s.sb("hb", [P, 2, C, T])
        ctx = s.sb("ctx", [P, 2, C, NCTX]) if ctxT is not None else None
        qT = s.sb("qT", [P, 2, NG, T])
        kT = s.sb("kT", [P, 2, NG, NCTX + MEM if memory else T])
        v = s.sb("v", [P, 2, CHUNKS, H, 32])
        rowmax = s.sb("rowmax", [T, 2, H])
        negmax = s.sb("negmax", [T, 2, H]) if memory else None
        probs = s.sb("probs", [T, 2, H, KEYS])
        turned = s.sb("turned", [P, 4, 4, T])
        mixT = s.sb("mixT", [P, 2, NG * T])
        rden = s.sb("rden", [P, 2, NG * T])
        names = [x for x in w if x not in ("m_k", "m_v")]
        wt = {x: s.sb(x, list(w[x][1])) for x in names}
        if future:
            fT = s.sb("fT", [P, 2, C, T])
            qm = s.sb("qm", [T, 2, D])
            upT = s.sb("upT", [P, 2, C, FUT, T])
            vf = s.sb("vf", [T, 2, FUT, D])
            qk = s.sb("qk", [T, FUT, D])
            fscore = s.sb("fscore", [T, 2, FUT, H])
            fmax = s.sb("fmax", [T, 2, H])
            fprob = s.sb("fprob", [T, 2, FUT, H])
            weighted = s.sb("weighted", [T, FUT, D])
            fmix = s.sb("fmix", [T, 2, H, 32])
        if offset:
            factor = s.sb("factor", [T, 2, H, T])
            bias = s.sb("bias", [T, H, T])
        if memory:
            mk = s.sb("mk", [P, NG, MEM])
            mv = s.sb("mv", [MEM, H, HD])
            mvs = s.sb("mvs", [MEM, H, 32])

        units = Units(s, UNITS[kind])
        n_in = 1 + (ctxT is not None) + offset
        inputs = s.loads("inputs_loaded", n_in)
        factors = s.loads("factors_loaded", 1)
        scored = s.counter("scored", NS)
        maxed = s.counter("maxed", NS)
        shifted = s.counter("shifted", NS)
        probs_ready = s.counter("probs_ready", NS)
        tile_turned = s.counter("tile_turned", NT)
        turned_act = s.counter("turned_copied_by_act", NT // 2)
        turned_dve = s.counter("turned_copied_by_dve", NT // 2)
        mixed_in = s.counter("mixed_in", NT)
        dve_step = s.counter("dve_step", 6) if future else s.counter("scaled", NS) if offset else None
        biased = s.counter("biased", NS) if offset else None
        mix_copied = s.counter("mix_copied", 1)
        spread = s.counter("denominators_spread", 1)
        logged = s.counter("denominators_logged", 1)
        inverted = s.counter("denominators_inverted", 1)
        normed = s.counter("mix_normed", 1)
        gated = s.counter("mix_gated", 1) if offset else normed
        projected = s.counter("projected", 1)
        added = s.counter("added", 1)
        max_with_future = s.counter("max_with_future", NS) if future else None
        fexp = s.counter("future_exps", 1) if future else None
        ready = s.chain("ready")

        with nc.Block() as block:

            @block.sync
            def _(sp):
                for x in names:
                    ready.inc(sp.dma_start(wt[x][:], w[x][0]), 16)
                if offset:
                    ready.inc(sp.dma_start(bias[:], skewed["bias"]), 16)
                if memory:
                    ready.inc(sp.dma_start(mk[:], w["m_k"][0]), 16)
                    ready.inc(sp.dma_start(mv[:], w["m_v"][0]), 16)
                sp.wait_ge(ready.sem, ready.n)

            @block.vector
            def _(dve):
                nc.vector.memset(v[:], 1.0)
                if future:
                    nc.vector.memset(fmix[:], 1.0)
                if memory:
                    nc.vector.memset(probs[:, :, :, NKEY - 1:NKEY], 0.0)
                    nc.vector.memset(mvs[:], 1.0)

        if memory:
            with nc.Block() as block:

                @block.vector
                def _(dve):
                    for u in range(2):
                        nc.vector.tensor_scalar(kT[:, u, :, S2:S2 + MEM], mk[:], HD ** 0.5, None, ALU.mult)
                    nc.vector.tensor_scalar(mvs[:, :, 0:HD], mv[:], MEM ** 0.5, None, ALU.mult)

            with nc.Block() as block:

                @block.sync
                def _(sp):
                    first = S2 - 3 * KC
                    for u in range(2):
                        ready.inc(sp.dma_start(v[first:first + MEM, u, 3], mvs[:]), 16)
                    sp.wait_ge(ready.sem, ready.n)

        def slot_heads(j):
            return [2 * j, 2 * j + 1] if memory else [HG * c + j for c in range(NG)]

        def heads_view(ap, j):
            return ap[:, 2 * j:2 * j + 2] if memory else ap.rearrange("p (c j) -> p j c", j=HG)[:, j]

        def turn_tiles(i):
            if memory:
                return [(i, c) for c in range(4)]
            return [(HG * c + i, 0) for c in range(NG)]

        def last_slot(i):
            return i // 2 if memory else i

        block = s.block()

        @block.sync
        def _(sp):
            with sp.Fori(0, NB // 2) as i:
                for u in range(2):
                    n = At(u, [(i, 2)])
                    sp.wait_ge(*units.after_made(units.all[-1][0], n - 2))
                    sp.dma_start(hb[:, u], hT[:, :, tok(n)]).then_inc(inputs.sem(n), 16)
                    if ctxT is not None:
                        src = ctxT[bass.ds(n.times(1), 1)].rearrange("o (c p) s -> p (o c) s", p=P)[:, :, 0:NCTX]
                        sp.dma_start(ctx[:, u], src).then_inc(inputs.sem(n), 16)
                    if offset:
                        start = sp.snap(n.times(H * T * T, T - 1))
                        sp.wait_ge(*dve_step.after(n - 2, NS - 1))
                        src = bass.AP(skewed["dram"].tensor, start, [[T - 1, T], [T * T, H], [1, T]])
                        sp.dma_start(factor[:, u], src).then_inc(factors.sem(n), 16)
                        sp.dma_start(qT[:, u], qT_all[:, :, tok(n)]).then_inc(inputs.sem(n), 16)

        @block.tensor
        def _(pe):
            for x in (units.made, scored, tile_turned, mixed_in, spread, projected):
                x.start(pe)
            src_kv = ctx if ctxT is not None else hb

            def product(parts):
                for out, terms in parts:
                    for k, (a, b) in enumerate(terms):
                        mm = nc.tensor.matmul(out, a, b, start=k == 0, stop=k == len(terms) - 1)
                mm.then_inc(units.made.sem, 1)

            def front(n):
                u = n.parity
                pe.wait_ge(*inputs.after(n))
                for name, b, _ in units.all:
                    before = units.bank_before(name)
                    if before:
                        pe.wait_ge(*units.after_read(before, n))
                    else:
                        pe.wait_ge(*units.after_read(units.last_in(b), n - 1))
                        pe.wait_ge(*(added.after(n - 3) if b == 6 else (turned_act if b == 4 else turned_dve).after(n - 2, NT // 2 - 1)))
                    out = psum[:, b]
                    if name in ("q", "k") and not (name == "k" and memory):
                        src = hb if name == "q" else src_kv
                        product([(out[:, g * T:(g + 1) * T],
                                           [(wt["w" + name][:, c, g * P:(g + 1) * P], src[:, u, c, 0:T]) for c in range(C)])
                                          for g in range(NG)])
                    elif memory and name[0] == "k":
                        g = int(name[1])
                        product([(out[:, 0:S2], [(wt["wk"][:, c, g * P:(g + 1) * P], ctx[:, u, c, :]) for c in range(C)]
                                           + [(const["maskrow"][0:1, :], const["masked"][0:1, bass.ds(n.times(S2), S2)])])])
                    elif memory and name[0] == "v":
                        k0 = int(name[1]) * KC
                        rows = min(KC, S2 - k0)
                        product([(out[0:rows, 0:D], [(ctx[:, u, c, k0:k0 + rows], wt["wv"][:, c, :]) for c in range(C)])])
                    elif name == "v":
                        product([(out[0:T, 0:D], [(src_kv[:, u, c, 0:T], wt["wv"][:, c, :]) for c in range(C)])])
                    elif name == "f":
                        product([(out[:, m * T:(m + 1) * T],
                                           [(wt["wf"][:, c, m * P:(m + 1) * P], hb[:, u, c, :]) for c in range(C)]) for m in range(C)])
                    elif name == "qm":
                        product([(out[0:T, 0:D], [(hb[:, u, c, :], wt["wqm"][:, c, :]) for c in range(C)])])
                    elif name[:2] == "up":
                        m = int(name[2])
                        if m == 0:
                            pe.wait_ge(*units.after_read("f", n))
                        product([(out[:, f * T:(f + 1) * T], [(wt["conv"][:, f, :], fT[:, u, m, :])]) for f in range(FUT)])
                    else:
                        if name == "kf0":
                            pe.wait_ge(*units.after_read("up1", n))
                        half = int(name[2])
                        wx = wt["wkm" if name[0] == "k" else "wv"]
                        product([(out[0:T, f * D:(f + 1) * D],
                                           [(upT[:, u, c, 2 * half + f, :], wx[:, c, :]) for c in range(C)]) for f in range(2)])

            def scores(n, j):
                u = n.parity
                if j == 0:
                    for name in ("q", "k", "k3"):
                        if name in units.reader:
                            pe.wait_ge(*units.after_read(name, n))
                if memory:
                    pe.wait_ge(*probs_ready.after(n if j >= 2 else n - 1, (j - 2) % NS))
                    for b, h in enumerate(slot_heads(j)):
                        r = 32 * (h % HG)
                        mm = nc.tensor.matmul(psum[0:T, 2 * (j % 2) + b, 0:S2 + MEM], qT[r:r + 32, u, h // HG, :], kT[r:r + 32, u, h // HG, :], start=True, stop=True)
                else:
                    pe.wait_ge(*(dve_step if offset else shifted).after(n - 1, j))
                    if not offset:
                        nc.tensor.matmul(psum[0:T, j, 0:G], identb[0:T, 0:T], maskb[:], start=True, stop=False, skip_group_check=True)
                    for c, h in enumerate(slot_heads(j)):
                        r = 32 * j
                        mm = nc.tensor.matmul(psum[0:T, j, c * T:(c + 1) * T], qT[r:r + 32, u, c, :], kT[r:r + 32, u, c, :],
                                              start=offset, stop=True, skip_group_check=not offset)
                mm.then_inc(scored.sem, 1)

            def turn(n, i, last):
                u = n.parity
                if i < 2 and not last and units.last_in(4 + i):
                    pe.wait_ge(*units.after_read(units.last_in(4 + i), n + 1))
                pe.wait_ge(*probs_ready.after(n, last_slot(i)))
                pe.wait_ge(*(turned_act if i % 2 == 0 else turned_dve).after(n if i >= 2 else n - 1, ((i - 2) % NT) // 2))
                for k, (h, c) in enumerate(turn_tiles(i)):
                    col = h if memory else i * NG + k
                    mm = nc.tensor.transpose(psum[0:KR, 4 + i % 2, k * T:(k + 1) * T], probs[:, u, col, c * KR:(c + 1) * KR], ident[0:T, 0:T])
                mm.then_inc(tile_turned.sem, 1)

            def mix(n, i):
                u = n.parity
                if i == 0:
                    for name in ("v", "v3"):
                        if name in units.reader:
                            pe.wait_ge(*units.after_read(name, n))
                    pe.wait_ge(*mix_copied.after(n - 1))
                    if future:
                        pe.wait_ge(*dve_step.after(n, 5))
                        for g in range(NG):
                            nc.tensor.matmul(psum[:, 7, g * T:(g + 1) * T], fmix[:, u, HG * g:HG * (g + 1)].rearrange("p h e -> p (h e)"),
                                             ident[0:T, 0:T], start=g == 0, stop=False, skip_group_check=True)
                wait_for = turned_act if i % 2 == 0 else turned_dve
                pe.wait_ge(*wait_for.after(n, i // 2))
                for k, (h, c) in enumerate(turn_tiles(i)):
                    g, r = h // HG, 32 * (h % HG)
                    mm = nc.tensor.matmul(psum[r:r + 32, 7, g * T:(g + 1) * T], v[0:KR, u, c, h, :], turned[0:KR, i % 4, k, :],
                                          start=c == 0 and not future, stop=c == CHUNKS - 1, skip_group_check=future)
                mm.then_inc(mixed_in.sem, 1)

            def spread_denominators(n, last):
                pe.wait_ge(*units.after_read(units.last_in(6), At(NB - 1) if last else n + 2))
                pe.wait_ge(*added.after(n - 1))
                pe.wait_ge(*mix_copied.after(n))
                nc.tensor.matmul(psum[:, 6, 0:NG * T], const["spreader"][:], mixT[:, n.parity], start=True, stop=True).then_inc(spread.sem, 1)

            def output(n):
                pe.wait_ge(*gated.after(n))
                pe.wait_ge(*inverted.after(n))
                for m in range(C):
                    for g in range(NG):
                        mm = nc.tensor.matmul(psum[:, 6, m * T:(m + 1) * T], wt["wo"][:, g, m * P:(m + 1) * P], mixT[:, n.parity, g * T:(g + 1) * T],
                                              start=g == 0, stop=g == NG - 1)
                mm.then_inc(projected.sem, 1)

            def step(n, now=True, mid=True, end=True):
                if now:
                    front(n)
                for j in range(NS):
                    if now:
                        scores(n, j)
                    if end and j == 0:
                        spread_denominators(n - 2, not now)
                    if end and j == OUT_SLOT:
                        output(n - 2)
                    if mid:
                        for i in range(j * NT // NS, (j + 1) * NT // NS):
                            turn(n - 1, i, not now)
                            if i >= 2:
                                mix(n - 1, i - 2)
                if mid:
                    mix(n - 1, NT - 2)
                    mix(n - 1, NT - 1)

            batch_steps(pe, step)

        @block.scalar
        def _(act):
            units.start_reads(act, "act")
            for x in [probs_ready, turned_act, mix_copied, logged, inverted] + ([fexp] if future else []):
                x.start(act)
            nc.scalar.preload_act_table_set("natural_log_exp_and_others")

            def read(name, n, out, in_, **how):
                act.wait_ge(*units.after_made(name, n))
                nc.scalar.activation(out, in_, ACT.Identity if "bias" in how else ACT.Copy, **how).then_inc(units.read[name][0].sem, 1)

            def front(n):
                u = n.parity
                for name, b, eng in units.all:
                    if eng != "act":
                        continue
                    if memory:
                        if name == "k0":
                            act.wait_ge(*scored.after(n - 2, NS - 1))
                        g = int(name[1])
                        read(name, n, kT[:, u, g, 0:S2], psum[:, b, 0:S2], bias=wt["bk"][:, g:g + 1])
                        continue
                    if name == "q":
                        act.wait_ge(*scored.after(n - 2, NS - 1))
                        read(name, n, qT[:, u], psum[:, b, 0:G].rearrange("p (g t) -> p g t", g=NG), scale=HD ** -0.5)
                    elif name == "k":
                        read(name, n, kT[:, u], psum[:, b, 0:G].rearrange("p (g t) -> p g t", g=NG))
                    elif name == "f":
                        act.wait_ge(*units.after_made("vf1", n - 2))
                        read(name, n, fT[:, u], psum[:, b, 0:C * T].rearrange("p (c t) -> p c t", c=C))
                    elif name == "v":
                        act.wait_ge(*mixed_in.after(n - 2, NT - 1))
                        read(name, n, v[0:T, u, 0, :, 0:HD], psum[0:T, b, 0:D].rearrange("p (h d) -> p h d", h=H))
                    elif name == "qm":
                        act.wait_ge(*units.after_read("kf1", n - 2))
                        read(name, n, qm[:, u], psum[0:T, b, 0:D])
                    elif name[:2] == "up":
                        read(name, n, upT[:, u, int(name[2])], psum[:, b, 0:G].rearrange("p (f t) -> p f t", f=FUT))
                    else:
                        if name == "vf0":
                            act.wait_ge(*dve_step.after(n - 2, 4))
                        k = int(name[2])
                        read(name, n, vf[:, u, 2 * k:2 * k + 2], psum[0:T, b, :].rearrange("p (f d) -> p f d", f=2))

            def exps(n, j):
                u = n.parity
                if memory:
                    act.wait_ge(*shifted.after(n, j))
                    act.wait_ge(*tile_turned.after(n - 2, 2 * j + 1))
                    for b, h in enumerate(slot_heads(j)):
                        e = nc.scalar.activation(probs[:, u, h, 0:S2 + MEM], psum[0:T, 2 * (j % 2) + b, 0:S2 + MEM], ACT.Exp, bias=negmax[:, u, h:h + 1], scale=scale)
                else:
                    act.wait_ge(*shifted.after(n, j))
                    x = probs[:, u, j * NG:(j + 1) * NG, :]
                    e = nc.scalar.activation(x, x, ACT.Exp, scale=scale)
                e.then_inc(probs_ready.sem, 1)

            def copy_turned(n, i):
                act.wait_ge(*tile_turned.after(n, i))
                act.wait_ge(*mixed_in.after(n if i >= 4 else n - 1, (i - 4) % NT))
                nc.scalar.copy(turned[0:KR, i % 4], psum[0:KR, 4 + i % 2, 0:G].rearrange("p (k t) -> p k t", k=4)).then_inc(turned_act.sem, 1)

            def invert(n):
                u = n.parity
                act.wait_ge(*spread.after(n))
                act.wait_ge(*normed.after(n - 2))
                nc.scalar.activation(rden[:, u], psum[:, 6, 0:NG * T], ACT.Ln).then_inc(logged.sem, 1)
                act.wait_ge(*logged.after(n))
                nc.scalar.activation(rden[:, u], rden[:, u], ACT.Exp, scale=-1.0).then_inc(inverted.sem, 1)

            def step(n, now=True, mid=True, end=True):
                if now:
                    front(n)
                for j in range(NS):
                    if mid:
                        for i in range(j * NT // NS, (j + 1) * NT // NS):
                            if i % 2 == 0:
                                copy_turned(n - 1, i)
                    if now:
                        exps(n, j)
                    if end and j == 0:
                        invert(n - 2)
                if now and future:
                    act.wait_ge(*dve_step.after(n, 2))
                    act.wait_ge(*dve_step.after(n - 2, 4))
                    nc.scalar.activation(fprob[:, n.parity], fscore[:, n.parity], ACT.Exp).then_inc(fexp.sem, 1)
                if mid:
                    act.wait_ge(*mixed_in.after(n - 1, NT - 1))
                    act.wait_ge(*projected.after(n - 3))
                    nc.scalar.copy(mixT[:, (n - 1).parity], psum[:, 7, 0:NG * T]).then_inc(mix_copied.sem, 1)

            batch_steps(act, step)

        @block.vector
        def _(dve):
            units.start_reads(dve, "dve")
            for x in [maxed, shifted, turned_dve, added] + ([dve_step, max_with_future] if future else []) + ([dve_step, biased] if offset else []):
                x.start(dve)

            def read(name, n, out, in_, other, op=ALU.add):
                dve.wait_ge(*units.after_made(name, n))
                nc.vector.tensor_tensor(out, in_, other, op).then_inc(units.read[name][0].sem, 1)

            def front(n):
                u = n.parity
                for name, b, eng in units.all:
                    if eng != "dve":
                        continue
                    if name in ("q", "k"):
                        dve.wait_ge(*scored.after(n - 2, NS - 1))
                        dst = qT if name == "q" else kT
                        bb = wt["b" + name][:].unsqueeze(2).broadcast_to([P, NG, T])
                        read(name, n, dst[:, u], psum[:, b, 0:G].rearrange("p (g t) -> p g t", g=NG), bb)
                    elif name[0] == "v":
                        dve.wait_ge(*mixed_in.after(n - 2, NT - 1))
                        c = int(name[1]) if memory else 0
                        rows = min(KC, S2 - c * KC) if memory else T
                        read(name, n, v[0:rows, u, c, :, 0:HD], psum[0:rows, b, 0:D].rearrange("p (h d) -> p h d", h=H),
                             wt["bv"][0:rows, :].rearrange("p (h d) -> p h d", h=H))
                    else:
                        if name == "kf0":
                            dve.wait_ge(*units.after_read("qm", n))
                            dve.wait_ge(*dve_step.after(n - 1, 0))
                        k = int(name[2])
                        read(name, n, qk[:, 2 * k:2 * k + 2], psum[0:T, b, :].rearrange("p (f d) -> p f d", f=2),
                             qm[:, u].unsqueeze(1).broadcast_to([T, 2, D]), ALU.mult)
                if future:
                    dve.wait_ge(*units.after_read("kf1", n))
                    dve.wait_ge(*dve_step.after(n - 2, 2))
                    dve.wait_ge(*fexp.after(n - 2))
                    nc.vector.tensor_reduce(fscore[:, u], qk[:].rearrange("p f (h d) -> p f h d", d=HD), X, ALU.add).then_inc(dve_step.sem, 1)
                    dve.wait_ge(*dve_step.after(n, 0))
                    dve.wait_ge(*max_with_future.after(n - 2, NS - 1))
                    nc.vector.tensor_reduce(fmax[:, u], fscore[:, u].rearrange("p f h -> p h f"), X, ALU.max).then_inc(dve_step.sem, 1)

            def shift(n, j):
                u = n.parity
                dve.wait_ge(*scored.after(n, j))
                mx = heads_view(rowmax[:, u], j)
                if memory:
                    nc.vector.tensor_reduce(mx, psum[0:T, 2 * (j % 2):2 * (j % 2) + 2, 0:S2 + MEM], X, ALU.max).then_inc(maxed.sem, 1)
                    dve.wait_ge(*maxed.after(n, j))
                    dve.wait_ge(*probs_ready.after(n - 2, j))
                    nc.vector.tensor_scalar(heads_view(negmax[:, u], j), mx, -scale, None, ALU.mult).then_inc(shifted.sem, 1)
                    return
                x = probs[:, u, j * NG:(j + 1) * NG, :]
                src = psum[0:T, j, 0:G].rearrange("p (c s) -> p c s", c=NG)
                dve.wait_ge(*tile_turned.after(n - 2, j))
                if offset:
                    f = factor[:, u].rearrange("p (c j) s -> p j c s", j=HG)[:, j]
                    bj = bias[:].rearrange("p (c j) s -> p j c s", j=HG)[:, j]
                    if j == 0:
                        dve.wait_ge(*factors.after(n))
                    nc.vector.scalar_tensor_tensor(x, f, 1.0, src, ALU.add, ALU.mult).then_inc(dve_step.sem, 1)
                    dve.wait_ge(*dve_step.after(n, j))
                    nc.vector.scalar_tensor_tensor(x, x, HD ** -0.5, bj, ALU.mult, ALU.add).then_inc(biased.sem, 1)
                    dve.wait_ge(*biased.after(n, j))
                    src = x
                nc.vector.tensor_reduce(mx, src, X, ALU.max).then_inc(maxed.sem, 1)
                dve.wait_ge(*maxed.after(n, j))
                if future:
                    dve.wait_ge(*dve_step.after(n, 1))
                    nc.vector.tensor_tensor(mx, mx, heads_view(fmax[:, u], j), ALU.max).then_inc(max_with_future.sem, 1)
                    dve.wait_ge(*max_with_future.after(n, j))
                nc.vector.tensor_tensor(x, src, mx.unsqueeze(2).broadcast_to([T, NG, T]), ALU.subtract).then_inc(shifted.sem, 1)

            def copy_turned(n, i):
                dve.wait_ge(*tile_turned.after(n, i))
                dve.wait_ge(*mixed_in.after(n if i >= 4 else n - 1, (i - 4) % NT))
                nc.vector.tensor_copy(turned[0:KR, i % 4], psum[0:KR, 4 + i % 2, 0:G].rearrange("p (k t) -> p k t", k=4)).then_inc(turned_dve.sem, 1)

            def future_centered(n):
                u = n.parity
                dve.wait_ge(*max_with_future.after(n, NS - 1))
                nc.vector.tensor_tensor(fscore[:, u], fscore[:, u], rowmax[:, u].unsqueeze(1).broadcast_to([T, FUT, H]), ALU.subtract).then_inc(dve_step.sem, 1)

            def future_mix(n):
                u = n.parity
                dve.wait_ge(*fexp.after(n))
                dve.wait_ge(*units.after_read("vf1", n))
                dve.wait_ge(*dve_step.after(n - 1, 5))
                dve.wait_ge(*mixed_in.after(n - 2, 0))
                nc.vector.tensor_reduce(fmix[:, u, :, HD:HD + 1].rearrange("p h e -> p (h e)"), fprob[:, u].rearrange("p f h -> p h f"), X, ALU.add).then_inc(dve_step.sem, 1)
                w4 = weighted[:].rearrange("p f (h d) -> p (f h) d", d=HD)
                v4 = vf[:, u].rearrange("p f (h d) -> p (f h) d", d=HD)
                p4 = fprob[:, u].rearrange("p f h -> p (f h)").unsqueeze(2).broadcast_to([T, FUT * H, HD])
                nc.vector.tensor_tensor(w4, v4, p4, ALU.mult).then_inc(dve_step.sem, 1)
                dve.wait_ge(*dve_step.after(n, 4))
                nc.vector.tensor_reduce(fmix[:, u, :, 0:HD], weighted[:].rearrange("p f (h d) -> p h d f", d=HD), X, ALU.add).then_inc(dve_step.sem, 1)

            def add_output(n):
                dve.wait_ge(*projected.after(n))
                out = psum[:, 6, 0:C * T].rearrange("p (c t) -> p c t", c=C)
                if future:
                    nc.vector.tensor_tensor(accT[:, :, tok(n)], accT[:, :, tok(n)], out, ALU.add).then_inc(added.sem, 1)
                    return
                for c in range(C):
                    a = nc.vector.scalar_tensor_tensor(accT[:, c, tok(n)], out[:, c], wt["bo"][:, c:c + 1], accT[:, c, tok(n)], ALU.add, ALU.add)
                a.then_inc(added.sem, 1)

            def step(n, now=True, mid=True, end=True):
                if now:
                    front(n)
                for j in range(NS):
                    if now:
                        shift(n, j)
                    if mid:
                        for i in range(j * NT // NS, (j + 1) * NT // NS):
                            if i % 2:
                                copy_turned(n - 1, i)
                    if end and j == OUT_SLOT:
                        add_output(n - 2)
                if now and future:
                    future_centered(n)
                if now and future:
                    future_mix(n)

            batch_steps(dve, step)

        @block.gpsimd
        def _(pool):
            normed.start(pool)
            if offset:
                gated.start(pool)

            def normalise(n):
                u = n.parity
                pool.wait_ge(*inverted.after(n))
                nc.gpsimd.tensor_tensor(mixT[:, u], mixT[:, u], rden[:, u], ALU.mult).then_inc(normed.sem, 1)
                if offset:
                    pool.wait_ge(*normed.after(n))
                    m = mixT[:, u].rearrange("p (g t) -> p g t", g=NG)
                    nc.gpsimd.tensor_tensor(m, m, gateT[:, :, tok(n)], ALU.mult).then_inc(gated.sem, 1)

            with pool.Fori(0, NB // 2) as i:
                for u in range(2):
                    normalise(At(u, [(i, 2)]))


def offset_factors(nc, psum, w, hT, qT_all, gateT, skewed):
    with Scope(nc, "prep") as s:
        names = ("wq", "bq", "gate_w", "gate_b", "gain", "rel")
        wt = {x: s.sb(x, list(w[x][1])) for x in names}
        loaded = s.chain("weights_loaded")
        with nc.Block() as block:

            @block.sync
            def _(sp):
                for x in names:
                    loaded.inc(sp.dma_start(wt[x][:], w[x][0]), 16)
                sp.wait_ge(loaded.sem, loaded.n)

        made = s.counter("made", 2 * NG)
        q_read = s.counter("queries_read", NG)
        gate_read = s.counter("gates_read", NG)
        gained = s.counter("gained", NG)
        with nc.Block() as block:

            @block.tensor
            def _(pe):
                made.start(pe)
                with pe.Fori(0, GROUPS) as g:
                    n, t = At(0, [(g, 1)]), bass.ds(g * G, G)
                    for k in range(2 * NG):
                        if k < NG:
                            pe.wait_ge(*q_read.after(n - 1, k))
                            lhs = wt["wq"][:, :, k * P:(k + 1) * P]
                        else:
                            pe.wait_ge(*gate_read.after(n - 1, k - NG))
                            lhs = wt["gate_w"][:, :, (k - NG) * P:(k - NG + 1) * P]
                        for c in range(C):
                            mm = nc.tensor.matmul(psum[:, k, 0:G], lhs[:, c], hT[:, c, t], start=c == 0, stop=c == C - 1)
                        mm.then_inc(made.sem, 1)

            @block.scalar
            def _(act):
                gate_read.start(act)
                nc.scalar.preload_act_table(ACT.Sigmoid)
                with act.Fori(0, GROUPS) as g:
                    n, t = At(0, [(g, 1)]), bass.ds(g * G, G)
                    for k in range(NG):
                        act.wait_ge(*made.after(n, NG + k))
                        nc.scalar.activation(gateT[:, k, t], psum[:, NG + k, 0:G], ACT.Sigmoid, bias=wt["gate_b"][:, k:k + 1]).then_inc(gate_read.sem, 1)

            @block.vector
            def _(dve):
                q_read.start(dve)
                gained.start(dve)
                with dve.Fori(0, GROUPS) as g:
                    n, t = At(0, [(g, 1)]), bass.ds(g * G, G)
                    for k in range(NG):
                        dve.wait_ge(*made.after(n, k))
                        nc.vector.tensor_scalar(qT_all[:, k, t], psum[:, k, 0:G], wt["bq"][:, k:k + 1], None, ALU.add).then_inc(q_read.sem, 1)
                    for k in range(NG):
                        dve.wait_ge(*gate_read.after(n, k))
                        nc.vector.tensor_scalar(gateT[:, k, t], gateT[:, k, t], wt["gain"][:, k:k + 1], None, ALU.mult).then_inc(gained.sem, 1)

        WAYS = 4
        qb = s.sb("qb", [P, WAYS, NG, T])
        rows = s.sb("rows", [T, WAYS, H, T])
        queries = s.loads("queries_loaded", 1, WAYS)
        stored = s.loads("rows_stored", 1, WAYS)
        product = s.counter("product", NG)
        even = s.counter("even_copied", NG // 2)
        odd = s.counter("odd_copied", NG // 2)
        block = s.block()

        def batches(eng):
            with eng.Fori(0, NB // WAYS) as i:
                yield [(At(k, [(i, WAYS)]), k) for k in range(WAYS)]

        def head_rows(k, j):
            return rows[:, k].rearrange("p (c j) s -> p j c s", j=HG)[:, j]

        def bank(k, j):
            return psum[0:T, 4 * (k % 2) + j, 0:G]

        @block.sync
        def _(sp):
            def load(n, k):
                sp.dma_start(qb[:, k], qT_all[:, :, tok(n)]).then_inc(queries.sem(n), 16)

            def store(n, k):
                start = sp.snap(n.times(H * T * T))
                sp.wait_ge(*even.after(n, NG // 2 - 1))
                sp.wait_ge(*odd.after(n, NG // 2 - 1))
                dst = bass.AP(skewed.tensor, start, [[T, T], [T * T, H], [1, T]])
                sp.dma_start(dst, rows[:, k]).then_inc(stored.sem(n), 16)

            for k in range(WAYS):
                load(At(k), k)
            with sp.Fori(0, NB // WAYS - 1) as i:
                for k in range(WAYS):
                    store(At(k, [(i, WAYS)]), k)
                    load(At(k + WAYS, [(i, WAYS)]), k)
            for k in range(WAYS):
                store(At(NB - WAYS + k), k)
            for k in range(WAYS):
                sp.wait_ge(*stored.after(At(NB - WAYS + k)))

        @block.tensor
        def _(pe):
            product.start(pe)
            for some in batches(pe):
                for n, k in some:
                    pe.wait_ge(*queries.after(n))
                    for j in range(NG):
                        pe.wait_ge(*(odd if j % 2 else even).after(n - 2, j // 2))
                        r = slice(32 * j, 32 * j + 32)
                        for c in range(NG):
                            mm = nc.tensor.matmul(bank(k, j)[:, c * T:(c + 1) * T], qb[r, k, c, :], wt["rel"][r, :], start=True, stop=True)
                        mm.then_inc(product.sem, 1)

        @block.scalar
        def _(act):
            even.start(act)
            for some in batches(act):
                for n, k in some:
                    act.wait_ge(*stored.after_one_before(n))
                    for j in (0, 2):
                        act.wait_ge(*product.after(n, j))
                        nc.scalar.copy(head_rows(k, j), bank(k, j).rearrange("p (c s) -> p c s", c=NG)).then_inc(even.sem, 1)

        @block.vector
        def _(dve):
            odd.start(dve)
            for some in batches(dve):
                for n, k in some:
                    dve.wait_ge(*stored.after_one_before(n))
                    for j in (1, 3):
                        dve.wait_ge(*product.after(n, j))
                        nc.vector.tensor_copy(head_rows(k, j), bank(k, j).rearrange("p (c s) -> p c s", c=NG)).then_inc(odd.sem, 1)




BLOCK = 256
HALVES = BLOCK // P
BLOCKS = (2 * TOK - E) // BLOCK + E
SLOTS = BLOCKS * BLOCK


FETCH = 2


class Routes:

    def __init__(self, nc, sb, slots_x, slots_y):
        self.hrow = sb("hrow", [T, NB, D])
        self.result = [self.hrow, sb("second_result", [T, NB, D])]
        self.slot = [sb(f"slot{k}", [T, NB], U32) for k in range(2)]
        self.weight = [sb(f"route_weight{k}", [T, NB]) for k in range(2)]
        self.expert = sb("block_expert", [1, BLOCKS], U32)
        self.slots_x, self.slots_y = slots_x, slots_y
        self.scattered = Chain(nc.alloc_semaphore("tokens_scattered"))
        self.fetched = [Chain(nc.alloc_semaphore(f"results_fetched{k}")) for k in range(NB // FETCH)]


def scatter_tokens(nc, pool, routes, zeroed):
    pool.wait_ge(zeroed.sem, zeroed.n)
    for k in range(2):
        for b in range(NB):
            routes.scattered.inc(nc.gpsimd.indirect_dma_start(
                routes.slots_x, bass.IndirectOffsetOnAxis(ap=routes.slot[k][:, b:b + 1], axis=0), routes.hrow[:, b, :], None), 16)


def gather_results(nc, pool, routes):
    for b in range(NB):
        for k in range(2):
            routes.fetched[b // FETCH].inc(nc.gpsimd.indirect_dma_start(
                routes.result[k][:, b, :], None, routes.slots_y, bass.IndirectOffsetOnAxis(ap=routes.slot[k][:, b:b + 1], axis=0)), 16)


def router(nc, psum, const, w_router, hT, routes):
    with Scope(nc, "router") as s:
        rw = s.sb("rw", [P, C, E])
        plan = s.sb("plan", [P, T + 3 * P + 1 + BLOCKS])
        before = plan[0:T, 0:T]
        earlier = plan[:, T:T + P]
        same = plan[:, T + P:T + 2 * P]
        lower = plan[:, T + 2 * P:T + 3 * P]
        head = plan[:, T + 3 * P:T + 3 * P + 1]
        block_start = plan[:, T + 3 * P + 1:]
        ones = s.sb("ones", [P, 1])
        names = ["shifted", "prob", "is1", "rank1", "pick1", "rest", "is2", "rank2", "pick2", "kept", "at1", "at2"]
        t = {x: s.sb(x, [T, NB, E]) for x in names}
        picks = s.sb("picks", [T, E, NB])
        small = {x: s.sb(x, [T, NB]) for x in ("mx", "sum", "inv", "top1", "best1", "top2", "best2", "both", "den", "iden", "slot1", "slot2")}
        count = s.sb("count", [P, 1])
        col = s.sb("col", [P, 5])
        offset = s.sb("offset", [P, T])
        begun = s.sb("begun", [P, BLOCKS])
        loaded, scored, chain, exped, rows_made, rows_read = (s.chain(x) for x in ("loaded", "scored", "chain", "exped", "rows_made", "rows_read"))
        counted = s.chain("counted")
        hrow = routes.hrow
        block = s.block()

        @block.sync
        def _(sp):
            sp.dma_start(rw[:], w_router.rearrange("(c p) e -> p c e", p=P)).then_inc(loaded.sem, 16)
            sp.dma_start(plan[:], const["plan"]).then_inc(loaded.sem, 16)
            sp.wait_ge(loaded.sem, 32)

        @block.tensor
        def _(pe):
            pe.wait_ge(loaded.sem, 32)
            for b in range(NB):
                for c in range(C):
                    mm = nc.tensor.matmul(psum[0:T, 0, b * E:(b + 1) * E], hT[:, c, b * T:(b + 1) * T], rw[:, c, :], start=c == 0, stop=c == C - 1)
            mm.then_inc(scored.sem, 1)
            for b in range(NB):
                if b % 2 == 0 and b >= 8:
                    pe.wait_ge(rows_read.sem, b // 2 - 3)
                for c in range(C):
                    mm = nc.tensor.transpose(psum[0:T, 4 + b // 2 % 4, (b % 2) * D + c * P:(b % 2) * D + (c + 1) * P], hT[:, c, b * T:(b + 1) * T], const["ident"][:])
                mm.then_inc(rows_made.sem, 1)
            flat_picks = picks[:].rearrange("p e b -> p (e b)")
            pe.wait_ge(chain.sem, PICKED)
            nc.tensor.matmul(psum[0:T, 1, 0:P], before, flat_picks, start=True, stop=False)
            nc.tensor.matmul(psum[:, 2, 0:1], flat_picks, ones[0:T, :], start=True, stop=True).then_inc(counted.sem, 1)
            pe.wait_ge(chain.sem, COUNTED)
            nc.tensor.matmul(psum[:, 2, 1:2], same, count[:], start=True, stop=True).then_inc(counted.sem, 1)
            pe.wait_ge(chain.sem, BLOCKED)
            nc.tensor.matmul(psum[:, 3, 0:1], lower, col[:, 2:3], start=True, stop=True)
            nc.tensor.matmul(psum[:, 3, 1:2], earlier, count[:], start=True, stop=True).then_inc(counted.sem, 1)
            pe.wait_ge(chain.sem, OFFSET)
            nc.tensor.matmul(psum[0:T, 1, 0:P], offset[:], const["ident"][:], start=False, stop=True).then_inc(counted.sem, 1)
            pe.wait_ge(chain.sem, BEGUN)
            nc.tensor.matmul(psum[0:1, 0, 0:BLOCKS], ones[:], begun[:], start=True, stop=True).then_inc(counted.sem, 1)

        @block.scalar
        def _(act):
            act.wait_ge(chain.sem, 2)
            nc.scalar.activation(t["prob"][:], t["shifted"][:], ACT.Exp).then_inc(exped.sem, 1)
            for b in range(0, NB, 2):
                act.wait_ge(rows_made.sem, b + 2)
                nc.scalar.copy(hrow[:, b:b + 2].rearrange("p b d -> p (b d)"), psum[0:T, 4 + b // 2 % 4, 0:2 * D]).then_inc(rows_read.sem, 1)

        @block.vector
        def _(dve):
            def link(ins):
                dve.wait_ge(chain.sem, chain.inc(ins))

            def wide(x):
                return small[x][:].unsqueeze(2).broadcast_to([T, NB, E])

            tt, ts, red = nc.vector.tensor_tensor, nc.vector.tensor_scalar, nc.vector.tensor_reduce
            rank = const["rank"][0:T].unsqueeze(1).broadcast_to([T, NB, E])
            nc.vector.memset(ones[:], 1.0)
            dve.wait_ge(scored.sem, 1)
            logits = psum[0:T, 0, 0:NB * E].rearrange("p (b e) -> p b e", e=E)
            link(red(small["mx"][:], logits, X, ALU.max))
            link(tt(t["shifted"][:], logits, wide("mx"), ALU.subtract))
            dve.wait_ge(exped.sem, 1)
            link(red(small["sum"][:], t["prob"][:], X, ALU.add))
            link(nc.vector.reciprocal(small["inv"][:], small["sum"][:]))
            link(tt(t["kept"][:], t["prob"][:], wide("inv"), ALU.mult))
            link(red(small["top1"][:], t["kept"][:], X, ALU.max))
            link(tt(t["is1"][:], t["kept"][:], wide("top1"), ALU.is_equal))
            link(tt(t["rank1"][:], t["is1"][:], rank, ALU.mult))
            link(red(small["best1"][:], t["rank1"][:], X, ALU.max))
            link(tt(t["pick1"][:], t["rank1"][:], wide("best1"), ALU.is_equal))
            link(nc.vector.scalar_tensor_tensor(t["rest"][:], t["pick1"][:], -4.0, t["kept"][:], ALU.mult, ALU.add))
            link(red(small["top2"][:], t["rest"][:], X, ALU.max))
            link(tt(t["is2"][:], t["rest"][:], wide("top2"), ALU.is_equal))
            link(tt(t["rank2"][:], t["is2"][:], rank, ALU.mult))
            link(red(small["best2"][:], t["rank2"][:], X, ALU.max))
            link(tt(t["pick2"][:], t["rank2"][:], wide("best2"), ALU.is_equal))
            link(tt(picks[:].rearrange("p e b -> p b e"), t["pick1"][:], t["pick2"][:], ALU.add))
            assert chain.n == PICKED
            link(tt(small["both"][:], small["top1"][:], small["top2"][:], ALU.add))
            link(ts(small["den"][:], small["both"][:], 1e-9, None, ALU.max))
            link(nc.vector.reciprocal(small["iden"][:], small["den"][:]))
            for k, top in enumerate(("top1", "top2")):
                link(tt(routes.weight[k][:], small[top][:], small["iden"][:], ALU.mult))
            dve.wait_ge(counted.sem, 1)
            link(nc.vector.tensor_copy(count[:], psum[:, 2, 0:1]))
            assert chain.n == COUNTED
            dve.wait_ge(counted.sem, 2)
            link(ts(col[:, 0:1], psum[:, 2, 1:2], 1.0 / BLOCK, (BLOCK - 1.0) / BLOCK - 0.498, ALU.mult, ALU.add))
            link(ts(col[:, 1:2], col[:, 0:1], ROUND, None, ALU.add))
            link(ts(col[:, 2:3], col[:, 1:2], ROUND, BLOCK * 1.0, ALU.subtract, ALU.mult))
            assert chain.n == BLOCKED
            dve.wait_ge(counted.sem, 3)
            link(nc.vector.tensor_copy(col[:, 3:5], psum[:, 3, 0:2]))
            link(ts(offset[:], col[:, 3:4].broadcast_to([P, T]), col[:, 4:5], None, ALU.add))
            assert chain.n == OFFSET
            link(ts(begun[:], block_start, col[:, 3:4], head, ALU.is_ge, ALU.mult))
            assert chain.n == BEGUN
            dve.wait_ge(counted.sem, 4)
            at = psum[0:T, 1, 0:P].rearrange("p (e b) -> p b e", e=E)
            for k in (1, 2):
                link(tt(t[f"at{k}"][:], t[f"pick{k}"][:], at, ALU.mult))
                link(red(small[f"slot{k}"][:], t[f"at{k}"][:], X, ALU.add))
                link(nc.vector.tensor_copy(routes.slot[k - 1][:], small[f"slot{k}"][:]))
            dve.wait_ge(counted.sem, 5)
            link(ts(routes.expert[:], psum[0:1, 0, 0:BLOCKS], 1.0, None, ALU.subtract))
            assert chain.n == LINKS


PICKED = 17
COUNTED = PICKED + 6
BLOCKED = COUNTED + 3
OFFSET = BLOCKED + 2
BEGUN = OFFSET + 1
LINKS = BEGUN + 7


def experts(nc, psum, const, routes, w_up, w_down):
    with Scope(nc, "experts") as s:
        up = s.sb("up", [P, 2, C, DFF])
        down = s.sb("down", [P, 2, M8, D])
        rows = s.sb("rows", [P, 2, HALVES, D])
        xb = s.sb("xb", [P, 2, C, BLOCK])
        relu = s.sb("relu", [P, 2, BLOCK])
        hidden = s.sb("hidden", [P, 2, M8, BLOCK])
        result = s.sb("result", [P, 2, HALVES, D])
        loaded = s.loads("weights_loaded", 2)
        rows_loaded = s.loads("rows_loaded", 1)
        stored = s.loads("result_stored", 1)
        turned = s.counter("turned", 1)
        xb_ready = s.counter("xb_ready", 1)
        up_ready = s.counter("up_ready", M8)
        relu_done = s.counter("relu_done", M8)
        hidden_ready = s.counter("hidden_ready", M8)
        down_done = s.counter("down_done", HALVES)
        result_ready = s.counter("result_ready", 1)
        block = s.block()
        PAIRS = BLOCKS // 2
        assert BLOCKS % 2

        def block_steps(eng, step):
            with eng.Fori(0, PAIRS) as i:
                step(At(0, [(i, 2)]), False)
                step(At(1, [(i, 2)]), False)
            step(At(BLOCKS - 1), True)

        @block.sync
        def _(sp):
            def load(n):
                u = n.parity
                e = nc.values_load(routes.expert[0:1, bass.ds(n.times(1), 1)], engines=(mybir.EngineType.SP,), min_val=0, max_val=E - 1,
                                   skip_runtime_bounds_check_because="it counts, less one, the experts that begin at or before the block, and the first always does")
                sp.dma_start(rows[:, u], routes.slots_x[bass.ds(n.times(BLOCK), BLOCK), :].rearrange("(a p) d -> p a d", p=P)).then_inc(rows_loaded.sem(n), 16)
                sp.dma_start(up[:, u], w_up[bass.ds(e, 1)].rearrange("o (c p) n -> p (o c) n", p=P)).then_inc(loaded.sem(n), 16)
                sp.dma_start(down[:, u], w_down[bass.ds(e, 1)].rearrange("o (k p) n -> p (o k) n", p=P)).then_inc(loaded.sem(n), 16)

            def store(n):
                sp.wait_ge(*result_ready.after(n))
                dst = routes.slots_y[bass.ds(n.times(BLOCK), BLOCK), :].rearrange("(a p) d -> p a d", p=P)
                sp.dma_start(dst, result[:, n.parity]).then_inc(stored.sem(n), 16)

            sp.wait_ge(routes.scattered.sem, routes.scattered.n)
            load(At(0))
            load(At(1))
            with sp.Fori(0, PAIRS - 1) as i:
                for u in range(2):
                    store(At(u, [(i, 2)]))
                    load(At(u + 2, [(i, 2)]))
            store(At(BLOCKS - 3))
            load(At(BLOCKS - 1))
            store(At(BLOCKS - 2))
            store(At(BLOCKS - 1))
            sp.wait_ge(*stored.after(At(BLOCKS - 2)))
            sp.wait_ge(*stored.after(At(BLOCKS - 1)))

        @block.tensor
        def _(pe):
            for x in (turned, up_ready, down_done):
                x.start(pe)

            def turn(n):
                u = n.parity
                pe.wait_ge(*rows_loaded.after(n))
                pe.wait_ge(*xb_ready.after(n - 1))
                for c in range(C):
                    for a in range(HALVES):
                        mm = nc.tensor.transpose(psum[:, 4, c * BLOCK + a * P:c * BLOCK + (a + 1) * P], rows[:, u, a, c * P:(c + 1) * P], const["ident"][:])
                mm.then_inc(turned.sem, 1)

            def step(n, last):
                u = n.parity
                pe.wait_ge(*loaded.after(n))
                pe.wait_ge(*xb_ready.after(n))
                for m in range(M8):
                    pe.wait_ge(*relu_done.after(n if m >= 4 else n - 1, (m - 4) % M8))
                    for c in range(C):
                        mm = nc.tensor.matmul(psum[:, m % 4, 0:BLOCK], up[:, u, c, m * P:(m + 1) * P], xb[:, u, c, :], start=c == 0, stop=c == C - 1)
                    mm.then_inc(up_ready.sem, 1)
                if not last:
                    turn(n + 1)
                pe.wait_ge(*result_ready.after(n - 2))
                for a in range(HALVES):
                    for k in range(M8):
                        if a == 0:
                            pe.wait_ge(*hidden_ready.after(n, k))
                        mm = nc.tensor.matmul(psum[:, 6 + u, a * D:(a + 1) * D], hidden[:, u, k, a * P:(a + 1) * P], down[:, u, k, :], start=k == 0, stop=k == M8 - 1)
                    mm.then_inc(down_done.sem, 1)

            turn(At(0))
            block_steps(pe, step)

        @block.scalar
        def _(act):
            relu_done.start(act)
            xb_ready.start(act)
            nc.scalar.preload_act_table(ACT.Relu)

            def take(n):
                act.wait_ge(*turned.after(n))
                act.wait_ge(*up_ready.after(n - 2, M8 - 1))
                nc.scalar.copy(xb[:, n.parity], psum[:, 4, :].rearrange("p (c t) -> p c t", c=C)).then_inc(xb_ready.sem, 1)

            def step(n, last):
                for m in range(M8):
                    act.wait_ge(*up_ready.after(n, m))
                    act.wait_ge(*hidden_ready.after(n if m >= 2 else n - 1, (m - 2) % M8))
                    nc.scalar.activation(relu[:, m % 2], psum[:, m % 4, 0:BLOCK], ACT.Relu).then_inc(relu_done.sem, 1)
                if not last:
                    take(n + 1)

            take(At(0))
            block_steps(act, step)

        @block.vector
        def _(dve):
            hidden_ready.start(dve)
            result_ready.start(dve)

            def step(n, last):
                u = n.parity
                for m in range(M8):
                    dve.wait_ge(*relu_done.after(n, m))
                    dve.wait_ge(*down_done.after(n - 2, HALVES - 1))
                    nc.vector.tensor_tensor(hidden[:, u, m], relu[:, m % 2], relu[:, m % 2], ALU.mult).then_inc(hidden_ready.sem, 1)
                dve.wait_ge(*down_done.after(n, HALVES - 1))
                dve.wait_ge(*stored.after_one_before(n))
                nc.vector.tensor_copy(result[:, u].rearrange("p a d -> p (a d)"), psum[:, 6 + u, 0:HALVES * D]).then_inc(result_ready.sem, 1)

            block_steps(dve, step)


def combine_experts(nc, psum, const, routes, accT):
    got = routes.result
    with Scope(nc, "combine") as s:
        scaled, joined, turned, added = (s.chain(x) for x in ("scaled", "joined", "turned", "added"))
        block = s.block()

        @block.vector
        def _(dve):
            def join(b):
                if b % FETCH == 0:
                    dve.wait_ge(routes.fetched[b // FETCH].sem, routes.fetched[b // FETCH].n)
                nc.vector.tensor_scalar(got[0][:, b], got[0][:, b], routes.weight[0][:, b:b + 1], None, ALU.mult).then_inc(scaled.sem, 1)
                dve.wait_ge(scaled.sem, b + 1)
                nc.vector.scalar_tensor_tensor(got[0][:, b], got[1][:, b], routes.weight[1][:, b:b + 1], got[0][:, b], ALU.mult, ALU.add).then_inc(joined.sem, 1)

            def add(b):
                dve.wait_ge(turned.sem, b + 1)
                x = accT[:, :, b * T:(b + 1) * T]
                nc.vector.tensor_tensor(x, x, psum[:, b % 4, 0:C * T].rearrange("p (c t) -> p c t", c=C), ALU.add).then_inc(added.sem, 1)

            for b in range(NB + 1):
                if b < NB:
                    join(b)
                if b:
                    add(b - 1)

        @block.tensor
        def _(pe):
            for b in range(NB):
                pe.wait_ge(joined.sem, b + 1)
                if b >= 4:
                    pe.wait_ge(added.sem, b - 3)
                for c in range(C):
                    mm = nc.tensor.transpose(psum[:, b % 4, c * T:(c + 1) * T], got[0][:, b, c * P:(c + 1) * P], const["ident"][0:T, 0:T])
                mm.then_inc(turned.sem, 1)




def quantised(nc, psum, const, w, hT, accT):
    NT_, FULL, REST = 6, 4, 96
    tiles = [(m, P if m < FULL else REST) for m in range(NT_)]
    first = [m * P if m < FULL else FULL * P + (m - FULL) * REST for m in range(NT_)]
    assert first[-1] + REST == INTER
    with Scope(nc, "quant") as s:
        wg = s.sb("wg", [P, NT_, D])
        wu = s.sb("wu", [P, NT_, D])
        wd = s.sb("wd", [P, C, INTER])
        clips = s.sb("clips", [P, 2])
        clip_sig = s.sb("clip_sig", [P, 2])
        wmax = s.sb("wmax", [P, 2 * NT_ + C])
        wscale = s.sb("wscale", [P, 2 * NT_ + C])
        winv = s.sb("winv", [P, 2 * NT_ + C])
        big = s.sb("big", [P, 3, NT_ * D])
        qb = s.sb("qb", [P, 3, NT_ * D], BF16)
        wgT = s.sb("wgT", [P, C, INTER], BF16)
        wuT = s.sb("wuT", [P, C, INTER], BF16)
        wdT = s.sb("wdT", [P, NT_, D], BF16)
        xq = s.sb("xq", [P, C, TOK], BF16)
        hq = s.sb("hq", [P, NT_, G], BF16)
        h = s.sb("h", [P, NT_, TOK])
        gates = s.sb("gates", [P, 2, G])
        sc = s.sb("scales", [P, 16])
        both = s.sb("both", [P, 2 * NT_])
        outs = s.sb("outs", [P, C])
        hmax = s.sb("hmax", [P, GROUPS * NT_])
        ld = s.chain("ld")

        with nc.Block() as block:

            @block.sync
            def _(sp):
                for dst, src in ((wg, w["gate"]), (wu, w["up"])):
                    ld.inc(sp.dma_start(dst[:, 0:FULL], src[0:FULL * P].rearrange("(m p) n -> p m n", p=P)), 16)
                    ld.inc(sp.dma_start(dst[0:REST, FULL:NT_], src[FULL * P:INTER].rearrange("(m p) n -> p m n", p=REST)), 16)
                ld.inc(sp.dma_start(wd[:], w["down"].rearrange("(c p) n -> p c n", p=P)), 16)
                ld.inc(sp.dma_start(clips[:, 0:1], w["clip_x"].unsqueeze(0).broadcast_to([P, 1])), 16)
                ld.inc(sp.dma_start(clips[:, 1:2], w["clip_down"].unsqueeze(0).broadcast_to([P, 1])), 16)
                sp.wait_ge(ld.sem, ld.n)

            @block.vector
            def _(dve):
                for x in (wmax, hmax):
                    nc.vector.memset(x[:], 1.0)
                nc.vector.memset(sc[:], 0.0)

        parts = [(wg, 0), (wu, 1), (wd, 2)]

        def pieces():
            for a, k in parts[:2]:
                for m, rows in tiles:
                    yield rows, a[0:rows, m], k * NT_ + m, (k, m * D, D)
            for c in range(C):
                yield P, wd[:, c], 2 * NT_ + c, (2, c * INTER, INTER)

        vx, ax, gx, tx = (s.chain(x) for x in ("vx", "ax", "gx", "tx"))
        n_pieces = len(list(pieces()))
        with nc.Block() as block:

            @block.vector
            def _(dve):
                def link(ins):
                    dve.wait_ge(vx.sem, vx.inc(ins))

                nc.vector.memset(hmax[:], 0.0)
                link(nc.vector.tensor_reduce(sc[:, 0:1], hT[:].rearrange("p c t -> p (c t)"), X, ALU.max, apply_absolute_value=True))
                for rows, a, col, _ in pieces():
                    last = nc.vector.tensor_reduce(wmax[0:rows, col:col + 1], a, X, ALU.max, apply_absolute_value=True)
                link(last)
                link(nc.vector.tensor_scalar(wscale[:], wmax[:], 1.0 / QMAX, None, ALU.mult))
                link(nc.vector.reciprocal(winv[:], wscale[:]))
                for k, (rows, a, col, (p, o, width)) in enumerate(pieces()):
                    dve.wait_ge(ax.sem, 2 + k)
                    b = big[0:rows, p, o:o + width]
                    link(nc.vector.tensor_scalar(b, b, ROUND + QMAX, ROUND - QMAX - 1, ALU.min, ALU.max))
                    link(nc.vector.tensor_scalar(qb[0:rows, p, o:o + width], b, ROUND, None, ALU.subtract))

            @block.gpsimd
            def _(pool):
                pool.wait_ge(vx.sem, 1)
                nc.gpsimd.partition_all_reduce(sc[:, 1:2], sc[:, 0:1], P, bass.bass_isa.ReduceOp.max).then_inc(gx.sem, 1)

            @block.scalar
            def _(act):
                nc.scalar.activation(clip_sig[:], clips[:], ACT.Sigmoid).then_inc(ax.sem, 1)
                act.wait_ge(vx.sem, 4)
                for rows, a, col, (p, o, width) in pieces():
                    nc.scalar.activation(big[0:rows, p, o:o + width], a, ACT.Identity, bias=const["round"][0:rows, 0:1], scale=winv[0:rows, col:col + 1]).then_inc(ax.sem, 1)

        turns = [(0, m, c, rows) for m, rows in tiles for c in range(C)] + [(1, m, c, rows) for m, rows in tiles for c in range(C)]
        turns += [(2, m, c, rows) for m, rows in tiles for c in range(C)]
        tp, tr, rx = (s.chain(x) for x in ("tp", "tr", "rx"))
        xf = s.sb("xf", [P, C, TOK])
        with nc.Block() as block:

            @block.tensor
            def _(pe):
                for k, (p, m, c, rows) in enumerate(turns):
                    if k >= 8:
                        pe.wait_ge(tr.sem, k - 7)
                    dst = psum[:, k % 8, :].bitcast(BF16)
                    if p < 2:
                        mm = nc.tensor.transpose(dst[:, 0:rows], qb[0:rows, p, m * D + c * P:m * D + (c + 1) * P], const["identb"][0:rows, 0:rows])
                    else:
                        mm = nc.tensor.transpose(dst[0:rows, 0:P], qb[:, 2, c * INTER + first[m]:c * INTER + first[m] + rows], const["identb"][:])
                    mm.then_inc(tp.sem, 1)

            @block.scalar
            def _(act):
                for k, (p, m, c, rows) in enumerate(turns):
                    act.wait_ge(tp.sem, k + 1)
                    src = psum[:, k % 8, :].bitcast(BF16)
                    if p < 2:
                        nc.scalar.copy((wgT, wuT)[p][:, c, first[m]:first[m] + rows], src[:, 0:rows]).then_inc(tr.sem, 1)
                    else:
                        nc.scalar.copy(wdT[0:rows, m, c * P:(c + 1) * P], src[0:rows, 0:P]).then_inc(tr.sem, 1)

            @block.vector
            def _(dve):
                def link(ins):
                    dve.wait_ge(rx.sem, rx.inc(ins))

                link(nc.vector.scalar_tensor_tensor(sc[:, 2:3], sc[:, 1:2], 1.0 / QMAX, clip_sig[:, 0:1], ALU.mult, ALU.mult))
                link(nc.vector.reciprocal(sc[:, 3:4], sc[:, 2:3]))
                link(nc.vector.tensor_scalar(both[:], wscale[:, 0:2 * NT_], sc[:, 2:3], None, ALU.mult))
                flat = xf[:].rearrange("p c t -> p (c t)")
                link(nc.vector.tensor_scalar(flat, hT[:].rearrange("p c t -> p (c t)"), sc[:, 3:4], ROUND, ALU.mult, ALU.add))
                link(nc.vector.tensor_scalar(flat, flat, ROUND + QMAX, ROUND - QMAX - 1, ALU.min, ALU.max))
                link(nc.vector.tensor_scalar(xq[:].rearrange("p c t -> p (c t)"), flat, ROUND, None, ALU.subtract))

        up_made = s.counter("up_made", 2 * NT_)
        gated = s.counter("gated", NT_)
        joined = s.counter("joined", NT_)
        measured = s.counter("measured", NT_)
        with nc.Block() as block:

            @block.tensor
            def _(pe):
                up_made.start(pe)
                with pe.Fori(0, GROUPS) as g:
                    n, t = At(0, [(g, 1)]), bass.ds(g * G, G)
                    for m, rows in tiles:
                        b = m % 3
                        for k, wT in enumerate((wgT, wuT)):
                            pe.wait_ge(*(gated, joined)[k].after(n if m >= 3 else n - 1, (m - 3) % NT_))
                            for c in range(C):
                                mm = nc.tensor.matmul(psum[0:rows, 2 * b + k, 0:G], wT[:, c, first[m]:first[m] + rows], xq[:, c, t], start=c == 0, stop=c == C - 1)
                            mm.then_inc(up_made.sem, 1)

            @block.scalar
            def _(act):
                gated.start(act)
                nc.scalar.preload_act_table(ACT.Silu)
                with act.Fori(0, GROUPS) as g:
                    n = At(0, [(g, 1)])
                    for m, rows in tiles:
                        act.wait_ge(*up_made.after(n, 2 * m))
                        act.wait_ge(*joined.after(n if m >= 2 else n - 1, (m - 2) % NT_))
                        nc.scalar.activation(gates[0:rows, m % 2], psum[0:rows, 2 * (m % 3), 0:G], ACT.Silu, scale=both[0:rows, m:m + 1]).then_inc(gated.sem, 1)

            @block.vector
            def _(dve):
                joined.start(dve)
                measured.start(dve)
                with dve.Fori(0, GROUPS) as g:
                    n, t = At(0, [(g, 1)]), bass.ds(g * G, G)
                    for m, rows in tiles:
                        dve.wait_ge(*gated.after(n, m))
                        dve.wait_ge(*up_made.after(n, 2 * m + 1))
                        nc.vector.scalar_tensor_tensor(h[0:rows, m, t], psum[0:rows, 2 * (m % 3) + 1, 0:G], both[0:rows, NT_ + m:NT_ + m + 1], gates[0:rows, m % 2], ALU.mult, ALU.mult).then_inc(joined.sem, 1)
                    for m, rows in tiles:
                        dve.wait_ge(*joined.after(n, m))
                        nc.vector.tensor_reduce(hmax[0:rows, bass.ds(g * NT_ + m, 1)], h[0:rows, m, t], X, ALU.max, apply_absolute_value=True).then_inc(measured.sem, 1)

        hx, hg = s.chain("hx"), s.chain("hg")
        with nc.Block() as block:

            @block.vector
            def _(dve):
                def link(ins):
                    dve.wait_ge(hx.sem, hx.inc(ins))

                link(nc.vector.tensor_reduce(sc[:, 4:5], hmax[:], X, ALU.max))
                dve.wait_ge(hg.sem, 1)
                link(nc.vector.scalar_tensor_tensor(sc[:, 6:7], sc[:, 5:6], 1.0 / QMAX, clip_sig[:, 1:2], ALU.mult, ALU.mult))
                link(nc.vector.reciprocal(sc[:, 7:8], sc[:, 6:7]))
                link(nc.vector.tensor_scalar(outs[:], wscale[:, 2 * NT_:2 * NT_ + C], sc[:, 6:7], None, ALU.mult))

            @block.gpsimd
            def _(pool):
                pool.wait_ge(hx.sem, 1)
                nc.gpsimd.partition_all_reduce(sc[:, 5:6], sc[:, 4:5], P, bass.bass_isa.ReduceOp.max).then_inc(hg.sem, 1)

        scaled = s.counter("h_scaled", NT_)
        clipped = s.counter("h_clipped", NT_)
        rounded = s.counter("h_rounded", NT_)
        down_used = s.counter("down_used", NT_)
        added = s.counter("added", 1)
        block = s.block()

        @block.scalar
        def _(act):
            scaled.start(act)
            with act.Fori(0, GROUPS) as g:
                n, t = At(0, [(g, 1)]), bass.ds(g * G, G)
                for m, rows in tiles:
                    nc.scalar.activation(h[0:rows, m, t], h[0:rows, m, t], ACT.Identity, bias=const["round"][0:rows, 0:1], scale=sc[0:rows, 7:8]).then_inc(scaled.sem, 1)

        @block.vector
        def _(dve):
            clipped.start(dve)
            rounded.start(dve)
            added.start(dve)
            with dve.Fori(0, GROUPS) as g:
                n, t = At(0, [(g, 1)]), bass.ds(g * G, G)
                for m, rows in tiles:
                    dve.wait_ge(*scaled.after(n, m))
                    x = h[0:rows, m, t]
                    nc.vector.tensor_scalar(x, x, ROUND + QMAX, ROUND - QMAX - 1, ALU.min, ALU.max).then_inc(clipped.sem, 1)
                    dve.wait_ge(*clipped.after(n, m))
                    dve.wait_ge(*down_used.after(n - 1, m))
                    nc.vector.tensor_scalar(hq[0:rows, m], x, ROUND, None, ALU.subtract).then_inc(rounded.sem, 1)
                dve.wait_ge(*down_used.after(n, NT_ - 1))
                for c in range(C):
                    a = nc.vector.scalar_tensor_tensor(accT[:, c, t], psum[:, c, 0:G], outs[:, c:c + 1], accT[:, c, t], ALU.mult, ALU.add)
                a.then_inc(added.sem, 1)

        @block.tensor
        def _(pe):
            down_used.start(pe)
            with pe.Fori(0, GROUPS) as g:
                n = At(0, [(g, 1)])
                pe.wait_ge(*added.after(n - 1))
                for m, rows in tiles:
                    pe.wait_ge(*rounded.after(n, m))
                    for c in range(C):
                        mm = nc.tensor.matmul(psum[:, c, 0:G], wdT[0:rows, m, c * P:(c + 1) * P], hq[0:rows, m], start=m == 0, stop=m == NT_ - 1)
                    mm.then_inc(down_used.sem, 1)




def decoder(nc, a, out, stages=6):
    with ExitStack() as stack:
        def sb(name, shape, dt=F32):
            return stack.enter_context(nc.sbuf_tensor(name, shape, dt))

        psum = stack.enter_context(nc.psum_tensor("psum", [P, 8, 512], F32))
        xT = sb("xT", [P, C, TOK])
        hT = sb("hT", [P, C, TOK])
        averager = sb("averager", [P, P])
        eps = sb("eps", [P, 1])
        rnd = sb("rnd", [P, 1])
        ident = sb("ident", [P, P])
        identb = sb("identb", [P, P], BF16)
        spreader = sb("spreader", [P, P])
        maskf = sb("maskf", [T, T])
        maskb = sb("maskb", [T, HG * T], BF16)
        rank = sb("rank", [P, E])
        rowf = sb("rowf", [1, P])
        maskrow = sb("maskrow", [1, P], BF16)
        ln1 = sb("ln1", [P, 2, C])
        ln2 = sb("ln2", [P, 2, C])
        flags = sb("flags", [1, NB * S2 // 4], mybir.dt.uint32)
        masked = sb("masked", [1, NB * S2], BF16)
        const = {"ident": ident, "spreader": spreader, "identb": identb, "maskb": maskb, "maskrow": maskrow, "masked": masked, "round": rnd, "rank": rank, "plan": a["plan"]}
        loaded = Chain(nc.alloc_semaphore("constants_loaded"))
        zeroed = Chain(nc.alloc_semaphore("slots_zeroed"))
        zeros = sb("zeros", [P, D])

        def dram(name, shape):
            return nc.dram_tensor(name, shape, F32).ap()

        slots_x, slots_y = dram("slots_x", (SLOTS, D)), dram("slots_y", (SLOTS, D))

        with nc.Block() as block:

            @block.sync
            def _(sp):
                for dst, src in ((xT[:], a["xT"].rearrange("(c p) t -> p c t", p=P)), (ident[:], a["ident"]), (spreader[:], a["spreader"]), (maskf[:], a["causal"]),
                                 (rank[:], a["rank"]), (rowf[:], a["maskrow"]), (ln1[:], a["ln1"]), (ln2[:], a["ln2"]),
                                 (flags[:], a["mask"])):
                    loaded.inc(sp.dma_start(dst, src), 16)
                sp.wait_ge(loaded.sem, loaded.n)

            @block.vector
            def _(dve):
                nc.vector.memset(averager[:], 1.0 / D)
                nc.vector.memset(eps[:], EPS)
                nc.vector.memset(rnd[:], ROUND)
                nc.vector.memset(zeros[:], 0.0)

        with nc.Block() as block:

            @block.sync
            def _(sp):
                zeroed.inc(sp.dma_start(slots_x.rearrange("(n p) d -> p n d", p=P), zeros[:].unsqueeze(1).broadcast_to([P, SLOTS // P, D])), 16)

            @block.vector
            def _(dve):
                nc.vector.tensor_copy(identb[:], ident[:])
                nc.vector.tensor_copy(maskb[:].rearrange("p (g s) -> p g s", g=HG), maskf[:].unsqueeze(1).broadcast_to([T, HG, T]))
                nc.vector.tensor_copy(maskrow[:], rowf[:])
                nc.vector.tensor_scalar(masked[:], flags[:].bitcast(U8), NEG, None, ALU.mult)

        ns = NormSignals(nc)

        def fm(x, n):
            return a[x].rearrange("(c p) n -> p c n", p=P), (P, C, n)

        def flat(x, *shape):
            return a[x], shape

        def wide(x):
            return a[x].rearrange("(g p) n -> p g n", p=P), (P, NG, D)

        def row(x):
            return a[x].unsqueeze(0).broadcast_to([P, D]), (P, D)

        with nc.sbuf_tensor("yT", [P, C, TOK], F32) as yT:
            layer_norm(nc, "n0", ns, psum, averager, xT, yT, eps)
            layer_norm(nc, "n1", ns, psum, averager, yT, hT, eps, ln1)
            attention(nc, "a0", "future", psum, const,
                      {"wq": fm("a0_wq", PADW), "wk": fm("a0_wk", PADW), "wv": fm("a0_wv", D), "wf": fm("a0_wf", D),
                       "wqm": fm("a0_wqm", D), "wkm": fm("a0_wkm", D), "conv": flat("a0_conv", P, FUT, P), "wo": wide("a0_wo")}, hT, yT)
            add_into(nc, "s0", xT, yT)
            layer_norm(nc, "n2", ns, psum, averager, yT, hT, eps, ln2)
        perceptron(nc, "f0", psum, hT, xT, a["a0_ff1"], a["a0_ff2"], ACT.Gelu)
        if stages > 1:
            layer_norm(nc, "n3", ns, psum, averager, xT, hT, eps)
            attention(nc, "x0", "memory", psum, const,
                      {"wq": fm("x0_wq", PADW), "wk": fm("x0_wk", PADW), "wv": fm("x0_wv", D), "wo": wide("x0_wo"),
                       "bq": flat("x0_bq", P, NG), "bk": flat("x0_bk", P, NG), "bv": row("x0_bv"), "bo": flat("x0_bo", P, C),
                       "m_k": flat("x0_mk", P, NG, MEM), "m_v": flat("x0_mv", MEM, H, HD)}, hT, xT, a["ctxT"])
        if stages > 2:
            layer_norm(nc, "n4", ns, psum, averager, xT, hT, eps)
            with ExitStack() as held:
                routes = Routes(nc, lambda name, shape, dt=F32: held.enter_context(nc.sbuf_tensor(name, shape, dt)), slots_x, slots_y)
                router(nc, psum, const, a["router_w"], hT, routes)

                def shared(stage, groups, beside):
                    perceptron(nc, stage, psum, hT, xT, a["shared_up"], a["shared_down"], ACT.Relu, groups, beside)

                shared("s1", range(GROUPS // 2), lambda pool: scatter_tokens(nc, pool, routes, zeroed))
                experts(nc, psum, const, routes, a["moe_up"], a["moe_down"])
                shared("s2", range(GROUPS // 2, GROUPS), lambda pool: gather_results(nc, pool, routes))
                combine_experts(nc, psum, const, routes, xT)
        if stages > 3:
            layer_norm(nc, "n5", ns, psum, averager, xT, hT, eps)
            with nc.sbuf_tensor("qT_all", [P, NG, TOK], F32) as qT_all, nc.sbuf_tensor("gateT", [P, NG, TOK], F32) as gateT:
                skew = dram("offset_rows", (NB * H * T * T,))
                offset_factors(nc, psum, {"wq": fm("a1_wq", PADW), "bq": flat("a1_bq", P, NG), "gate_w": fm("a1_gate_w", PADW),
                                          "gate_b": flat("a1_gate_b", P, NG), "gain": flat("a1_gain", P, NG), "rel": flat("a1_rel", P, T)},
                               hT, qT_all, gateT, skew)
                attention(nc, "a1", "offset", psum, const,
                          {"wk": fm("a1_wk", PADW), "wv": fm("a1_wv", D), "wo": wide("a1_wo"), "bk": flat("a1_bk", P, NG),
                           "bv": row("a1_bv"), "bo": flat("a1_bo", P, C)}, hT, xT, qT_all=qT_all, gateT=gateT,
                          skewed={"dram": skew, "bias": a["a1_bias"]})
        if stages > 4:
            layer_norm(nc, "n6", ns, psum, averager, xT, hT, eps)
            attention(nc, "x1", "causal", psum, const,
                      {"wq": fm("x1_wq", PADW), "wk": fm("x1_wk", PADW), "wv": fm("x1_wv", D), "wo": wide("x1_wo"),
                       "bq": flat("x1_bq", P, NG), "bk": flat("x1_bk", P, NG), "bv": row("x1_bv"), "bo": flat("x1_bo", P, C)}, hT, xT, a["ctxT"])
        if stages > 5:
            layer_norm(nc, "n7", ns, psum, averager, xT, hT, eps)
            quantised(nc, psum, const, {"gate": a["q_gate"], "up": a["q_up"], "down": a["q_down"], "clip_x": a["q_clip_x"], "clip_down": a["q_clip_down"]}, hT, xT)

        with nc.Block() as block:

            @block.sync
            def _(sp):
                done = Chain(nc.alloc_semaphore("stored"))
                done.inc(sp.dma_start(out.rearrange("(c p) t -> p c t", p=P), xT[:]), 16)
                sp.wait_ge(done.sem, done.n)




def padded_heads(w):
    w = np.asarray(w)
    out = np.zeros(w.shape[:-1] + (H, 32), np.float32)
    out[..., :HD] = w.reshape(w.shape[:-1] + (H, HD))
    return out.reshape(w.shape[:-1] + (PADW,))


def padded_rows(w):
    return np.ascontiguousarray(padded_heads(np.asarray(w).T).T)


def head_rows(b, spare=0.0):
    p = padded_heads(b).reshape(H, 32).copy()
    p[:, HD] = spare
    return np.ascontiguousarray(p.reshape(NG, P).T)


def laid_out(i):
    t = lambda x: np.ascontiguousarray(np.asarray(x).T)
    col = lambda x: np.ascontiguousarray(np.asarray(x).reshape(C, P).T)
    f = {}
    f["xT"] = np.ascontiguousarray(i["x"].reshape(TOK, D).T)
    f["ctxT"] = np.ascontiguousarray(i["ctx_1024"].transpose(0, 2, 1))
    f["mask"] = np.ascontiguousarray(i["mask_Bx1x1xS2_bk0"].reshape(1, NB * S2)).view(np.uint32)
    f["ident"] = np.eye(P, dtype=np.float32)
    f["causal"] = np.where(np.arange(T)[None, :] <= np.arange(T)[:, None], 0.0, NEG).astype(np.float32)
    f["rank"] = np.ascontiguousarray(np.broadcast_to(np.arange(E, 0, -1, dtype=np.float32), (P, E)))
    e, b = np.arange(P) // NB, np.arange(P) % NB
    tokens = np.zeros((P, T))
    tokens[:T] = np.arange(T)[:, None] < np.arange(T)
    f["plan"] = np.concatenate([tokens, (e[:, None] == e) & (b[:, None] < b), e[:, None] == e,
                                np.broadcast_to(((e[:, None] < e) & (b[:, None] == 0)), (P, P)), (b == 0)[:, None],
                                np.broadcast_to(BLOCK * np.arange(BLOCKS), (P, BLOCKS))], 1).astype(np.float32)
    f["spreader"] = ((np.arange(P)[:, None] // 32 == np.arange(P) // 32) & (np.arange(P)[:, None] % 32 == HD)).astype(np.float32)
    f["maskrow"] = (np.arange(P) % 32 == HD).astype(np.float32)[None]
    for k in (1, 2):
        f[f"ln{k}"] = np.ascontiguousarray(np.stack([col(i[f"L0_attn_ln{k}_g"]), col(i[f"L0_attn_ln{k}_b"])], 1))
    wq, wk, wv, wf = (t(x) for x in np.split(i["L0_attn_W_qkvf"], 4))
    f["a0_wq"], f["a0_wk"], f["a0_wv"], f["a0_wf"], f["a0_wqm"], f["a0_wkm"] = padded_heads(wq), padded_heads(wk), wv, wf, wq, wk
    conv = np.zeros((P // HD, HD, FUT, P // HD, HD), np.float32)
    for h in range(P // HD):
        conv[h, :, :, h, :] = i["L0_attn_W_conv"].transpose(0, 2, 1)
    f["a0_conv"] = conv.reshape(P, FUT, P)
    f["a0_wo"] = padded_rows(t(i["L0_attn_W_proj"]))
    f["a0_ff1"], f["a0_ff2"] = i["L0_attn_W_ff1"], i["L0_attn_W_ff2"]
    for n, l in (("x0", "L0_xattn"), ("x1", "L1_xattn")):
        tt = t if n == "x0" else np.ascontiguousarray
        f[n + "_wq"], f[n + "_wk"] = padded_heads(tt(i[l + "_Wq"])), padded_heads(tt(i[l + "_Wk"]))
        f[n + "_wv"], f[n + "_wo"] = tt(i[l + "_Wv"]), padded_rows(tt(i[l + "_Wo"]))
        f[n + "_bq"] = head_rows(i[l + "_bq"], 1.0 if n == "x0" else 0.0)
        f[n + "_bk"], f[n + "_bv"], f[n + "_bo"] = head_rows(i[l + "_bk"]), i[l + "_bv"], col(i[l + "_bo"])
    f["x0_mk"] = np.ascontiguousarray(padded_heads(i["L0_xattn_m_k"][0]).reshape(MEM, NG, P).transpose(2, 1, 0))
    f["x0_mv"] = np.ascontiguousarray(i["L0_xattn_m_v"][0].reshape(MEM, H, HD))
    f["router_w"] = t(i["L0_ffn_router_w"])
    f["moe_up"], f["moe_down"] = (np.ascontiguousarray(i[x].transpose(0, 2, 1)) for x in ("L0_ffn_w_fc", "L0_ffn_w_proj"))
    f["shared_up"], f["shared_down"] = t(i["L0_ffn_shared_fc"]), t(i["L0_ffn_shared_proj"])
    wq, wk, wv = (t(x) for x in np.split(i["L1_attn_qkv_w"], 3))
    bq, bk, bv = np.split(i["L1_attn_qkv_b"], 3)
    f["a1_wq"], f["a1_wk"], f["a1_wv"], f["a1_wo"] = padded_heads(wq), padded_heads(wk), wv, padded_rows(t(i["L1_attn_out_w"]))
    f["a1_bq"], f["a1_bk"], f["a1_bv"], f["a1_bo"] = head_rows(bq), head_rows(bk), np.ascontiguousarray(bv), col(i["L1_attn_out_b"])
    f["a1_gate_w"], f["a1_gate_b"] = padded_heads(t(i["L1_attn_gate_w"])), head_rows(i["L1_attn_gate_b"])
    f["a1_gain"] = head_rows(np.repeat(i["L1_attn_if_gain"], HD))
    rel = np.zeros((HG, 32, T), np.float32)
    bias = np.full((T, H, T), NEG, np.float32)
    for k, o in enumerate(OFFSETS):
        if o < T:
            rel[:, :HD, T - 1 - o] = i["L1_attn_scale_embed"][k]
            for q in range(o, T):
                bias[q, :, q - o] = i["L1_attn_pos_bias"][k]
    f["a1_rel"], f["a1_bias"] = rel.reshape(P, T), bias
    f["q_gate"], f["q_up"], f["q_down"] = i["L1_ffn_w_gate"], i["L1_ffn_w_up"], i["L1_ffn_w_down"]
    f["q_clip_x"], f["q_clip_down"] = i["L1_ffn_clip_x"], i["L1_ffn_clip_down"]
    return f


def kernel(**inputs):
    import concourse.bacc as bacc
    from concourse.bass_utils import run_bass_kernel_spmd

    fed = {f"in_{k}": np.ascontiguousarray(v) for k, v in laid_out({k: np.asarray(v) for k, v in inputs.items()}).items()}
    nc = bacc.Bacc("TRN2", target_bir_lowering=False, num_devices=1)
    a = {k[3:]: nc.dram_tensor(k, v.shape, mybir.dt.from_np(v.dtype), kind="ExternalInput").ap() for k, v in fed.items()}
    out = nc.dram_tensor("out_xT", (D, TOK), F32, kind="ExternalOutput").ap()
    decoder(nc, a, out)
    r = run_bass_kernel_spmd(nc, [fed], core_ids=[0])
    return np.ascontiguousarray(r.results[0]["out_xT"].T).reshape(NB, T, D)
```

```python
from contextlib import ExitStack

import numpy as np

import concourse.bass as bass
from concourse import mybir

F32 = mybir.dt.float32
BF16 = mybir.dt.bfloat16
U8 = mybir.dt.uint8
U32 = mybir.dt.uint32
ALU = mybir.AluOpType
ACT = mybir.ActivationFunctionType
X = mybir.AxisListType.X

P = 128
NB, T, D = 16, 112, 256
C = D // P
TOK = NB * T
S2, MEM = 375, 64
H, HD = 16, 16
HG = 4
NG = H // HG
PADW = NG * P
FUT = 4
G = 448
GROUPS = TOK // G
DFF, E = 1024, 8
M8 = DFF // P
INTER = 704
KC = 110
NKEY = 4 * KC
NEG = -1e30
EPS = 1e-5
ROUND = 12582912.0
QMAX = 127.0
OFFSETS = [o for o in sorted(set(range(33)) | {48, 64, 96, 128, 192, 256, 384})]


class At:

    def __init__(self, const=0, regs=()):
        self.const, self.regs = const, tuple(regs)

    def __add__(self, k):
        return At(self.const + k, self.regs)

    def __sub__(self, k):
        return self + (-k)

    def times(self, f, plus=0):
        v = self.const * f + plus
        for r, c in self.regs:
            v = r * (c * f) + v
        return v

    @property
    def parity(self):
        return self.const % 2


AHEAD = 4


class Signal:

    def __init__(self, sem, per):
        self.sem, self.per = sem, per

    def start(self, eng):
        eng.sem_inc(self.sem, AHEAD * self.per)

    def after(self, step, k=0):
        return self.sem, step.times(self.per, AHEAD * self.per + k + 1)


class Loads:

    def __init__(self, sems, per):
        self.sems, self.per = sems, per

    def sem(self, step):
        return self.sems[step.const % len(self.sems)]

    def after(self, step):
        ways = len(self.sems)
        turn = At(step.const // ways, [(r, c // ways) for r, c in step.regs])
        return self.sem(step), turn.times(16 * self.per, 16 * self.per)

    def after_one_before(self, step):
        turn = At(0, [(r, c // len(self.sems)) for r, c in step.regs])
        return self.sem(step), turn.times(16 * self.per)


class Chain:

    def __init__(self, sem):
        self.sem, self.n = sem, 0

    def inc(self, ins, by=1):
        ins.then_inc(self.sem, by)
        self.n += by
        return self.n


def tok(step, width=T):
    return bass.ds(step.times(width), width)


def batch_steps(eng, step):
    step(At(0), mid=False, end=False)
    step(At(1), end=False)
    with eng.Fori(0, (NB - 2) // 2) as i:
        step(At(2, [(i, 2)]))
        step(At(3, [(i, 2)]))
    step(At(NB), now=False)
    step(At(NB + 1), now=False, mid=False)


class Scope:

    def __init__(self, nc, stage, reuse=False):
        self.nc, self.stage, self.reuse, self.stack, self.sems = nc, stage, reuse, ExitStack(), []

    def __enter__(self):
        self.stack.__enter__()
        return self

    def __exit__(self, *e):
        self.stack.__exit__(*e)
        if self.reuse:
            with self.nc.Block() as block:

                @block.gpsimd
                def _(pool):
                    for sem in self.sems:
                        pool.sem_clear(sem)

            for sem in self.sems:
                self.nc.release_semaphore(sem)

    def semaphore(self, name):
        self.sems.append(self.nc.alloc_semaphore(f"{self.stage}_{name}"))
        return self.sems[-1]

    def sb(self, name, shape, dt=F32):
        return self.stack.enter_context(self.nc.sbuf_tensor(f"{self.stage}_{name}", shape, dt))

    def counter(self, name, per):
        return Signal(self.semaphore(name), per)

    def loads(self, name, per, ways=2):
        return Loads([self.semaphore(f"{name}_{w}") for w in range(ways)], per)

    def chain(self, name):
        return Chain(self.semaphore(name))

    def block(self):
        return self.stack.enter_context(self.nc.Block())




class NormSignals:

    def __init__(self, nc):
        self.summed, self.mean, self.centered, self.squared, self.paired, self.var, self.logvar, self.rstd, self.normed = (
            nc.alloc_semaphore(f"norm_{name}")
            for name in ("summed", "mean", "centered", "squared", "paired", "var", "logvar", "rstd", "normed"))
        self.groups = 0


def layer_norm(nc, stage, ns, psum, averager, src, dst, eps, gb=None):
    done = [ns.groups + g + 1 for g in range(GROUPS)]
    ns.groups += GROUPS
    tokens = [slice(g * G, (g + 1) * G) for g in range(GROUPS)]
    with Scope(nc, stage) as s:
        sq = s.sb("sq", [P, GROUPS, C, G])
        rs = s.sb("rs", [P, GROUPS, G])
        block = s.block()

        def mean(g):
            return psum[:, g, 0:G]

        def var(g):
            return psum[:, 4 + g, 0:G]

        @block.gpsimd
        def _(pool):
            for g, t in enumerate(tokens):
                nc.gpsimd.tensor_tensor(sq[:, g, 0], src[:, 0, t], src[:, 1, t], ALU.add).then_inc(ns.summed, 1)

        @block.tensor
        def _(pe):
            for g in range(GROUPS):
                pe.wait_ge(ns.summed, done[g])
                nc.tensor.matmul(mean(g), averager[:], sq[:, g, 0], start=True, stop=True).then_inc(ns.mean, 1)
            for g in range(GROUPS):
                pe.wait_ge(ns.paired, done[g])
                nc.tensor.matmul(var(g), averager[:], sq[:, g, 0], start=True, stop=True).then_inc(ns.var, 1)

        @block.scalar
        def _(act):
            nc.scalar.preload_act_table_set("natural_log_exp_and_others")
            for g, t in enumerate(tokens):
                act.wait_ge(ns.centered, done[g])
                nc.scalar.activation(sq[:, g], dst[:, :, t], ACT.Square).then_inc(ns.squared, 1)
            for g in range(GROUPS):
                act.wait_ge(ns.var, done[g])
                nc.scalar.activation(rs[:, g], var(g), ACT.Ln, bias=eps[:, 0:1]).then_inc(ns.logvar, 1)
                act.wait_ge(ns.logvar, done[g])
                nc.scalar.activation(rs[:, g], rs[:, g], ACT.Exp, scale=-0.5).then_inc(ns.rstd, 1)
            if gb is not None:
                for g, t in enumerate(tokens):
                    act.wait_ge(ns.normed, done[g])
                    for c in range(C):
                        nc.scalar.activation(dst[:, c, t], dst[:, c, t], ACT.Identity, bias=gb[:, 1, c:c + 1], scale=gb[:, 0, c:c + 1])

        @block.vector
        def _(dve):
            for g, t in enumerate(tokens):
                dve.wait_ge(ns.mean, done[g])
                nc.vector.tensor_tensor(dst[:, :, t], src[:, :, t], mean(g).unsqueeze(1).broadcast_to([P, C, G]), ALU.subtract).then_inc(ns.centered, 1)
            for g in range(GROUPS):
                dve.wait_ge(ns.squared, done[g])
                nc.vector.tensor_tensor(sq[:, g, 0], sq[:, g, 0], sq[:, g, 1], ALU.add).then_inc(ns.paired, 1)
            for g, t in enumerate(tokens):
                dve.wait_ge(ns.rstd, done[g])
                dve.wait_ge(ns.centered, done[g])
                nc.vector.tensor_tensor(dst[:, :, t], dst[:, :, t], rs[:, g].unsqueeze(1).broadcast_to([P, C, G]), ALU.mult).then_inc(ns.normed, 1)




def perceptron(nc, stage, psum, hT, accT, w_up, w_down, func, groups=range(GROUPS), beside=None, while_loading=None):
    gelu = func == ACT.Gelu
    with Scope(nc, stage) as s:
        up = s.sb("up", [P, C, DFF])
        down = s.sb("down", [P, M8, D])
        hidden = s.sb("hidden", [P, M8, G])
        relu = None if gelu else s.sb("relu", [P, 2, G])
        up_loaded, down_loaded = s.chain("up_loaded"), s.chain("down_loaded")
        up_ready = s.counter("up_ready", M8)
        act_done = s.counter("act_done", M8)
        hidden_ready = act_done if gelu else s.counter("hidden_ready", M8)
        hidden_read = s.counter("hidden_read", M8)
        added = s.counter("added", 1)

        with nc.Block() as block:

            @block.sync
            def _(sp):
                sp.dma_start(up[:], w_up.rearrange("(c p) n -> p c n", p=P)).then_inc(up_loaded.sem, 16)
                sp.dma_start(down[:], w_down.rearrange("(k p) n -> p k n", p=P)).then_inc(down_loaded.sem, 16)

        if while_loading:
            while_loading()
        block = s.block()

        def group_steps(eng, step):
            with eng.Fori(0, len(groups)) as g:
                step(At(0, [(g, 1)]), bass.ds(g * G + groups[0] * G, G))

        if beside:

            @block.gpsimd
            def _(pool):
                beside(pool)

        @block.tensor
        def _(pe):
            up_ready.start(pe)
            hidden_read.start(pe)

            def step(n, t):
                pe.wait_ge(up_loaded.sem, 16)
                for m in range(M8):
                    pe.wait_ge(*act_done.after(n if m >= 4 else n - 1, (m - 4) % M8))
                    for c in range(C):
                        mm = nc.tensor.matmul(psum[:, m % 4, 0:G], up[:, c, m * P:(m + 1) * P], hT[:, c, t], start=c == 0, stop=c == C - 1)
                    mm.then_inc(up_ready.sem, 1)
                pe.wait_ge(down_loaded.sem, 16)
                pe.wait_ge(*added.after(n - 1))
                for k in range(M8):
                    pe.wait_ge(*hidden_ready.after(n, k))
                    for m in range(C):
                        mm = nc.tensor.matmul(psum[:, 4 + m, 0:G], down[:, k, m * P:(m + 1) * P], hidden[:, k], start=k == 0, stop=k == M8 - 1)
                    mm.then_inc(hidden_read.sem, 1)

            group_steps(pe, step)

        @block.scalar
        def _(act):
            act_done.start(act)
            nc.scalar.preload_act_table(func)

            def step(n, t):
                for m in range(M8):
                    act.wait_ge(*up_ready.after(n, m))
                    if gelu:
                        act.wait_ge(*hidden_read.after(n - 1, m))
                        dst = hidden[:, m]
                    else:
                        act.wait_ge(*hidden_ready.after(n if m >= 2 else n - 1, (m - 2) % M8))
                        dst = relu[:, m % 2]
                    nc.scalar.activation(dst, psum[:, m % 4, 0:G], func).then_inc(act_done.sem, 1)

            group_steps(act, step)

        @block.vector
        def _(dve):
            if not gelu:
                hidden_ready.start(dve)
            added.start(dve)

            def step(n, t):
                if not gelu:
                    for m in range(M8):
                        dve.wait_ge(*act_done.after(n, m))
                        dve.wait_ge(*hidden_read.after(n - 1, m))
                        nc.vector.tensor_tensor(hidden[:, m], relu[:, m % 2], relu[:, m % 2], ALU.mult).then_inc(hidden_ready.sem, 1)
                dve.wait_ge(*hidden_read.after(n, M8 - 1))
                nc.vector.tensor_tensor(accT[:, :, t], accT[:, :, t], psum[:, 4:4 + C, 0:G], ALU.add).then_inc(added.sem, 1)

            group_steps(dve, step)


def add_into(nc, stage, dst, src):
    with Scope(nc, stage) as s:
        block = s.block()

        @block.vector
        def _(dve):
            nc.vector.tensor_tensor(dst[:], dst[:], src[:], ALU.add)




class Units:

    def __init__(self, s, units):
        self.all = units
        self.bank = {name: b for name, b, _ in units}
        self.reader = {name: eng for name, _, eng in units}
        self.made = s.counter("product_made", len(units))
        self.order = {name: k for k, (name, _, _) in enumerate(units)}
        self.read = {}
        for eng in ("act", "dve"):
            named = [name for name, _, e in units if e == eng]
            read = s.counter(f"product_read_by_{eng}", len(named)) if named else None
            self.read.update((name, (read, k)) for k, name in enumerate(named))

    def start_reads(self, eng, which):
        for sig in {sig for name, (sig, _) in self.read.items() if self.reader[name] == which}:
            sig.start(eng)

    def after_made(self, name, n):
        return self.made.after(n, self.order[name])

    def after_read(self, name, n):
        sig, k = self.read[name]
        return sig.after(n, k)

    def bank_before(self, name):
        before = [u for u, b, _ in self.all[:self.order[name]] if b == self.bank[name]]
        return before[-1] if before else None

    def last_in(self, bank):
        return ([None] + [u for u, b, _ in self.all if b == bank])[-1]


UNITS = {
    "future": [("q", 4, "act"), ("f", 5, "act"), ("k", 6, "act"), ("qm", 4, "act"), ("up0", 5, "act"),
               ("up1", 6, "act"), ("v", 4, "act"), ("kf0", 5, "dve"), ("kf1", 6, "dve"),
               ("vf0", 4, "act"), ("vf1", 5, "act")],
    "memory": [("q", 4, "dve"), ("k0", 5, "act"), ("k1", 6, "act"), ("k2", 4, "act"), ("k3", 5, "act"),
               ("v0", 6, "dve"), ("v1", 4, "dve"), ("v2", 5, "dve"), ("v3", 6, "dve")],
    "offset": [("k", 4, "act"), ("v", 5, "dve")],
    "causal": [("q", 4, "dve"), ("k", 5, "dve"), ("v", 6, "dve")],
}


def attention(nc, stage, kind, psum, const, w, hT, accT, ctxT=None, qT_all=None, gateT=None, skewed=None, while_loading=None):
    memory, future, offset = kind == "memory", kind == "future", kind == "offset"
    NS = 8 if memory else NG
    NT = H if memory else NG
    KEYS = NKEY if memory else T
    KR = KC if memory else T
    CHUNKS = NKEY // KC if memory else 1
    NCTX = S2 if memory else T
    OUT_SLOT = NS - 1 if not memory else 4
    scale = 1.0 if future or offset else HD ** -0.5
    ident, identb, maskb = const["ident"], const["identb"], const["maskb"]

    with Scope(nc, stage, reuse=True) as s:
        hb = s.sb("hb", [P, 2, C, T])
        ctx = s.sb("ctx", [P, 2, C, NCTX]) if ctxT is not None else None
        qT = s.sb("qT", [P, 2, NG, T])
        kT = s.sb("kT", [P, 2, NG, NCTX + MEM if memory else T])
        v = s.sb("v", [P, 2, CHUNKS, H, 32])
        rowmax = s.sb("rowmax", [T, 2, H])
        negmax = s.sb("negmax", [T, 2, H]) if memory else None
        probs = s.sb("probs", [T, 2, H, KEYS])
        turned = s.sb("turned", [P, 4, 4, T])
        mixT = s.sb("mixT", [P, 2, NG * T])
        rden = s.sb("rden", [P, 2, NG * T])
        gmixT = s.sb("gmixT", [P, 2, NG * T]) if offset else mixT
        names = [x for x in w if x not in ("m_k", "m_v")]
        wt = {x: s.sb(x, list(w[x][1])) for x in names}
        if future:
            fT = s.sb("fT", [P, 2, C, T])
            qm = s.sb("qm", [T, 2, D])
            upT = s.sb("upT", [P, 2, C, FUT, T])
            vf = s.sb("vf", [T, 2, FUT, D])
            qk = s.sb("qk", [T, FUT, D])
            fscore = s.sb("fscore", [T, 2, FUT, H])
            fmax = s.sb("fmax", [T, 2, H])
            fprob = s.sb("fprob", [T, 2, FUT, H])
            weighted = s.sb("weighted", [T, FUT, D])
            fmix = s.sb("fmix", [T, 2, H, 32])
        if offset:
            factor = s.sb("factor", [T, 2, H, T])
            bias = s.sb("bias", [T, H, T])
        if memory:
            mk = s.sb("mk", [P, NG, MEM])
            mv = s.sb("mv", [MEM, H, HD])
            mvs = s.sb("mvs", [MEM, H, 32])

        units = Units(s, UNITS[kind])
        n_in = 1 + (ctxT is not None) + offset
        inputs = s.loads("inputs_loaded", n_in)
        factors = s.loads("factors_loaded", 1)
        scored = s.counter("scored", NS)
        maxed = s.counter("maxed", NS)
        shifted = s.counter("shifted", NS)
        probs_ready = s.counter("probs_ready", NS)
        tile_turned = s.counter("tile_turned", NT)
        turned_act = s.counter("turned_copied_by_act", NT if offset else NT // 2)
        turned_dve = None if offset else s.counter("turned_copied_by_dve", NT // 2)
        mixed_in = s.counter("mixed_in", NT)
        dve_step = s.counter("dve_step", 6) if future else s.counter("scaled", NS) if offset else None
        biased = s.counter("biased", NS) if offset else None
        mix_copied = s.counter("mix_copied", 1)
        spread = s.counter("denominators_spread", 1)
        logged = s.counter("denominators_logged", 1)
        inverted = s.counter("denominators_inverted", 1)
        normed = s.counter("mix_normed", 1)
        gated = s.counter("mix_gated", 1) if offset else None
        projected = s.counter("projected", 1)
        added = s.counter("added", 1)
        max_with_future = s.counter("max_with_future", NS) if future else None
        fexp = s.counter("future_exps", 1) if future else None
        ready = s.chain("ready")

        with nc.Block() as block:

            @block.sync
            def _(sp):
                for x in names:
                    ready.inc(sp.dma_start(wt[x][:], w[x][0]), 16)
                if offset:
                    ready.inc(sp.dma_start(bias[:], skewed["bias"]), 16)
                if memory:
                    ready.inc(sp.dma_start(mk[:], w["m_k"][0]), 16)
                    ready.inc(sp.dma_start(mv[:], w["m_v"][0]), 16)

            @block.vector
            def _(dve):
                nc.vector.memset(v[:], 1.0)
                if future:
                    nc.vector.memset(fmix[:], 1.0)
                if memory:
                    nc.vector.memset(probs[:, :, :, NKEY - 1:NKEY], 0.0)
                    nc.vector.memset(mvs[:], 1.0)

        while_loading()

        with nc.Block() as block:

            @block.sync
            def _(sp):
                sp.wait_ge(ready.sem, ready.n)

        if memory:
            with nc.Block() as block:

                @block.vector
                def _(dve):
                    for u in range(2):
                        nc.vector.tensor_scalar(kT[:, u, :, S2:S2 + MEM], mk[:], HD ** 0.5, None, ALU.mult)
                    nc.vector.tensor_scalar(mvs[:, :, 0:HD], mv[:], MEM ** 0.5, None, ALU.mult)

            with nc.Block() as block:

                @block.sync
                def _(sp):
                    first = S2 - 3 * KC
                    for u in range(2):
                        ready.inc(sp.dma_start(v[first:first + MEM, u, 3], mvs[:]), 16)
                    sp.wait_ge(ready.sem, ready.n)

        def slot_heads(j):
            return [2 * j, 2 * j + 1] if memory else [HG * c + j for c in range(NG)]

        def heads_view(ap, j):
            return ap[:, 2 * j:2 * j + 2] if memory else ap.rearrange("p (c j) -> p j c", j=HG)[:, j]

        def turn_tiles(i):
            if memory:
                return [(i, c) for c in range(4)]
            return [(HG * c + i, 0) for c in range(NG)]

        def copied(i):
            return (turned_act, i) if offset else ((turned_act, turned_dve)[i % 2], i // 2)

        def last_slot(i):
            return i // 2 if memory else i

        block = s.block()

        @block.sync
        def _(sp):
            with sp.Fori(0, NB // 2) as i:
                for u in range(2):
                    n = At(u, [(i, 2)])
                    sp.wait_ge(*units.after_made(units.all[-1][0], n - 2))
                    sp.dma_start(hb[:, u], hT[:, :, tok(n)]).then_inc(inputs.sem(n), 16)
                    if ctxT is not None:
                        src = ctxT[bass.ds(n.times(1), 1)].rearrange("o (c p) s -> p (o c) s", p=P)[:, :, 0:NCTX]
                        sp.dma_start(ctx[:, u], src).then_inc(inputs.sem(n), 16)
                    if offset:
                        start = sp.snap(n.times(H * T * T, T - 1))
                        sp.wait_ge(*dve_step.after(n - 2, NS - 1))
                        src = bass.AP(skewed["dram"].tensor, start, [[T - 1, T], [T * T, H], [1, T]])
                        sp.dma_start(factor[:, u], src).then_inc(factors.sem(n), 16)
                        sp.dma_start(qT[:, u], qT_all[:, :, tok(n)]).then_inc(inputs.sem(n), 16)

        @block.tensor
        def _(pe):
            for x in (units.made, scored, tile_turned, mixed_in, spread, projected):
                x.start(pe)
            src_kv = ctx if ctxT is not None else hb

            def product(parts):
                for out, terms in parts:
                    for k, (a, b) in enumerate(terms):
                        mm = nc.tensor.matmul(out, a, b, start=k == 0, stop=k == len(terms) - 1)
                mm.then_inc(units.made.sem, 1)

            def front(n):
                u = n.parity
                pe.wait_ge(*inputs.after(n))
                for name, b, _ in units.all:
                    before = units.bank_before(name)
                    if before:
                        pe.wait_ge(*units.after_read(before, n))
                    else:
                        pe.wait_ge(*units.after_read(units.last_in(b), n - 1))
                        if b == 6:
                            pe.wait_ge(*added.after(n - 3))
                        else:
                            sig, k = copied(NT - 6 + b)
                            pe.wait_ge(*sig.after(n - 2, k))
                    out = psum[:, b]
                    if name in ("q", "k") and not (name == "k" and memory):
                        src = hb if name == "q" else src_kv
                        product([(out[:, g * T:(g + 1) * T],
                                           [(wt["w" + name][:, c, g * P:(g + 1) * P], src[:, u, c, 0:T]) for c in range(C)])
                                          for g in range(NG)])
                    elif memory and name[0] == "k":
                        g = int(name[1])
                        product([(out[:, 0:S2], [(wt["wk"][:, c, g * P:(g + 1) * P], ctx[:, u, c, :]) for c in range(C)]
                                           + [(const["maskrow"][0:1, :], const["masked"][0:1, bass.ds(n.times(S2), S2)])])])
                    elif memory and name[0] == "v":
                        k0 = int(name[1]) * KC
                        rows = min(KC, S2 - k0)
                        product([(out[0:rows, 0:D], [(ctx[:, u, c, k0:k0 + rows], wt["wv"][:, c, :]) for c in range(C)])])
                    elif name == "v":
                        product([(out[0:T, 0:D], [(src_kv[:, u, c, 0:T], wt["wv"][:, c, :]) for c in range(C)])])
                    elif name == "f":
                        product([(out[:, m * T:(m + 1) * T],
                                           [(wt["wf"][:, c, m * P:(m + 1) * P], hb[:, u, c, :]) for c in range(C)]) for m in range(C)])
                    elif name == "qm":
                        product([(out[0:T, 0:D], [(hb[:, u, c, :], wt["wqm"][:, c, :]) for c in range(C)])])
                    elif name[:2] == "up":
                        m = int(name[2])
                        if m == 0:
                            pe.wait_ge(*units.after_read("f", n))
                        product([(out[:, f * T:(f + 1) * T], [(wt["conv"][:, f, :], fT[:, u, m, :])]) for f in range(FUT)])
                    else:
                        if name == "kf0":
                            pe.wait_ge(*units.after_read("up1", n))
                        half = int(name[2])
                        wx = wt["wkm" if name[0] == "k" else "wv"]
                        product([(out[0:T, f * D:(f + 1) * D],
                                           [(upT[:, u, c, 2 * half + f, :], wx[:, c, :]) for c in range(C)]) for f in range(2)])

            def scores(n, j):
                u = n.parity
                if j == 0:
                    for name in ("q", "k", "k3"):
                        if name in units.reader:
                            pe.wait_ge(*units.after_read(name, n))
                if memory:
                    pe.wait_ge(*probs_ready.after(n if j >= 2 else n - 1, (j - 2) % NS))
                    for b, h in enumerate(slot_heads(j)):
                        r = 32 * (h % HG)
                        mm = nc.tensor.matmul(psum[0:T, 2 * (j % 2) + b, 0:S2 + MEM], qT[r:r + 32, u, h // HG, :], kT[r:r + 32, u, h // HG, :], start=True, stop=True)
                else:
                    pe.wait_ge(*(dve_step if offset else shifted).after(n - 1, j))
                    if not offset:
                        nc.tensor.matmul(psum[0:T, j, 0:G], identb[0:T, 0:T], maskb[:], start=True, stop=False, skip_group_check=True)
                    for c, h in enumerate(slot_heads(j)):
                        r = 32 * j
                        mm = nc.tensor.matmul(psum[0:T, j, c * T:(c + 1) * T], qT[r:r + 32, u, c, :], kT[r:r + 32, u, c, :],
                                              start=offset, stop=True, skip_group_check=not offset)
                mm.then_inc(scored.sem, 1)

            def turn(n, i, last):
                u = n.parity
                if i < 2 and not last and units.last_in(4 + i):
                    pe.wait_ge(*units.after_read(units.last_in(4 + i), n + 1))
                pe.wait_ge(*probs_ready.after(n, last_slot(i)))
                sig, k = copied((i - 2) % NT)
                pe.wait_ge(*sig.after(n if i >= 2 else n - 1, k))
                for k, (h, c) in enumerate(turn_tiles(i)):
                    col = h if memory else i * NG + k
                    mm = nc.tensor.transpose(psum[0:KR, 4 + i % 2, k * T:(k + 1) * T], probs[:, u, col, c * KR:(c + 1) * KR], ident[0:T, 0:T])
                mm.then_inc(tile_turned.sem, 1)

            def mix(n, i):
                u = n.parity
                if i == 0:
                    for name in ("v", "v3"):
                        if name in units.reader:
                            pe.wait_ge(*units.after_read(name, n))
                    pe.wait_ge(*mix_copied.after(n - 1))
                    if future:
                        pe.wait_ge(*dve_step.after(n, 5))
                        for g in range(NG):
                            nc.tensor.matmul(psum[:, 7, g * T:(g + 1) * T], fmix[:, u, HG * g:HG * (g + 1)].rearrange("p h e -> p (h e)"),
                                             ident[0:T, 0:T], start=g == 0, stop=False, skip_group_check=True)
                sig, k = copied(i)
                pe.wait_ge(*sig.after(n, k))
                for k, (h, c) in enumerate(turn_tiles(i)):
                    g, r = h // HG, 32 * (h % HG)
                    mm = nc.tensor.matmul(psum[r:r + 32, 7, g * T:(g + 1) * T], v[0:KR, u, c, h, :], turned[0:KR, i % 4, k, :],
                                          start=c == 0 and not future, stop=c == CHUNKS - 1, skip_group_check=future)
                mm.then_inc(mixed_in.sem, 1)

            def spread_denominators(n, last):
                if units.last_in(6):
                    pe.wait_ge(*units.after_read(units.last_in(6), At(NB - 1) if last else n + 2))
                pe.wait_ge(*added.after(n - 1))
                pe.wait_ge(*mix_copied.after(n))
                nc.tensor.matmul(psum[:, 6, 0:NG * T], const["spreader"][:], mixT[:, n.parity], start=True, stop=True).then_inc(spread.sem, 1)

            def output(n):
                pe.wait_ge(*normed.after(n))
                pe.wait_ge(*inverted.after(n))
                for m in range(C):
                    for g in range(NG):
                        mm = nc.tensor.matmul(psum[:, 6, m * T:(m + 1) * T], wt["wo"][:, g, m * P:(m + 1) * P], gmixT[:, n.parity, g * T:(g + 1) * T],
                                              start=g == 0, stop=g == NG - 1)
                mm.then_inc(projected.sem, 1)

            def step(n, now=True, mid=True, end=True):
                if now:
                    front(n)
                for j in range(NS):
                    if now:
                        scores(n, j)
                    if end and j == 0:
                        spread_denominators(n - 2, not now)
                    if mid:
                        for i in range(j * NT // NS, (j + 1) * NT // NS):
                            turn(n - 1, i, not now)
                            if i >= 2:
                                mix(n - 1, i - 2)
                    if end and j == OUT_SLOT:
                        output(n - 2)
                if mid:
                    mix(n - 1, NT - 2)
                    mix(n - 1, NT - 1)

            batch_steps(pe, step)

        @block.scalar
        def _(act):
            units.start_reads(act, "act")
            for x in [probs_ready, turned_act, mix_copied, logged, inverted] + ([fexp] if future else []):
                x.start(act)
            nc.scalar.preload_act_table_set("natural_log_exp_and_others")

            def read(name, n, out, in_, **how):
                act.wait_ge(*units.after_made(name, n))
                nc.scalar.activation(out, in_, ACT.Identity if "bias" in how else ACT.Copy, **how).then_inc(units.read[name][0].sem, 1)

            def front(n):
                u = n.parity
                for name, b, eng in units.all:
                    if eng != "act":
                        continue
                    if memory:
                        if name == "k0":
                            act.wait_ge(*scored.after(n - 2, NS - 1))
                        g = int(name[1])
                        read(name, n, kT[:, u, g, 0:S2], psum[:, b, 0:S2], bias=wt["bk"][:, g:g + 1])
                        continue
                    if name == "q":
                        act.wait_ge(*scored.after(n - 2, NS - 1))
                        read(name, n, qT[:, u], psum[:, b, 0:G].rearrange("p (g t) -> p g t", g=NG), scale=HD ** -0.5)
                    elif name == "k" and offset:
                        act.wait_ge(*scored.after(n - 2, NS - 1))
                        act.wait_ge(*units.after_made(name, n))
                        for g in range(NG):
                            copy = nc.scalar.activation(kT[:, u, g, :], psum[:, b, g * T:(g + 1) * T], ACT.Identity, bias=wt["bk"][:, g:g + 1])
                        copy.then_inc(units.read[name][0].sem, 1)
                    elif name == "k":
                        read(name, n, kT[:, u], psum[:, b, 0:G].rearrange("p (g t) -> p g t", g=NG))
                    elif name == "f":
                        act.wait_ge(*units.after_made("vf1", n - 2))
                        read(name, n, fT[:, u], psum[:, b, 0:C * T].rearrange("p (c t) -> p c t", c=C))
                    elif name == "v":
                        act.wait_ge(*mixed_in.after(n - 2, NT - 1))
                        read(name, n, v[0:T, u, 0, :, 0:HD], psum[0:T, b, 0:D].rearrange("p (h d) -> p h d", h=H))
                    elif name == "qm":
                        act.wait_ge(*units.after_read("kf1", n - 2))
                        read(name, n, qm[:, u], psum[0:T, b, 0:D])
                    elif name[:2] == "up":
                        read(name, n, upT[:, u, int(name[2])], psum[:, b, 0:G].rearrange("p (f t) -> p f t", f=FUT))
                    else:
                        if name == "vf0":
                            act.wait_ge(*dve_step.after(n - 2, 4))
                        k = int(name[2])
                        read(name, n, vf[:, u, 2 * k:2 * k + 2], psum[0:T, b, :].rearrange("p (f d) -> p f d", f=2))

            def exps(n, j):
                u = n.parity
                if memory:
                    act.wait_ge(*shifted.after(n, j))
                    act.wait_ge(*tile_turned.after(n - 2, 2 * j + 1))
                    for b, h in enumerate(slot_heads(j)):
                        e = nc.scalar.activation(probs[:, u, h, 0:S2 + MEM], psum[0:T, 2 * (j % 2) + b, 0:S2 + MEM], ACT.Exp, bias=negmax[:, u, h:h + 1], scale=scale)
                else:
                    act.wait_ge(*shifted.after(n, j))
                    x = probs[:, u, j * NG:(j + 1) * NG, :]
                    e = nc.scalar.activation(x, x, ACT.Exp, scale=scale)
                e.then_inc(probs_ready.sem, 1)

            def copy_turned(n, i):
                act.wait_ge(*tile_turned.after(n, i))
                act.wait_ge(*mixed_in.after(n if i >= 4 else n - 1, (i - 4) % NT))
                nc.scalar.copy(turned[0:KR, i % 4], psum[0:KR, 4 + i % 2, 0:G].rearrange("p (k t) -> p k t", k=4)).then_inc(turned_act.sem, 1)

            def invert(n):
                u = n.parity
                act.wait_ge(*spread.after(n))
                act.wait_ge(*normed.after(n - 2))
                nc.scalar.activation(rden[:, u], psum[:, 6, 0:NG * T], ACT.Ln).then_inc(logged.sem, 1)
                act.wait_ge(*logged.after(n))
                nc.scalar.activation(rden[:, u], rden[:, u], ACT.Exp, scale=-1.0).then_inc(inverted.sem, 1)

            def step(n, now=True, mid=True, end=True):
                if now:
                    front(n)
                if mid and offset:
                    for j in range(NS):
                        exps(n - 1, j)
                for j in range(NS):
                    if mid:
                        for i in range(j * NT // NS, (j + 1) * NT // NS):
                            if copied(i)[0] is turned_act:
                                copy_turned(n - 1, i)
                    if now and memory:
                        exps(n, j)
                    if end and j == 0:
                        invert(n - 2)
                if mid:
                    act.wait_ge(*mixed_in.after(n - 1, NT - 1))
                    act.wait_ge(*projected.after(n - 3))
                    nc.scalar.copy(mixT[:, (n - 1).parity], psum[:, 7, 0:NG * T]).then_inc(mix_copied.sem, 1)
                if now and not memory and not offset:
                    for j in range(NS):
                        exps(n, j)
                if now and future:
                    act.wait_ge(*dve_step.after(n, 2))
                    act.wait_ge(*dve_step.after(n - 2, 4))
                    nc.scalar.activation(fprob[:, n.parity], fscore[:, n.parity], ACT.Exp).then_inc(fexp.sem, 1)

            batch_steps(act, step)

        @block.vector
        def _(dve):
            units.start_reads(dve, "dve")
            for x in [maxed, shifted, added] + ([] if offset else [turned_dve]) + ([dve_step, max_with_future] if future else []) + ([dve_step, biased] if offset else []):
                x.start(dve)

            def read(name, n, out, in_, other, op=ALU.add):
                dve.wait_ge(*units.after_made(name, n))
                nc.vector.tensor_tensor(out, in_, other, op).then_inc(units.read[name][0].sem, 1)

            def front(n):
                u = n.parity
                for name, b, eng in units.all:
                    if eng != "dve":
                        continue
                    if name in ("q", "k"):
                        dve.wait_ge(*scored.after(n - 2, NS - 1))
                        dst = qT if name == "q" else kT
                        bb = wt["b" + name][:].unsqueeze(2).broadcast_to([P, NG, T])
                        read(name, n, dst[:, u], psum[:, b, 0:G].rearrange("p (g t) -> p g t", g=NG), bb)
                    elif name[0] == "v":
                        dve.wait_ge(*mixed_in.after(n - 2, NT - 1))
                        c = int(name[1]) if memory else 0
                        rows = min(KC, S2 - c * KC) if memory else T
                        read(name, n, v[0:rows, u, c, :, 0:HD], psum[0:rows, b, 0:D].rearrange("p (h d) -> p h d", h=H),
                             wt["bv"][0:rows, :].rearrange("p (h d) -> p h d", h=H))
                    else:
                        if name == "kf0":
                            dve.wait_ge(*units.after_read("qm", n))
                            dve.wait_ge(*dve_step.after(n - 1, 0))
                        k = int(name[2])
                        read(name, n, qk[:, 2 * k:2 * k + 2], psum[0:T, b, :].rearrange("p (f d) -> p f d", f=2),
                             qm[:, u].unsqueeze(1).broadcast_to([T, 2, D]), ALU.mult)
                if future:
                    dve.wait_ge(*units.after_read("kf1", n))
                    dve.wait_ge(*dve_step.after(n - 2, 2))
                    dve.wait_ge(*fexp.after(n - 2))
                    nc.vector.tensor_reduce(fscore[:, u], qk[:].rearrange("p f (h d) -> p f h d", d=HD), X, ALU.add).then_inc(dve_step.sem, 1)
                    dve.wait_ge(*dve_step.after(n, 0))
                    dve.wait_ge(*max_with_future.after(n - 2, NS - 1))
                    nc.vector.tensor_reduce(fmax[:, u], fscore[:, u].rearrange("p f h -> p h f"), X, ALU.max).then_inc(dve_step.sem, 1)

            def shift(n, j):
                u = n.parity
                dve.wait_ge(*scored.after(n, j))
                mx = heads_view(rowmax[:, u], j)
                if memory:
                    nc.vector.tensor_reduce(mx, psum[0:T, 2 * (j % 2):2 * (j % 2) + 2, 0:S2 + MEM], X, ALU.max).then_inc(maxed.sem, 1)
                    dve.wait_ge(*maxed.after(n, j))
                    dve.wait_ge(*probs_ready.after(n - 2, j))
                    nc.vector.tensor_scalar(heads_view(negmax[:, u], j), mx, -scale, None, ALU.mult).then_inc(shifted.sem, 1)
                    return
                x = probs[:, u, j * NG:(j + 1) * NG, :]
                src = psum[0:T, j, 0:G].rearrange("p (c s) -> p c s", c=NG)
                dve.wait_ge(*tile_turned.after(n - 2, j))
                nc.vector.tensor_reduce(mx, src, X, ALU.max).then_inc(maxed.sem, 1)
                dve.wait_ge(*maxed.after(n, j))
                if future:
                    dve.wait_ge(*dve_step.after(n, 1))
                    nc.vector.tensor_tensor(mx, mx, heads_view(fmax[:, u], j), ALU.max).then_inc(max_with_future.sem, 1)
                    dve.wait_ge(*max_with_future.after(n, j))
                nc.vector.tensor_tensor(x, src, mx.unsqueeze(2).broadcast_to([T, NG, T]), ALU.subtract).then_inc(shifted.sem, 1)

            def shift_offsets(n, slots):
                u = n.parity
                by_slot = lambda x: x.rearrange("p (c j) s -> p j c s", j=HG)
                x = {j: probs[:, u, j * NG:(j + 1) * NG, :] for j in slots}
                mx = {j: heads_view(rowmax[:, u], j) for j in slots}
                dve.wait_ge(*factors.after(n))
                for j in slots:
                    dve.wait_ge(*scored.after(n, j))
                    dve.wait_ge(*tile_turned.after(n - 2, j))
                    src = psum[0:T, j, 0:G].rearrange("p (c s) -> p c s", c=NG)
                    nc.vector.scalar_tensor_tensor(x[j], by_slot(factor[:, u])[:, j], 1.0, src, ALU.add, ALU.mult).then_inc(dve_step.sem, 1)
                for j in slots:
                    dve.wait_ge(*dve_step.after(n, j))
                    nc.vector.scalar_tensor_tensor(x[j], x[j], HD ** -0.5, by_slot(bias[:])[:, j], ALU.mult, ALU.add).then_inc(biased.sem, 1)
                for j in slots:
                    dve.wait_ge(*biased.after(n, j))
                    nc.vector.tensor_reduce(mx[j], x[j], X, ALU.max).then_inc(maxed.sem, 1)
                for j in slots:
                    dve.wait_ge(*maxed.after(n, j))
                    nc.vector.tensor_tensor(x[j], x[j], mx[j].unsqueeze(2).broadcast_to([T, NG, T]), ALU.subtract).then_inc(shifted.sem, 1)

            def copy_turned(n, i):
                dve.wait_ge(*tile_turned.after(n, i))
                dve.wait_ge(*mixed_in.after(n if i >= 4 else n - 1, (i - 4) % NT))
                nc.vector.tensor_copy(turned[0:KR, i % 4], psum[0:KR, 4 + i % 2, 0:G].rearrange("p (k t) -> p k t", k=4)).then_inc(turned_dve.sem, 1)

            def future_centered(n):
                u = n.parity
                dve.wait_ge(*max_with_future.after(n, NS - 1))
                nc.vector.tensor_tensor(fscore[:, u], fscore[:, u], rowmax[:, u].unsqueeze(1).broadcast_to([T, FUT, H]), ALU.subtract).then_inc(dve_step.sem, 1)

            def future_mix(n):
                u = n.parity
                dve.wait_ge(*fexp.after(n))
                dve.wait_ge(*units.after_read("vf1", n))
                dve.wait_ge(*dve_step.after(n - 1, 5))
                dve.wait_ge(*mixed_in.after(n - 2, 0))
                nc.vector.tensor_reduce(fmix[:, u, :, HD:HD + 1].rearrange("p h e -> p (h e)"), fprob[:, u].rearrange("p f h -> p h f"), X, ALU.add).then_inc(dve_step.sem, 1)
                w4 = weighted[:].rearrange("p f (h d) -> p (f h) d", d=HD)
                v4 = vf[:, u].rearrange("p f (h d) -> p (f h) d", d=HD)
                p4 = fprob[:, u].rearrange("p f h -> p (f h)").unsqueeze(2).broadcast_to([T, FUT * H, HD])
                nc.vector.tensor_tensor(w4, v4, p4, ALU.mult).then_inc(dve_step.sem, 1)
                dve.wait_ge(*dve_step.after(n, 4))
                nc.vector.tensor_reduce(fmix[:, u, :, 0:HD], weighted[:].rearrange("p f (h d) -> p h d f", d=HD), X, ALU.add).then_inc(dve_step.sem, 1)

            def add_output(n):
                dve.wait_ge(*projected.after(n))
                out = psum[:, 6, 0:C * T].rearrange("p (c t) -> p c t", c=C)
                if future:
                    nc.vector.tensor_tensor(accT[:, :, tok(n)], accT[:, :, tok(n)], out, ALU.add).then_inc(added.sem, 1)
                    return
                for c in range(C):
                    a = nc.vector.scalar_tensor_tensor(accT[:, c, tok(n)], out[:, c], wt["bo"][:, c:c + 1], accT[:, c, tok(n)], ALU.add, ALU.add)
                a.then_inc(added.sem, 1)

            def step(n, now=True, mid=True, end=True):
                if now:
                    front(n)
                for j in range(NS):
                    if now and not offset:
                        shift(n, j)
                    if now and offset and j % 2:
                        shift_offsets(n, (j - 1, j))
                    if mid:
                        for i in range(j * NT // NS, (j + 1) * NT // NS):
                            if copied(i)[0] is turned_dve:
                                copy_turned(n - 1, i)
                    if end and j == OUT_SLOT:
                        add_output(n - 2)
                if now and future:
                    future_centered(n)
                if now and future:
                    future_mix(n)

            batch_steps(dve, step)

        @block.gpsimd
        def _(pool):
            normed.start(pool)
            if offset:
                gated.start(pool)

            def normalise(n):
                u = n.parity
                if offset:
                    pool.wait_ge(*mix_copied.after(n))
                    pool.wait_ge(*projected.after(n - 2))
                    m, gm = (x[:, u].rearrange("p (g t) -> p g t", g=NG) for x in (mixT, gmixT))
                    nc.gpsimd.tensor_tensor(gm, m, gateT[:, :, tok(n)], ALU.mult).then_inc(gated.sem, 1)
                    pool.wait_ge(*gated.after(n))
                pool.wait_ge(*inverted.after(n))
                nc.gpsimd.tensor_tensor(gmixT[:, u], gmixT[:, u], rden[:, u], ALU.mult).then_inc(normed.sem, 1)

            with pool.Fori(0, NB // 2) as i:
                for u in range(2):
                    normalise(At(u, [(i, 2)]))


def offset_factors(nc, psum, w, hT, qT_all, gateT, skewed, while_loading):
    with Scope(nc, "prep") as s:
        names = ("wq", "bq", "gate_w", "gate_b", "gain", "rel")
        wt = {x: s.sb(x, list(w[x][1])) for x in names}
        loaded = s.chain("weights_loaded")
        with nc.Block() as block:

            @block.sync
            def _(sp):
                for x in names:
                    loaded.inc(sp.dma_start(wt[x][:], w[x][0]), 16)

        while_loading()

        with nc.Block() as block:

            @block.sync
            def _(sp):
                sp.wait_ge(loaded.sem, loaded.n)

        made = s.counter("made", 2 * NG)
        q_read = s.counter("queries_read", NG)
        gate_read = s.counter("gates_read", NG)
        gained = s.counter("gained", NG)
        with nc.Block() as block:

            @block.tensor
            def _(pe):
                made.start(pe)
                with pe.Fori(0, GROUPS) as g:
                    n, t = At(0, [(g, 1)]), bass.ds(g * G, G)
                    for k in range(2 * NG):
                        if k < NG:
                            pe.wait_ge(*q_read.after(n - 1, k))
                            lhs = wt["wq"][:, :, k * P:(k + 1) * P]
                        else:
                            pe.wait_ge(*gate_read.after(n - 1, k - NG))
                            lhs = wt["gate_w"][:, :, (k - NG) * P:(k - NG + 1) * P]
                        for c in range(C):
                            mm = nc.tensor.matmul(psum[:, k, 0:G], lhs[:, c], hT[:, c, t], start=c == 0, stop=c == C - 1)
                        mm.then_inc(made.sem, 1)

            @block.scalar
            def _(act):
                gate_read.start(act)
                nc.scalar.preload_act_table(ACT.Sigmoid)
                with act.Fori(0, GROUPS) as g:
                    n, t = At(0, [(g, 1)]), bass.ds(g * G, G)
                    for k in range(NG):
                        act.wait_ge(*made.after(n, NG + k))
                        nc.scalar.activation(gateT[:, k, t], psum[:, NG + k, 0:G], ACT.Sigmoid, bias=wt["gate_b"][:, k:k + 1]).then_inc(gate_read.sem, 1)

            @block.vector
            def _(dve):
                q_read.start(dve)
                gained.start(dve)
                with dve.Fori(0, GROUPS) as g:
                    n, t = At(0, [(g, 1)]), bass.ds(g * G, G)
                    for k in range(NG):
                        dve.wait_ge(*made.after(n, k))
                        nc.vector.tensor_scalar(qT_all[:, k, t], psum[:, k, 0:G], wt["bq"][:, k:k + 1], None, ALU.add).then_inc(q_read.sem, 1)
                    for k in range(NG):
                        dve.wait_ge(*gate_read.after(n, k))
                        nc.vector.tensor_scalar(gateT[:, k, t], gateT[:, k, t], wt["gain"][:, k:k + 1], None, ALU.mult).then_inc(gained.sem, 1)

        WAYS = 4
        qb = s.sb("qb", [P, WAYS, NG, T])
        rows = s.sb("rows", [T, WAYS, H, T])
        queries = s.loads("queries_loaded", 1, WAYS)
        stored = s.loads("rows_stored", 1, WAYS)
        product = s.counter("product", NG)
        even = s.counter("even_copied", NG // 2)
        odd = s.counter("odd_copied", NG // 2)
        block = s.block()

        def batches(eng):
            with eng.Fori(0, NB // WAYS) as i:
                yield [(At(k, [(i, WAYS)]), k) for k in range(WAYS)]

        def head_rows(k, j):
            return rows[:, k].rearrange("p (c j) s -> p j c s", j=HG)[:, j]

        def bank(k, j):
            return psum[0:T, 4 * (k % 2) + j, 0:G]

        @block.sync
        def _(sp):
            def load(n, k):
                sp.dma_start(qb[:, k], qT_all[:, :, tok(n)]).then_inc(queries.sem(n), 16)

            def store(n, k):
                start = sp.snap(n.times(H * T * T))
                sp.wait_ge(*even.after(n, NG // 2 - 1))
                sp.wait_ge(*odd.after(n, NG // 2 - 1))
                dst = bass.AP(skewed.tensor, start, [[T, T], [T * T, H], [1, T]])
                sp.dma_start(dst, rows[:, k]).then_inc(stored.sem(n), 16)

            for k in range(WAYS):
                load(At(k), k)
            with sp.Fori(0, NB // WAYS - 1) as i:
                for k in range(WAYS):
                    store(At(k, [(i, WAYS)]), k)
                    load(At(k + WAYS, [(i, WAYS)]), k)
            for k in range(WAYS):
                store(At(NB - WAYS + k), k)
            for k in range(WAYS):
                sp.wait_ge(*stored.after(At(NB - WAYS + k)))

        @block.tensor
        def _(pe):
            product.start(pe)
            for some in batches(pe):
                for n, k in some:
                    pe.wait_ge(*queries.after(n))
                    for j in range(NG):
                        pe.wait_ge(*(odd if j % 2 else even).after(n - 2, j // 2))
                        r = slice(32 * j, 32 * j + 32)
                        for c in range(NG):
                            mm = nc.tensor.matmul(bank(k, j)[:, c * T:(c + 1) * T], qb[r, k, c, :], wt["rel"][r, :], start=True, stop=True)
                        mm.then_inc(product.sem, 1)

        @block.scalar
        def _(act):
            even.start(act)
            for some in batches(act):
                for n, k in some:
                    act.wait_ge(*stored.after_one_before(n))
                    for j in (0, 2):
                        act.wait_ge(*product.after(n, j))
                        nc.scalar.copy(head_rows(k, j), bank(k, j).rearrange("p (c s) -> p c s", c=NG)).then_inc(even.sem, 1)

        @block.vector
        def _(dve):
            odd.start(dve)
            for some in batches(dve):
                for n, k in some:
                    dve.wait_ge(*stored.after_one_before(n))
                    for j in (1, 3):
                        dve.wait_ge(*product.after(n, j))
                        nc.vector.tensor_copy(head_rows(k, j), bank(k, j).rearrange("p (c s) -> p c s", c=NG)).then_inc(odd.sem, 1)




BLOCK = 256
HALVES = BLOCK // P
BLOCKS = (2 * TOK - E) // BLOCK + E
SLOTS = BLOCKS * BLOCK


FETCH = 2


class Routes:

    def __init__(self, nc, sb, slots_x, slots_y):
        self.hrow = sb("hrow", [T, NB, D])
        self.result = [self.hrow, sb("second_result", [T, NB, D])]
        self.slot = [sb(f"slot{k}", [T, NB], U32) for k in range(2)]
        self.weight = [sb(f"route_weight{k}", [T, NB]) for k in range(2)]
        self.expert = sb("block_expert", [1, BLOCKS], U32)
        self.slots_x, self.slots_y = slots_x, slots_y
        self.scattered = Chain(nc.alloc_semaphore("tokens_scattered"))
        self.fetched = [Chain(nc.alloc_semaphore(f"results_fetched{k}")) for k in range(NB // FETCH)]


def scatter_tokens(nc, pool, routes, zeroed):
    pool.wait_ge(zeroed.sem, zeroed.n)
    for k in range(2):
        for b in range(NB):
            routes.scattered.inc(nc.gpsimd.indirect_dma_start(
                routes.slots_x, bass.IndirectOffsetOnAxis(ap=routes.slot[k][:, b:b + 1], axis=0), routes.hrow[:, b, :], None), 16)


def gather_results(nc, pool, routes):
    for b in range(NB):
        for k in range(2):
            routes.fetched[b // FETCH].inc(nc.gpsimd.indirect_dma_start(
                routes.result[k][:, b, :], None, routes.slots_y, bass.IndirectOffsetOnAxis(ap=routes.slot[k][:, b:b + 1], axis=0)), 16)


def router(nc, psum, const, w_router, hT, routes, load_last):
    with Scope(nc, "router") as s:
        rw = s.sb("rw", [P, C, E])
        plan = s.sb("plan", [P, T + 3 * P + 1 + BLOCKS])
        before = plan[0:T, 0:T]
        earlier = plan[:, T:T + P]
        same = plan[:, T + P:T + 2 * P]
        lower = plan[:, T + 2 * P:T + 3 * P]
        head = plan[:, T + 3 * P:T + 3 * P + 1]
        block_start = plan[:, T + 3 * P + 1:]
        ones = s.sb("ones", [P, 1])
        names = ["shifted", "prob", "is1", "rank1", "pick1", "rest", "is2", "rank2", "pick2", "kept", "at1", "at2"]
        t = {x: s.sb(x, [T, NB, E]) for x in names}
        picks = s.sb("picks", [T, E, NB])
        small = {x: s.sb(x, [T, NB]) for x in ("mx", "sum", "inv", "top1", "best1", "top2", "best2", "both", "den", "iden", "slot1", "slot2")}
        count = s.sb("count", [P, 1])
        col = s.sb("col", [P, 5])
        offset = s.sb("offset", [P, T])
        begun = s.sb("begun", [P, BLOCKS])
        loaded, scored, chain, exped, rows_made, rows_read = (s.chain(x) for x in ("loaded", "scored", "chain", "exped", "rows_made", "rows_read"))
        counted = s.chain("counted")
        hrow = routes.hrow
        block = s.block()

        @block.sync
        def _(sp):
            sp.dma_start(rw[:], w_router.rearrange("(c p) e -> p c e", p=P)).then_inc(loaded.sem, 16)
            sp.dma_start(plan[:], const["plan"]).then_inc(loaded.sem, 16)
            sp.wait_ge(loaded.sem, 32)
            load_last(sp)

        @block.tensor
        def _(pe):
            pe.wait_ge(loaded.sem, 32)
            for b in range(NB):
                for c in range(C):
                    mm = nc.tensor.matmul(psum[0:T, 0, b * E:(b + 1) * E], hT[:, c, b * T:(b + 1) * T], rw[:, c, :], start=c == 0, stop=c == C - 1)
            mm.then_inc(scored.sem, 1)
            for b in range(NB):
                if b % 2 == 0 and b >= 8:
                    pe.wait_ge(rows_read.sem, b // 2 - 3)
                for c in range(C):
                    mm = nc.tensor.transpose(psum[0:T, 4 + b // 2 % 4, (b % 2) * D + c * P:(b % 2) * D + (c + 1) * P], hT[:, c, b * T:(b + 1) * T], const["ident"][:])
                mm.then_inc(rows_made.sem, 1)
            flat_picks = picks[:].rearrange("p e b -> p (e b)")
            pe.wait_ge(chain.sem, PICKED)
            nc.tensor.matmul(psum[0:T, 1, 0:P], before, flat_picks, start=True, stop=False)
            nc.tensor.matmul(psum[:, 2, 0:1], flat_picks, ones[0:T, :], start=True, stop=True).then_inc(counted.sem, 1)
            pe.wait_ge(chain.sem, COUNTED)
            nc.tensor.matmul(psum[:, 2, 1:2], same, count[:], start=True, stop=True).then_inc(counted.sem, 1)
            pe.wait_ge(chain.sem, BLOCKED)
            nc.tensor.matmul(psum[:, 3, 0:1], lower, col[:, 2:3], start=True, stop=True)
            nc.tensor.matmul(psum[:, 3, 1:2], earlier, count[:], start=True, stop=True).then_inc(counted.sem, 1)
            pe.wait_ge(chain.sem, OFFSET)
            nc.tensor.matmul(psum[0:T, 1, 0:P], offset[:], const["ident"][:], start=False, stop=True).then_inc(counted.sem, 1)
            pe.wait_ge(chain.sem, BEGUN)
            nc.tensor.matmul(psum[0:1, 0, 0:BLOCKS], ones[:], begun[:], start=True, stop=True).then_inc(counted.sem, 1)

        @block.scalar
        def _(act):
            act.wait_ge(chain.sem, 2)
            nc.scalar.activation(t["prob"][:], t["shifted"][:], ACT.Exp).then_inc(exped.sem, 1)
            for b in range(0, NB, 2):
                act.wait_ge(rows_made.sem, b + 2)
                nc.scalar.copy(hrow[:, b:b + 2].rearrange("p b d -> p (b d)"), psum[0:T, 4 + b // 2 % 4, 0:2 * D]).then_inc(rows_read.sem, 1)

        @block.vector
        def _(dve):
            def link(ins):
                dve.wait_ge(chain.sem, chain.inc(ins))

            def wide(x):
                return small[x][:].unsqueeze(2).broadcast_to([T, NB, E])

            tt, ts, red = nc.vector.tensor_tensor, nc.vector.tensor_scalar, nc.vector.tensor_reduce
            rank = const["rank"][0:T].unsqueeze(1).broadcast_to([T, NB, E])
            nc.vector.memset(ones[:], 1.0)
            dve.wait_ge(scored.sem, 1)
            logits = psum[0:T, 0, 0:NB * E].rearrange("p (b e) -> p b e", e=E)
            link(red(small["mx"][:], logits, X, ALU.max))
            link(tt(t["shifted"][:], logits, wide("mx"), ALU.subtract))
            dve.wait_ge(exped.sem, 1)
            link(red(small["sum"][:], t["prob"][:], X, ALU.add))
            link(nc.vector.reciprocal(small["inv"][:], small["sum"][:]))
            link(tt(t["kept"][:], t["prob"][:], wide("inv"), ALU.mult))
            link(red(small["top1"][:], t["kept"][:], X, ALU.max))
            link(tt(t["is1"][:], t["kept"][:], wide("top1"), ALU.is_equal))
            link(tt(t["rank1"][:], t["is1"][:], rank, ALU.mult))
            link(red(small["best1"][:], t["rank1"][:], X, ALU.max))
            link(tt(t["pick1"][:], t["rank1"][:], wide("best1"), ALU.is_equal))
            link(nc.vector.scalar_tensor_tensor(t["rest"][:], t["pick1"][:], -4.0, t["kept"][:], ALU.mult, ALU.add))
            link(red(small["top2"][:], t["rest"][:], X, ALU.max))
            link(tt(t["is2"][:], t["rest"][:], wide("top2"), ALU.is_equal))
            link(tt(t["rank2"][:], t["is2"][:], rank, ALU.mult))
            link(red(small["best2"][:], t["rank2"][:], X, ALU.max))
            link(tt(t["pick2"][:], t["rank2"][:], wide("best2"), ALU.is_equal))
            link(tt(picks[:].rearrange("p e b -> p b e"), t["pick1"][:], t["pick2"][:], ALU.add))
            assert chain.n == PICKED
            link(tt(small["both"][:], small["top1"][:], small["top2"][:], ALU.add))
            link(ts(small["den"][:], small["both"][:], 1e-9, None, ALU.max))
            link(nc.vector.reciprocal(small["iden"][:], small["den"][:]))
            for k, top in enumerate(("top1", "top2")):
                link(tt(routes.weight[k][:], small[top][:], small["iden"][:], ALU.mult))
            dve.wait_ge(counted.sem, 1)
            link(nc.vector.tensor_copy(count[:], psum[:, 2, 0:1]))
            assert chain.n == COUNTED
            dve.wait_ge(counted.sem, 2)
            link(ts(col[:, 0:1], psum[:, 2, 1:2], 1.0 / BLOCK, (BLOCK - 1.0) / BLOCK - 0.498, ALU.mult, ALU.add))
            link(ts(col[:, 1:2], col[:, 0:1], ROUND, None, ALU.add))
            link(ts(col[:, 2:3], col[:, 1:2], ROUND, BLOCK * 1.0, ALU.subtract, ALU.mult))
            assert chain.n == BLOCKED
            dve.wait_ge(counted.sem, 3)
            link(nc.vector.tensor_copy(col[:, 3:5], psum[:, 3, 0:2]))
            link(ts(offset[:], col[:, 3:4].broadcast_to([P, T]), col[:, 4:5], None, ALU.add))
            assert chain.n == OFFSET
            link(ts(begun[:], block_start, col[:, 3:4], head, ALU.is_ge, ALU.mult))
            assert chain.n == BEGUN
            dve.wait_ge(counted.sem, 4)
            at = psum[0:T, 1, 0:P].rearrange("p (e b) -> p b e", e=E)
            for k in (1, 2):
                link(tt(t[f"at{k}"][:], t[f"pick{k}"][:], at, ALU.mult))
                link(red(small[f"slot{k}"][:], t[f"at{k}"][:], X, ALU.add))
                link(nc.vector.tensor_copy(routes.slot[k - 1][:], small[f"slot{k}"][:]))
            dve.wait_ge(counted.sem, 5)
            link(ts(routes.expert[:], psum[0:1, 0, 0:BLOCKS], 1.0, None, ALU.subtract))
            assert chain.n == LINKS


PICKED = 17
COUNTED = PICKED + 6
BLOCKED = COUNTED + 3
OFFSET = BLOCKED + 2
BEGUN = OFFSET + 1
LINKS = BEGUN + 7


def experts(nc, psum, const, routes, w_up, w_down, dve_first, beside):
    with Scope(nc, "experts") as s:
        up = s.sb("up", [P, 2, C, DFF])
        down = s.sb("down", [P, 2, M8, D])
        rows = s.sb("rows", [P, 2, HALVES, D])
        xb = s.sb("xb", [P, 2, C, BLOCK])
        relu = s.sb("relu", [P, 2, BLOCK])
        hidden = s.sb("hidden", [P, 2, M8, BLOCK])
        result = s.sb("result", [P, 2, HALVES, D])
        loaded = s.loads("weights_loaded", 2)
        rows_loaded = s.loads("rows_loaded", 1)
        stored = s.loads("result_stored", 1)
        turned = s.counter("turned", 1)
        xb_ready = s.counter("xb_ready", 1)
        up_ready = s.counter("up_ready", M8)
        relu_done = s.counter("relu_done", M8)
        hidden_ready = s.counter("hidden_ready", M8)
        down_done = s.counter("down_done", HALVES)
        result_ready = s.counter("result_ready", 1)
        block = s.block()
        PAIRS = BLOCKS // 2
        assert BLOCKS % 2

        def block_steps(eng, step):
            with eng.Fori(0, PAIRS) as i:
                step(At(0, [(i, 2)]), False)
                step(At(1, [(i, 2)]), False)
            step(At(BLOCKS - 1), True)

        @block.sync
        def _(sp):
            def load(n):
                u = n.parity
                e = nc.values_load(routes.expert[0:1, bass.ds(n.times(1), 1)], engines=(mybir.EngineType.SP,), min_val=0, max_val=E - 1,
                                   skip_runtime_bounds_check_because="it counts, less one, the experts that begin at or before the block, and the first always does")
                sp.dma_start(rows[:, u], routes.slots_x[bass.ds(n.times(BLOCK), BLOCK), :].rearrange("(a p) d -> p a d", p=P)).then_inc(rows_loaded.sem(n), 16)
                sp.dma_start(up[:, u], w_up[bass.ds(e, 1)].rearrange("o (c p) n -> p (o c) n", p=P)).then_inc(loaded.sem(n), 16)
                sp.dma_start(down[:, u], w_down[bass.ds(e, 1)].rearrange("o (k p) n -> p (o k) n", p=P)).then_inc(loaded.sem(n), 16)

            def store(n):
                sp.wait_ge(*result_ready.after(n))
                dst = routes.slots_y[bass.ds(n.times(BLOCK), BLOCK), :].rearrange("(a p) d -> p a d", p=P)
                sp.dma_start(dst, result[:, n.parity]).then_inc(stored.sem(n), 16)

            sp.wait_ge(routes.scattered.sem, routes.scattered.n)
            load(At(0))
            load(At(1))
            with sp.Fori(0, PAIRS - 1) as i:
                for u in range(2):
                    store(At(u, [(i, 2)]))
                    load(At(u + 2, [(i, 2)]))
            store(At(BLOCKS - 3))
            load(At(BLOCKS - 1))
            store(At(BLOCKS - 2))
            store(At(BLOCKS - 1))
            sp.wait_ge(*stored.after(At(BLOCKS - 2)))
            sp.wait_ge(*stored.after(At(BLOCKS - 1)))

        @block.gpsimd
        def _(pool):
            beside(pool)

        @block.tensor
        def _(pe):
            for x in (turned, up_ready, down_done):
                x.start(pe)

            def turn(n):
                u = n.parity
                pe.wait_ge(*rows_loaded.after(n))
                pe.wait_ge(*xb_ready.after(n - 1))
                for c in range(C):
                    for a in range(HALVES):
                        mm = nc.tensor.transpose(psum[:, 4, c * BLOCK + a * P:c * BLOCK + (a + 1) * P], rows[:, u, a, c * P:(c + 1) * P], const["ident"][:])
                mm.then_inc(turned.sem, 1)

            def step(n, last):
                u = n.parity
                pe.wait_ge(*loaded.after(n))
                pe.wait_ge(*xb_ready.after(n))
                for m in range(M8):
                    pe.wait_ge(*relu_done.after(n if m >= 4 else n - 1, (m - 4) % M8))
                    for c in range(C):
                        mm = nc.tensor.matmul(psum[:, m % 4, 0:BLOCK], up[:, u, c, m * P:(m + 1) * P], xb[:, u, c, :], start=c == 0, stop=c == C - 1)
                    mm.then_inc(up_ready.sem, 1)
                if not last:
                    turn(n + 1)
                pe.wait_ge(*result_ready.after(n - 2))
                for a in range(HALVES):
                    for k in range(M8):
                        if a == 0:
                            pe.wait_ge(*hidden_ready.after(n, k))
                        mm = nc.tensor.matmul(psum[:, 6 + u, a * D:(a + 1) * D], hidden[:, u, k, a * P:(a + 1) * P], down[:, u, k, :], start=k == 0, stop=k == M8 - 1)
                    mm.then_inc(down_done.sem, 1)

            turn(At(0))
            block_steps(pe, step)

        @block.scalar
        def _(act):
            relu_done.start(act)
            xb_ready.start(act)
            nc.scalar.preload_act_table(ACT.Relu)

            def take(n):
                act.wait_ge(*turned.after(n))
                act.wait_ge(*up_ready.after(n - 2, M8 - 1))
                nc.scalar.copy(xb[:, n.parity], psum[:, 4, :].rearrange("p (c t) -> p c t", c=C)).then_inc(xb_ready.sem, 1)

            def step(n, last):
                for m in range(M8):
                    act.wait_ge(*up_ready.after(n, m))
                    act.wait_ge(*hidden_ready.after(n if m >= 2 else n - 1, (m - 2) % M8))
                    nc.scalar.activation(relu[:, m % 2], psum[:, m % 4, 0:BLOCK], ACT.Relu).then_inc(relu_done.sem, 1)
                if not last:
                    take(n + 1)

            take(At(0))
            block_steps(act, step)

        @block.vector
        def _(dve):
            dve_first(dve)
            hidden_ready.start(dve)
            result_ready.start(dve)

            def step(n, last):
                u = n.parity
                for m in range(M8):
                    dve.wait_ge(*relu_done.after(n, m))
                    dve.wait_ge(*down_done.after(n - 2, HALVES - 1))
                    nc.vector.tensor_tensor(hidden[:, u, m], relu[:, m % 2], relu[:, m % 2], ALU.mult).then_inc(hidden_ready.sem, 1)
                dve.wait_ge(*down_done.after(n, HALVES - 1))
                dve.wait_ge(*stored.after_one_before(n))
                nc.vector.tensor_copy(result[:, u].rearrange("p a d -> p (a d)"), psum[:, 6 + u, 0:HALVES * D]).then_inc(result_ready.sem, 1)

            block_steps(dve, step)


def combine_experts(nc, psum, const, routes, accT):
    got = routes.result
    with Scope(nc, "combine") as s:
        scaled, joined, turned, added = (s.chain(x) for x in ("scaled", "joined", "turned", "added"))
        block = s.block()

        @block.scalar
        def _(act):
            for b in range(NB):
                if b % FETCH == 0:
                    act.wait_ge(routes.fetched[b // FETCH].sem, routes.fetched[b // FETCH].n)
                nc.scalar.activation(got[0][:, b], got[0][:, b], ACT.Copy, scale=routes.weight[0][:, b:b + 1]).then_inc(scaled.sem, 1)

        @block.vector
        def _(dve):
            def join(b):
                dve.wait_ge(scaled.sem, b + 1)
                nc.vector.scalar_tensor_tensor(got[0][:, b], got[1][:, b], routes.weight[1][:, b:b + 1], got[0][:, b], ALU.mult, ALU.add).then_inc(joined.sem, 1)

            def add(b):
                dve.wait_ge(turned.sem, b + 1)
                x = accT[:, :, b * T:(b + 1) * T]
                nc.vector.tensor_tensor(x, x, psum[:, b % 4, 0:C * T].rearrange("p (c t) -> p c t", c=C), ALU.add).then_inc(added.sem, 1)

            for b in range(NB + 1):
                if b < NB:
                    join(b)
                if b:
                    add(b - 1)

        @block.tensor
        def _(pe):
            for b in range(NB):
                pe.wait_ge(joined.sem, b + 1)
                if b >= 4:
                    pe.wait_ge(added.sem, b - 3)
                for c in range(C):
                    mm = nc.tensor.transpose(psum[:, b % 4, c * T:(c + 1) * T], got[0][:, b, c * P:(c + 1) * P], const["ident"][0:T, 0:T])
                mm.then_inc(turned.sem, 1)




NT_, FULL, REST = 6, 4, 96
INTER_TILES = [(m, P if m < FULL else REST) for m in range(NT_)]
INTER_FIRST = [m * P if m < FULL else FULL * P + (m - FULL) * REST for m in range(NT_)]
assert INTER_FIRST[-1] + REST == INTER


class QuantisedWeights:

    def __init__(self, nc, sb):
        self.rounded = sb("rounded_weights", [P, 3, NT_ * D], BF16)
        self.largest_of, self.scale, self.inverse = (sb(f"weight_{x}", [P, 2 * NT_ + C]) for x in ("largest", "scale", "inverse"))
        self.loaded = Chain(nc.alloc_semaphore("quantised_weights_loaded"))
        self.largest, self.scaled, self.divided, self.clipped = (
            Chain(nc.alloc_semaphore(f"weights_{name}")) for name in ("largest", "scaled", "divided", "clipped"))


def load_to_quantise(nc, sp, quant, raw, w):
    for k, name in enumerate(("gate", "up")):
        dst = raw[:, k].rearrange("p (m n) -> p m n", n=D)
        quant.loaded.inc(sp.dma_start(dst[:, 0:FULL], w[name][0:FULL * P].rearrange("(m p) n -> p m n", p=P)), 16)
        quant.loaded.inc(sp.dma_start(dst[0:REST, FULL:NT_], w[name][FULL * P:INTER].rearrange("(m p) n -> p m n", p=REST)), 16)
    quant.loaded.inc(sp.dma_start(raw[:, 2, 0:C * INTER].rearrange("p (c n) -> p c n", c=C), w["down"].rearrange("(c p) n -> p c n", p=P)), 16)


def weight_pieces(quant, raw):
    places = [(rows, k, m * D, D, k * NT_ + m) for k in range(2) for m, rows in INTER_TILES]
    places += [(P, 2, c * INTER, INTER, 2 * NT_ + c) for c in range(C)]
    return [(raw[0:rows, k, o:o + width], quant.largest_of[0:rows, col:col + 1], quant.inverse[0:rows, col:col + 1], quant.rounded[0:rows, k, o:o + width])
            for rows, k, o, width, col in places]


def measure_weights(nc, dve, quant, raw):
    quant.largest.inc(nc.vector.memset(quant.largest_of[:], 1.0))
    dve.wait_ge(quant.largest.sem, quant.largest.n)
    dve.wait_ge(quant.loaded.sem, quant.loaded.n)
    for x, largest, _, _ in weight_pieces(quant, raw):
        quant.largest.inc(nc.vector.tensor_reduce(largest, x, X, ALU.max, apply_absolute_value=True))
    dve.wait_ge(quant.largest.sem, quant.largest.n)
    quant.scaled.inc(nc.vector.tensor_scalar(quant.scale[:], quant.largest_of[:], 1.0 / QMAX, None, ALU.mult))
    dve.wait_ge(quant.scaled.sem, 1)
    quant.scaled.inc(nc.vector.reciprocal(quant.inverse[:], quant.scale[:]))


def round_weights(nc, pool, quant, raw):
    pool.wait_ge(quant.scaled.sem, 2)
    for x, _, inverse, rounded in weight_pieces(quant, raw):
        pool.wait_ge(quant.divided.sem, quant.divided.inc(nc.gpsimd.tensor_scalar(x, x, inverse, ROUND, ALU.mult, ALU.add)))
        pool.wait_ge(quant.clipped.sem, quant.clipped.inc(nc.gpsimd.tensor_scalar(x, x, ROUND + QMAX, ROUND - QMAX - 1, ALU.min, ALU.max)))
        nc.gpsimd.tensor_scalar(rounded, x, ROUND, None, ALU.subtract)


def quantised(nc, psum, const, quant, clip_x, clip_down, hT, accT, while_loading):
    tiles, first = INTER_TILES, INTER_FIRST
    qb, wscale = quant.rounded, quant.scale
    with Scope(nc, "quant") as s:
        clips = s.sb("clips", [P, 2])
        clip_sig = s.sb("clip_sig", [P, 2])
        wgT = s.sb("wgT", [P, C, INTER], BF16)
        wuT = s.sb("wuT", [P, C, INTER], BF16)
        wdT = s.sb("wdT", [P, NT_, D], BF16)
        xq = s.sb("xq", [P, C, TOK], BF16)
        hq = s.sb("hq", [P, NT_, G], BF16)
        h = s.sb("h", [P, NT_, TOK])
        gates = s.sb("gates", [P, 2, G])
        sc = s.sb("scales", [P, 16])
        both = s.sb("both", [P, 2 * NT_])
        outs = s.sb("outs", [P, C])
        hmax = s.sb("hmax", [P, GROUPS * NT_])
        ld = s.chain("ld")

        with nc.Block() as block:

            @block.sync
            def _(sp):
                ld.inc(sp.dma_start(clips[:, 0:1], clip_x.unsqueeze(0).broadcast_to([P, 1])), 16)
                ld.inc(sp.dma_start(clips[:, 1:2], clip_down.unsqueeze(0).broadcast_to([P, 1])), 16)

            @block.vector
            def _(dve):
                nc.vector.memset(hmax[:], 0.0)
                nc.vector.memset(sc[:], 0.0)

        while_loading()

        vx, ax, gx = (s.chain(x) for x in ("vx", "ax", "gx"))
        with nc.Block() as block:

            @block.vector
            def _(dve):
                vx.inc(nc.vector.tensor_reduce(sc[:, 0:1], hT[:].rearrange("p c t -> p (c t)"), X, ALU.max, apply_absolute_value=True))

            @block.gpsimd
            def _(pool):
                pool.wait_ge(vx.sem, 1)
                nc.gpsimd.partition_all_reduce(sc[:, 1:2], sc[:, 0:1], P, bass.bass_isa.ReduceOp.max).then_inc(gx.sem, 1)

            @block.scalar
            def _(act):
                act.wait_ge(ld.sem, 32)
                nc.scalar.activation(clip_sig[:], clips[:], ACT.Sigmoid).then_inc(ax.sem, 1)

        turns = [(0, m, c, rows) for m, rows in tiles for c in range(C)] + [(1, m, c, rows) for m, rows in tiles for c in range(C)]
        turns += [(2, m, c, rows) for m, rows in tiles for c in range(C)]
        tp, tr, rx, px = (s.chain(x) for x in ("tp", "tr", "rx", "px"))
        xf = s.sb("xf", [P, C, TOK])
        with nc.Block() as block:

            @block.tensor
            def _(pe):
                for k, (p, m, c, rows) in enumerate(turns):
                    if k >= 8:
                        pe.wait_ge(tr.sem, k - 7)
                    dst = psum[:, k % 8, :].bitcast(BF16)
                    if p < 2:
                        mm = nc.tensor.transpose(dst[:, 0:rows], qb[0:rows, p, m * D + c * P:m * D + (c + 1) * P], const["identb"][0:rows, 0:rows])
                    else:
                        mm = nc.tensor.transpose(dst[0:rows, 0:P], qb[:, 2, c * INTER + first[m]:c * INTER + first[m] + rows], const["identb"][:])
                    mm.then_inc(tp.sem, 1)

            @block.scalar
            def _(act):
                for k, (p, m, c, rows) in enumerate(turns):
                    act.wait_ge(tp.sem, k + 1)
                    src = psum[:, k % 8, :].bitcast(BF16)
                    if p < 2:
                        nc.scalar.copy((wgT, wuT)[p][:, c, first[m]:first[m] + rows], src[:, 0:rows]).then_inc(tr.sem, 1)
                    else:
                        nc.scalar.copy(wdT[0:rows, m, c * P:(c + 1) * P], src[0:rows, 0:P]).then_inc(tr.sem, 1)

            @block.vector
            def _(dve):
                def link(ins):
                    dve.wait_ge(rx.sem, rx.inc(ins))

                link(nc.vector.scalar_tensor_tensor(sc[:, 2:3], sc[:, 1:2], 1.0 / QMAX, clip_sig[:, 0:1], ALU.mult, ALU.mult))
                link(nc.vector.reciprocal(sc[:, 3:4], sc[:, 2:3]))
                nc.vector.tensor_scalar(both[:], wscale[:, 0:2 * NT_], sc[:, 2:3], None, ALU.mult)
                for g in range(GROUPS):
                    x = xf[:, :, g * G:(g + 1) * G]
                    link(nc.vector.tensor_scalar(x, hT[:, :, g * G:(g + 1) * G], sc[:, 3:4], ROUND, ALU.mult, ALU.add))
                    px.inc(nc.vector.tensor_scalar(x, x, ROUND + QMAX, ROUND - QMAX - 1, ALU.min, ALU.max))
                for g in (2, 3):
                    dve.wait_ge(px.sem, g + 1)
                    nc.vector.tensor_scalar(xq[:, :, g * G:(g + 1) * G], xf[:, :, g * G:(g + 1) * G], ROUND, None, ALU.subtract)

            @block.gpsimd
            def _(pool):
                for g in (0, 1):
                    pool.wait_ge(px.sem, g + 1)
                    nc.gpsimd.tensor_scalar(xq[:, :, g * G:(g + 1) * G], xf[:, :, g * G:(g + 1) * G], ROUND, None, ALU.subtract)

        up_made = s.counter("up_made", 2 * NT_)
        gated = s.counter("gated", NT_)
        joined = s.counter("joined", NT_)
        measured = s.counter("measured", NT_)
        with nc.Block() as block:

            @block.tensor
            def _(pe):
                up_made.start(pe)
                with pe.Fori(0, GROUPS) as g:
                    n, t = At(0, [(g, 1)]), bass.ds(g * G, G)
                    for m, rows in tiles:
                        b = m % 3
                        for k, wT in enumerate((wgT, wuT)):
                            pe.wait_ge(*(gated, joined)[k].after(n if m >= 3 else n - 1, (m - 3) % NT_))
                            for c in range(C):
                                mm = nc.tensor.matmul(psum[0:rows, 2 * b + k, 0:G], wT[:, c, first[m]:first[m] + rows], xq[:, c, t], start=c == 0, stop=c == C - 1)
                            mm.then_inc(up_made.sem, 1)

            @block.scalar
            def _(act):
                gated.start(act)
                nc.scalar.preload_act_table(ACT.Silu)
                with act.Fori(0, GROUPS) as g:
                    n = At(0, [(g, 1)])
                    for m, rows in tiles:
                        act.wait_ge(*up_made.after(n, 2 * m))
                        act.wait_ge(*joined.after(n if m >= 2 else n - 1, (m - 2) % NT_))
                        nc.scalar.activation(gates[0:rows, m % 2], psum[0:rows, 2 * (m % 3), 0:G], ACT.Silu, scale=both[0:rows, m:m + 1]).then_inc(gated.sem, 1)

            @block.vector
            def _(dve):
                joined.start(dve)
                measured.start(dve)
                with dve.Fori(0, GROUPS) as g:
                    n, t = At(0, [(g, 1)]), bass.ds(g * G, G)
                    for m, rows in tiles:
                        dve.wait_ge(*gated.after(n, m))
                        dve.wait_ge(*up_made.after(n, 2 * m + 1))
                        nc.vector.scalar_tensor_tensor(h[0:rows, m, t], psum[0:rows, 2 * (m % 3) + 1, 0:G], both[0:rows, NT_ + m:NT_ + m + 1], gates[0:rows, m % 2], ALU.mult, ALU.mult).then_inc(joined.sem, 1)
                    for m, rows in tiles:
                        dve.wait_ge(*joined.after(n, m))
                        nc.vector.tensor_reduce(hmax[0:rows, bass.ds(g * NT_ + m, 1)], h[0:rows, m, t], X, ALU.max, apply_absolute_value=True).then_inc(measured.sem, 1)

        hx, hg = s.chain("hx"), s.chain("hg")
        with nc.Block() as block:

            @block.vector
            def _(dve):
                def link(ins):
                    dve.wait_ge(hx.sem, hx.inc(ins))

                link(nc.vector.tensor_reduce(sc[:, 4:5], hmax[:], X, ALU.max))
                dve.wait_ge(hg.sem, 1)
                link(nc.vector.scalar_tensor_tensor(sc[:, 6:7], sc[:, 5:6], 1.0 / QMAX, clip_sig[:, 1:2], ALU.mult, ALU.mult))
                link(nc.vector.reciprocal(sc[:, 7:8], sc[:, 6:7]))
                link(nc.vector.tensor_scalar(outs[:], wscale[:, 2 * NT_:2 * NT_ + C], sc[:, 6:7], None, ALU.mult))

            @block.gpsimd
            def _(pool):
                pool.wait_ge(hx.sem, 1)
                nc.gpsimd.partition_all_reduce(sc[:, 5:6], sc[:, 4:5], P, bass.bass_isa.ReduceOp.max).then_inc(hg.sem, 1)

        scaled = s.counter("h_scaled", NT_)
        clipped = s.counter("h_clipped", NT_)
        rounded = s.counter("h_rounded", NT_)
        down_used = s.counter("down_used", NT_)
        added = s.counter("added", 1)
        block = s.block()

        @block.scalar
        def _(act):
            scaled.start(act)
            with act.Fori(0, GROUPS) as g:
                n, t = At(0, [(g, 1)]), bass.ds(g * G, G)
                for m, rows in tiles:
                    nc.scalar.activation(h[0:rows, m, t], h[0:rows, m, t], ACT.Identity, bias=const["round"][0:rows, 0:1], scale=sc[0:rows, 7:8]).then_inc(scaled.sem, 1)

        @block.vector
        def _(dve):
            clipped.start(dve)
            rounded.start(dve)
            added.start(dve)
            with dve.Fori(0, GROUPS) as g:
                n, t = At(0, [(g, 1)]), bass.ds(g * G, G)
                for m, rows in tiles:
                    dve.wait_ge(*scaled.after(n, m))
                    x = h[0:rows, m, t]
                    nc.vector.tensor_scalar(x, x, ROUND + QMAX, ROUND - QMAX - 1, ALU.min, ALU.max).then_inc(clipped.sem, 1)
                    dve.wait_ge(*clipped.after(n, m))
                    dve.wait_ge(*down_used.after(n - 1, m))
                    nc.vector.tensor_scalar(hq[0:rows, m], x, ROUND, None, ALU.subtract).then_inc(rounded.sem, 1)
                dve.wait_ge(*down_used.after(n, NT_ - 1))
                for c in range(C):
                    a = nc.vector.scalar_tensor_tensor(accT[:, c, t], psum[:, c, 0:G], outs[:, c:c + 1], accT[:, c, t], ALU.mult, ALU.add)
                a.then_inc(added.sem, 1)

        @block.tensor
        def _(pe):
            down_used.start(pe)
            with pe.Fori(0, GROUPS) as g:
                n = At(0, [(g, 1)])
                pe.wait_ge(*added.after(n - 1))
                for m, rows in tiles:
                    pe.wait_ge(*rounded.after(n, m))
                    for c in range(C):
                        mm = nc.tensor.matmul(psum[:, c, 0:G], wdT[0:rows, m, c * P:(c + 1) * P], hq[0:rows, m], start=m == 0, stop=m == NT_ - 1)
                    mm.then_inc(down_used.sem, 1)




def decoder(nc, a, out, stages=6):
    with ExitStack() as stack:
        def sb(name, shape, dt=F32):
            return stack.enter_context(nc.sbuf_tensor(name, shape, dt))

        psum = stack.enter_context(nc.psum_tensor("psum", [P, 8, 512], F32))
        xT = sb("xT", [P, C, TOK])
        hT = sb("hT", [P, C, TOK])
        averager = sb("averager", [P, P])
        eps = sb("eps", [P, 1])
        rnd = sb("rnd", [P, 1])
        ident = sb("ident", [P, P])
        identb = sb("identb", [P, P], BF16)
        spreader = sb("spreader", [P, P])
        maskf = sb("maskf", [T, T])
        maskb = sb("maskb", [T, HG * T], BF16)
        rank = sb("rank", [P, E])
        rowf = sb("rowf", [1, P])
        maskrow = sb("maskrow", [1, P], BF16)
        ln1 = sb("ln1", [P, 2, C])
        ln2 = sb("ln2", [P, 2, C])
        flags = sb("flags", [1, NB * S2 // 4], mybir.dt.uint32)
        masked = sb("masked", [1, NB * S2], BF16)
        const = {"ident": ident, "spreader": spreader, "identb": identb, "maskb": maskb, "maskrow": maskrow, "masked": masked, "round": rnd, "rank": rank, "plan": a["plan"]}
        loaded = Chain(nc.alloc_semaphore("constants_loaded"))
        zeroed = Chain(nc.alloc_semaphore("slots_zeroed"))
        zeros = sb("zeros", [P, D])

        def dram(name, shape):
            return nc.dram_tensor(name, shape, F32).ap()

        slots_x, slots_y = dram("slots_x", (SLOTS, D)), dram("slots_y", (SLOTS, D))

        with nc.Block() as block:

            @block.sync
            def _(sp):
                for dst, src in ((xT[:], a["xT"].rearrange("(c p) t -> p c t", p=P)), (ident[:], a["ident"]), (spreader[:], a["spreader"]), (maskf[:], a["causal"]),
                                 (rank[:], a["rank"]), (rowf[:], a["maskrow"]), (ln1[:], a["ln1"]), (ln2[:], a["ln2"]),
                                 (flags[:], a["mask"])):
                    loaded.inc(sp.dma_start(dst, src), 16)
                sp.wait_ge(loaded.sem, loaded.n)

            @block.vector
            def _(dve):
                nc.vector.memset(averager[:], 1.0 / D)
                nc.vector.memset(eps[:], EPS)
                nc.vector.memset(rnd[:], ROUND)
                nc.vector.memset(zeros[:], 0.0)

        with nc.Block() as block:

            @block.sync
            def _(sp):
                zeroed.inc(sp.dma_start(slots_x.rearrange("(n p) d -> p n d", p=P), zeros[:].unsqueeze(1).broadcast_to([P, SLOTS // P, D])), 16)

            @block.vector
            def _(dve):
                nc.vector.tensor_copy(identb[:], ident[:])
                nc.vector.tensor_copy(maskb[:].rearrange("p (g s) -> p g s", g=HG), maskf[:].unsqueeze(1).broadcast_to([T, HG, T]))
                nc.vector.tensor_copy(maskrow[:], rowf[:])
                nc.vector.tensor_scalar(masked[:], flags[:].bitcast(U8), NEG, None, ALU.mult)

        ns = NormSignals(nc)

        def norm(stage, src, dst, gb=None):
            layer_norm(nc, stage, ns, psum, averager, src, dst, eps, gb)


        def fm(x, n):
            return a[x].rearrange("(c p) n -> p c n", p=P), (P, C, n)

        def flat(x, *shape):
            return a[x], shape

        def wide(x):
            return a[x].rearrange("(g p) n -> p g n", p=P), (P, NG, D)

        def row(x):
            return a[x].unsqueeze(0).broadcast_to([P, D]), (P, D)

        with nc.sbuf_tensor("yT", [P, C, TOK], F32) as yT:
            def two_norms():
                norm("n0", xT, yT)
                norm("n1", yT, hT, ln1)

            attention(nc, "a0", "future", psum, const,
                      {"wq": fm("a0_wq", PADW), "wk": fm("a0_wk", PADW), "wv": fm("a0_wv", D), "wf": fm("a0_wf", D),
                       "wqm": fm("a0_wqm", D), "wkm": fm("a0_wkm", D), "conv": flat("a0_conv", P, FUT, P), "wo": wide("a0_wo")}, hT, yT, while_loading=two_norms)

            def add_and_norm():
                add_into(nc, "s0", xT, yT)
                norm("n2", yT, hT, ln2)

            perceptron(nc, "f0", psum, hT, xT, a["a0_ff1"], a["a0_ff2"], ACT.Gelu, while_loading=add_and_norm)
        if stages > 1:
            attention(nc, "x0", "memory", psum, const,
                      {"wq": fm("x0_wq", PADW), "wk": fm("x0_wk", PADW), "wv": fm("x0_wv", D), "wo": wide("x0_wo"),
                       "bq": flat("x0_bq", P, NG), "bk": flat("x0_bk", P, NG), "bv": row("x0_bv"), "bo": flat("x0_bo", P, C),
                       "m_k": flat("x0_mk", P, NG, MEM), "m_v": flat("x0_mv", MEM, H, HD)}, hT, xT, a["ctxT"], while_loading=lambda: norm("n3", xT, hT))
        if stages > 2:
            quant = QuantisedWeights(nc, sb)
            norm("n4", xT, hT)
            with ExitStack() as held:
                routes = Routes(nc, lambda name, shape, dt=F32: held.enter_context(nc.sbuf_tensor(name, shape, dt)), slots_x, slots_y)
                raw = held.enter_context(nc.sbuf_tensor("raw_weights", [P, 3, NT_ * D], F32))
                router(nc, psum, const, a["router_w"], hT, routes,
                       lambda sp: load_to_quantise(nc, sp, quant, raw, {"gate": a["q_gate"], "up": a["q_up"], "down": a["q_down"]}))

                def shared(stage, groups, beside):
                    perceptron(nc, stage, psum, hT, xT, a["shared_up"], a["shared_down"], ACT.Relu, groups, beside)

                shared("s1", range(GROUPS // 2), lambda pool: scatter_tokens(nc, pool, routes, zeroed))
                experts(nc, psum, const, routes, a["moe_up"], a["moe_down"],
                        lambda dve: measure_weights(nc, dve, quant, raw), lambda pool: round_weights(nc, pool, quant, raw))
                shared("s2", range(GROUPS // 2, GROUPS), lambda pool: gather_results(nc, pool, routes))
                combine_experts(nc, psum, const, routes, xT)
        if stages > 3:
            with nc.sbuf_tensor("qT_all", [P, NG, TOK], F32) as qT_all, nc.sbuf_tensor("gateT", [P, NG, TOK], F32) as gateT:
                skew = dram("offset_rows", (NB * H * T * T,))
                offset_factors(nc, psum, {"wq": fm("a1_wq", PADW), "bq": flat("a1_bq", P, NG), "gate_w": fm("a1_gate_w", PADW),
                                          "gate_b": flat("a1_gate_b", P, NG), "gain": flat("a1_gain", P, NG), "rel": flat("a1_rel", P, T)},
                               hT, qT_all, gateT, skew, lambda: norm("n5", xT, hT))
                attention(nc, "a1", "offset", psum, const,
                          {"wk": fm("a1_wk", PADW), "wv": fm("a1_wv", D), "wo": wide("a1_wo"), "bk": flat("a1_bk", P, NG),
                           "bv": row("a1_bv"), "bo": flat("a1_bo", P, C)}, hT, xT, qT_all=qT_all, gateT=gateT,
                          skewed={"dram": skew, "bias": a["a1_bias"]}, while_loading=lambda: None)
        if stages > 4:
            attention(nc, "x1", "causal", psum, const,
                      {"wq": fm("x1_wq", PADW), "wk": fm("x1_wk", PADW), "wv": fm("x1_wv", D), "wo": wide("x1_wo"),
                       "bq": flat("x1_bq", P, NG), "bk": flat("x1_bk", P, NG), "bv": row("x1_bv"), "bo": flat("x1_bo", P, C)}, hT, xT, a["ctxT"],
                      while_loading=lambda: norm("n6", xT, hT))
        if stages > 5:
            quantised(nc, psum, const, quant, a["q_clip_x"], a["q_clip_down"], hT, xT,
                      lambda: norm("n7", xT, hT))

        with nc.Block() as block:

            @block.sync
            def _(sp):
                done = Chain(nc.alloc_semaphore("stored"))
                done.inc(sp.dma_start(out.rearrange("(c p) t -> p c t", p=P), xT[:]), 16)
                sp.wait_ge(done.sem, done.n)




def padded_heads(w):
    w = np.asarray(w)
    out = np.zeros(w.shape[:-1] + (H, 32), np.float32)
    out[..., :HD] = w.reshape(w.shape[:-1] + (H, HD))
    return out.reshape(w.shape[:-1] + (PADW,))


def padded_rows(w):
    return np.ascontiguousarray(padded_heads(np.asarray(w).T).T)


def head_rows(b, spare=0.0):
    p = padded_heads(b).reshape(H, 32).copy()
    p[:, HD] = spare
    return np.ascontiguousarray(p.reshape(NG, P).T)


def laid_out(i):
    t = lambda x: np.ascontiguousarray(np.asarray(x).T)
    col = lambda x: np.ascontiguousarray(np.asarray(x).reshape(C, P).T)
    f = {}
    f["xT"] = np.ascontiguousarray(i["x"].reshape(TOK, D).T)
    f["ctxT"] = np.ascontiguousarray(i["ctx_1024"].transpose(0, 2, 1))
    f["mask"] = np.ascontiguousarray(i["mask_Bx1x1xS2_bk0"].reshape(1, NB * S2)).view(np.uint32)
    f["ident"] = np.eye(P, dtype=np.float32)
    f["causal"] = np.where(np.arange(T)[None, :] <= np.arange(T)[:, None], 0.0, NEG).astype(np.float32)
    f["rank"] = np.ascontiguousarray(np.broadcast_to(np.arange(E, 0, -1, dtype=np.float32), (P, E)))
    e, b = np.arange(P) // NB, np.arange(P) % NB
    tokens = np.zeros((P, T))
    tokens[:T] = np.arange(T)[:, None] < np.arange(T)
    f["plan"] = np.concatenate([tokens, (e[:, None] == e) & (b[:, None] < b), e[:, None] == e,
                                np.broadcast_to(((e[:, None] < e) & (b[:, None] == 0)), (P, P)), (b == 0)[:, None],
                                np.broadcast_to(BLOCK * np.arange(BLOCKS), (P, BLOCKS))], 1).astype(np.float32)
    f["spreader"] = ((np.arange(P)[:, None] // 32 == np.arange(P) // 32) & (np.arange(P)[:, None] % 32 == HD)).astype(np.float32)
    f["maskrow"] = (np.arange(P) % 32 == HD).astype(np.float32)[None]
    for k in (1, 2):
        f[f"ln{k}"] = np.ascontiguousarray(np.stack([col(i[f"L0_attn_ln{k}_g"]), col(i[f"L0_attn_ln{k}_b"])], 1))
    wq, wk, wv, wf = (t(x) for x in np.split(i["L0_attn_W_qkvf"], 4))
    f["a0_wq"], f["a0_wk"], f["a0_wv"], f["a0_wf"], f["a0_wqm"], f["a0_wkm"] = padded_heads(wq), padded_heads(wk), wv, wf, wq, wk
    conv = np.zeros((P // HD, HD, FUT, P // HD, HD), np.float32)
    for h in range(P // HD):
        conv[h, :, :, h, :] = i["L0_attn_W_conv"].transpose(0, 2, 1)
    f["a0_conv"] = conv.reshape(P, FUT, P)
    f["a0_wo"] = padded_rows(t(i["L0_attn_W_proj"]))
    f["a0_ff1"], f["a0_ff2"] = i["L0_attn_W_ff1"], i["L0_attn_W_ff2"]
    for n, l in (("x0", "L0_xattn"), ("x1", "L1_xattn")):
        tt = t if n == "x0" else np.ascontiguousarray
        f[n + "_wq"], f[n + "_wk"] = padded_heads(tt(i[l + "_Wq"])), padded_heads(tt(i[l + "_Wk"]))
        f[n + "_wv"], f[n + "_wo"] = tt(i[l + "_Wv"]), padded_rows(tt(i[l + "_Wo"]))
        f[n + "_bq"] = head_rows(i[l + "_bq"], 1.0 if n == "x0" else 0.0)
        f[n + "_bk"], f[n + "_bv"], f[n + "_bo"] = head_rows(i[l + "_bk"]), i[l + "_bv"], col(i[l + "_bo"])
    f["x0_mk"] = np.ascontiguousarray(padded_heads(i["L0_xattn_m_k"][0]).reshape(MEM, NG, P).transpose(2, 1, 0))
    f["x0_mv"] = np.ascontiguousarray(i["L0_xattn_m_v"][0].reshape(MEM, H, HD))
    f["router_w"] = t(i["L0_ffn_router_w"])
    f["moe_up"], f["moe_down"] = (np.ascontiguousarray(i[x].transpose(0, 2, 1)) for x in ("L0_ffn_w_fc", "L0_ffn_w_proj"))
    f["shared_up"], f["shared_down"] = t(i["L0_ffn_shared_fc"]), t(i["L0_ffn_shared_proj"])
    wq, wk, wv = (t(x) for x in np.split(i["L1_attn_qkv_w"], 3))
    bq, bk, bv = np.split(i["L1_attn_qkv_b"], 3)
    f["a1_wq"], f["a1_wk"], f["a1_wv"], f["a1_wo"] = padded_heads(wq), padded_heads(wk), wv, padded_rows(t(i["L1_attn_out_w"]))
    f["a1_bq"], f["a1_bk"], f["a1_bv"], f["a1_bo"] = head_rows(bq), head_rows(bk), np.ascontiguousarray(bv), col(i["L1_attn_out_b"])
    f["a1_gate_w"], f["a1_gate_b"] = padded_heads(t(i["L1_attn_gate_w"])), head_rows(i["L1_attn_gate_b"])
    f["a1_gain"] = head_rows(np.repeat(i["L1_attn_if_gain"], HD))
    rel = np.zeros((HG, 32, T), np.float32)
    bias = np.full((T, H, T), NEG, np.float32)
    for k, o in enumerate(OFFSETS):
        if o < T:
            rel[:, :HD, T - 1 - o] = i["L1_attn_scale_embed"][k]
            for q in range(o, T):
                bias[q, :, q - o] = i["L1_attn_pos_bias"][k]
    f["a1_rel"], f["a1_bias"] = rel.reshape(P, T), bias
    f["q_gate"], f["q_up"], f["q_down"] = i["L1_ffn_w_gate"], i["L1_ffn_w_up"], i["L1_ffn_w_down"]
    f["q_clip_x"], f["q_clip_down"] = i["L1_ffn_clip_x"], i["L1_ffn_clip_down"]
    return f


def kernel(**inputs):
    import concourse.bacc as bacc
    from concourse.bass_utils import run_bass_kernel_spmd

    fed = {f"in_{k}": np.ascontiguousarray(v) for k, v in laid_out({k: np.asarray(v) for k, v in inputs.items()}).items()}
    nc = bacc.Bacc("TRN2", target_bir_lowering=False, num_devices=1)
    a = {k[3:]: nc.dram_tensor(k, v.shape, mybir.dt.from_np(v.dtype), kind="ExternalInput").ap() for k, v in fed.items()}
    out = nc.dram_tensor("out_xT", (D, TOK), F32, kind="ExternalOutput").ap()
    decoder(nc, a, out)
    r = run_bass_kernel_spmd(nc, [fed], core_ids=[0])
    return np.ascontiguousarray(r.results[0]["out_xT"].T).reshape(NB, T, D)
```
